# Optimizing a Trainium2 kernel written in Bass

```python
import numpy as np
import jax
import jax.numpy as jnp

def _softmax(x, axis=-1):
    return jax.nn.softmax(x, axis=axis)

def _gelu(x):
    return jax.nn.gelu(x, approximate=True)

def _silu(x):
    return jax.nn.silu(x)

def _sigmoid(x):
    return jax.nn.sigmoid(x)

def _layernorm(x, axis=-1, eps=1e-05):
    m = jnp.mean(x, axis=axis, keepdims=True)
    v = jnp.var(x, axis=axis, keepdims=True)
    return (x - m) / jnp.sqrt(v + eps)

def _scatter_add(tgt, idx, src, axis=0):
    return tgt.at[idx].add(src)

def _segment_sum(src, seg, n):
    return jax.ops.segment_sum(src, seg, n)
kernel_name = 'mk_xattn_ffn_d2_seqx_r8_9cd1f1'

def setup_inputs(seed: int=0):
    np.random.seed(seed)
    _w = jnp.asarray

    def _rec_inputs():
        import jax
        import jax.numpy as jnp
        _rk = jax.random.key(seed)
        x = -0.0002928 + 1 * jax.random.normal(jax.random.fold_in(_rk, 1), (4, 512, 128), jnp.float32)
        _lenS = 512 - jax.random.randint(jax.random.fold_in(_rk, 7), (4,), 0, max(1, 512 // 4) + 1, jnp.int32)
        _lenS2 = 154 - jax.random.randint(jax.random.fold_in(_rk, 8), (4,), 0, max(1, 154 // 4) + 1, jnp.int32)
        _ctx_1024P = jax.random.normal(jax.random.fold_in(_rk, 11), (4, 16, 128), jnp.float32)
        _ctx_1024c = jax.random.dirichlet(jax.random.fold_in(_rk, 511), 0.3 * jnp.ones((16,), jnp.float32), (4, 154))
        _ctx_1024t = jnp.einsum('bsk,bkd->bsd', _ctx_1024c, _ctx_1024P)
        _ctx_1024t = _ctx_1024t * jax.lax.rsqrt(jnp.mean(jnp.square(_ctx_1024t)) + 1e-12) * 0.953939
        ctx_1024 = -1.39393e-06 + 0.999914 * (_ctx_1024t + 0.3 * jax.random.normal(jax.random.fold_in(_rk, 611), (4, 154, 128), jnp.float32))
        _validS = jnp.arange(512)[None, :] < _lenS[:, None]
        _validS2 = jnp.arange(154)[None, :] < _lenS2[:, None]
        _causal = jnp.tril(jnp.ones((512, 512), dtype=bool))
        mask_BxS2_bf1 = jnp.ones((4, 154), dtype=bool)
        return (x, ctx_1024, mask_BxS2_bf1)
    x, ctx_1024, mask_BxS2_bf1 = _rec_inputs()

    def _L0_xattn_setup():
        import jax, jax.numpy as jnp
        import numpy as np
        N_HEADS = 16
        D_MODEL = 128
        HEAD_DIM = D_MODEL // N_HEADS
        MASK_FILL = -100000000.0

        def _split_heads(x):
            B, S, _ = x.shape
            return x.reshape(B, S, N_HEADS, HEAD_DIM).transpose(0, 2, 1, 3)
        key = jax.random.key(seed)
        ks = jax.random.split(key, 12)
        B, L, P = (2, 256, 256)
        s = 1.0 / np.sqrt(D_MODEL).astype(np.float32)
        inp = {'q': jax.random.normal(ks[0], (B, L, D_MODEL), dtype=jnp.float32), 'k': jax.random.normal(ks[1], (B, P, D_MODEL), dtype=jnp.float32), 'v': jax.random.normal(ks[2], (B, P, D_MODEL), dtype=jnp.float32), 'attention_mask': jnp.ones((B, P), dtype=bool), 'Wq': jax.random.normal(ks[3], (D_MODEL, D_MODEL), dtype=jnp.float32) * s, 'bq': jnp.zeros((D_MODEL,), dtype=jnp.float32), 'Wk': jax.random.normal(ks[4], (D_MODEL, D_MODEL), dtype=jnp.float32) * s, 'bk': jnp.zeros((D_MODEL,), dtype=jnp.float32), 'Wv': jax.random.normal(ks[5], (D_MODEL, D_MODEL), dtype=jnp.float32) * s, 'bv': jnp.zeros((D_MODEL,), dtype=jnp.float32), 'Wo': jax.random.normal(ks[6], (D_MODEL, D_MODEL), dtype=jnp.float32) * s, 'bo': jnp.zeros((D_MODEL,), dtype=jnp.float32)}
        return inp
    _L0_xattn_all = _L0_xattn_setup()
    _L0_xattn_in = {k: v for k, v in _L0_xattn_all.items() if k in ('Wq', 'bq', 'Wk', 'bk', 'Wv', 'bv', 'Wo', 'bo')}
    del _L0_xattn_all

    def _L0_ffn_setup():
        import jax, jax.numpy as jnp
        import numpy as np
        from jax import lax
        D = 128
        H = 512
        E = 8
        TOPK = 2
        key = jax.random.key(seed)
        ks = jax.random.split(key, 7)
        s = 0.02
        return {'x': jax.random.normal(ks[0], (2, 256, D), dtype=jnp.float32), 'W1': jax.random.normal(ks[1], (E, D, H), dtype=jnp.float32) * s, 'b1': jnp.zeros((E, H), dtype=jnp.float32), 'W2': jax.random.normal(ks[2], (E, H, D), dtype=jnp.float32) * s, 'b2': jnp.zeros((E, D), dtype=jnp.float32), 'Wr': jax.random.normal(ks[3], (D, E), dtype=jnp.float32) * s, 'br': jnp.zeros((E,), dtype=jnp.float32)}
    _L0_ffn_all = _L0_ffn_setup()
    _L0_ffn_in = {k: v for k, v in _L0_ffn_all.items() if k in ('W1', 'b1', 'W2', 'b2', 'Wr', 'br')}
    del _L0_ffn_all

    def _L1_xattn_setup():
        import jax, jax.numpy as jnp
        import numpy as np
        EPS = 0.001
        LEAKY_ALPHA = 0.2

        def layer_norm(x, gamma, beta):
            mu = jnp.mean(x, axis=-1, keepdims=True)
            var = jnp.mean(jnp.square(x - mu), axis=-1, keepdims=True)
            return (x - mu) * jax.lax.rsqrt(var + EPS) * gamma + beta

        def attention_head(x_k, x_v, x_q, Wk, Wq, Wv, use_mask):
            K = x_k @ Wk
            V = x_v @ Wv
            Q = x_q @ Wq
            Lq, Lk = (Q.shape[1], K.shape[1])
            score = jnp.einsum('bqd,bkd->bqk', Q, K) / jnp.sqrt(jnp.float32(Lk))
            if use_mask:
                mask = jnp.triu(jnp.full((Lq, Lk), -jnp.inf, dtype=score.dtype), k=1)
                score = score + mask
            return jax.nn.softmax(score, axis=-1) @ V
        key = jax.random.key(seed)
        ks = jax.random.split(key, 12)
        B, S, D = (8, 256, 128)
        inp = {'inputs': jax.random.normal(ks[0], (B, S, D), jnp.float32), 'context_sequence': jax.random.normal(ks[1], (B, S, D), jnp.float32), 'Wk1': jax.random.normal(ks[2], (D, D), jnp.float32) * 0.01, 'Wq1': jax.random.normal(ks[3], (D, D), jnp.float32) * 0.01, 'Wv1': jax.random.normal(ks[4], (D, D), jnp.float32) * 0.01, 'Wk2': jax.random.normal(ks[5], (D, D), jnp.float32) * 0.01, 'Wq2': jax.random.normal(ks[6], (D, D), jnp.float32) * 0.01, 'Wv2': jax.random.normal(ks[7], (D, D), jnp.float32) * 0.01, 'W1': jax.random.normal(ks[8], (D, D), jnp.float32) * (1.0 / np.sqrt(D)), 'b1': jnp.zeros((D,), jnp.float32), 'W2': jax.random.normal(ks[9], (D, D), jnp.float32) * (1.0 / np.sqrt(D)), 'b2': jnp.zeros((D,), jnp.float32), 'gamma': jnp.ones((D,), jnp.float32), 'beta': jnp.zeros((D,), jnp.float32)}
        return inp
    _L1_xattn_all = _L1_xattn_setup()
    _L1_xattn_in = {k: v for k, v in _L1_xattn_all.items() if k in ('Wk1', 'Wq1', 'Wv1', 'Wk2', 'Wq2', 'Wv2', 'W1', 'b1', 'W2', 'b2', 'gamma', 'beta')}
    del _L1_xattn_all

    def _L1_ffn_setup():
        import jax, jax.numpy as jnp
        import numpy as np
        H = 128
        I = 64
        E = 32
        TOP_K = 6
        N_GROUP = 8
        TOPK_GROUP = 4
        SCALE = 2.5
        N_SHARED = 2
        SI = I * N_SHARED
        B, S = (2, 128)
        key = jax.random.key(seed)
        ks = jax.random.split(key, 8)
        x = jax.random.normal(ks[0], (B, S, H), jnp.float32)
        gate_weight = jax.random.normal(ks[1], (E, H), jnp.float32) * 0.02
        e_score_correction_bias = jax.random.normal(ks[2], (E,), jnp.float32) * 0.01
        experts_gate_up = jax.random.normal(ks[3], (E, 2 * I, H), jnp.float32) * 0.02
        experts_down = jax.random.normal(ks[4], (E, H, I), jnp.float32) * 0.02
        shared_gate_w = jax.random.normal(ks[5], (SI, H), jnp.float32) * 0.02
        shared_up_w = jax.random.normal(ks[6], (SI, H), jnp.float32) * 0.02
        shared_down_w = jax.random.normal(ks[7], (H, SI), jnp.float32) * 0.02
        return {'x': x, 'gate_weight': gate_weight, 'e_score_correction_bias': e_score_correction_bias, 'experts_gate_up': experts_gate_up, 'experts_down': experts_down, 'shared_gate_w': shared_gate_w, 'shared_up_w': shared_up_w, 'shared_down_w': shared_down_w}
    _L1_ffn_all = _L1_ffn_setup()
    _L1_ffn_in = {k: v for k, v in _L1_ffn_all.items() if k in ('gate_weight', 'e_score_correction_bias', 'experts_gate_up', 'experts_down', 'shared_gate_w', 'shared_up_w', 'shared_down_w')}
    del _L1_ffn_all
    return {'x': x, 'ctx_1024': ctx_1024, 'mask_BxS2_bf1': mask_BxS2_bf1, 'L0_xattn_Wq': _L0_xattn_in['Wq'], 'L0_xattn_bq': _L0_xattn_in['bq'], 'L0_xattn_Wk': _L0_xattn_in['Wk'], 'L0_xattn_bk': _L0_xattn_in['bk'], 'L0_xattn_Wv': _L0_xattn_in['Wv'], 'L0_xattn_bv': _L0_xattn_in['bv'], 'L0_xattn_Wo': _L0_xattn_in['Wo'], 'L0_xattn_bo': _L0_xattn_in['bo'], 'L0_ffn_W1': _L0_ffn_in['W1'], 'L0_ffn_b1': _L0_ffn_in['b1'], 'L0_ffn_W2': _L0_ffn_in['W2'], 'L0_ffn_b2': _L0_ffn_in['b2'], 'L0_ffn_Wr': _L0_ffn_in['Wr'], 'L0_ffn_br': _L0_ffn_in['br'], 'L1_xattn_Wk1': _L1_xattn_in['Wk1'], 'L1_xattn_Wq1': _L1_xattn_in['Wq1'], 'L1_xattn_Wv1': _L1_xattn_in['Wv1'], 'L1_xattn_Wk2': _L1_xattn_in['Wk2'], 'L1_xattn_Wq2': _L1_xattn_in['Wq2'], 'L1_xattn_Wv2': _L1_xattn_in['Wv2'], 'L1_xattn_W1': _L1_xattn_in['W1'], 'L1_xattn_b1': _L1_xattn_in['b1'], 'L1_xattn_W2': _L1_xattn_in['W2'], 'L1_xattn_b2': _L1_xattn_in['b2'], 'L1_xattn_gamma': _L1_xattn_in['gamma'], 'L1_xattn_beta': _L1_xattn_in['beta'], 'L1_ffn_gate_weight': _L1_ffn_in['gate_weight'], 'L1_ffn_e_score_correction_bias': _L1_ffn_in['e_score_correction_bias'], 'L1_ffn_experts_gate_up': _L1_ffn_in['experts_gate_up'], 'L1_ffn_experts_down': _L1_ffn_in['experts_down'], 'L1_ffn_shared_gate_w': _L1_ffn_in['shared_gate_w'], 'L1_ffn_shared_up_w': _L1_ffn_in['shared_up_w'], 'L1_ffn_shared_down_w': _L1_ffn_in['shared_down_w']}

def reference(x, ctx_1024, mask_BxS2_bf1, L0_xattn_Wq, L0_xattn_bq, L0_xattn_Wk, L0_xattn_bk, L0_xattn_Wv, L0_xattn_bv, L0_xattn_Wo, L0_xattn_bo, L0_ffn_W1, L0_ffn_b1, L0_ffn_W2, L0_ffn_b2, L0_ffn_Wr, L0_ffn_br, L1_xattn_Wk1, L1_xattn_Wq1, L1_xattn_Wv1, L1_xattn_Wk2, L1_xattn_Wq2, L1_xattn_Wv2, L1_xattn_W1, L1_xattn_b1, L1_xattn_W2, L1_xattn_b2, L1_xattn_gamma, L1_xattn_beta, L1_ffn_gate_weight, L1_ffn_e_score_correction_bias, L1_ffn_experts_gate_up, L1_ffn_experts_down, L1_ffn_shared_gate_w, L1_ffn_shared_up_w, L1_ffn_shared_down_w):
    import jax
    import jax.numpy as jnp

    def _L0_xattn_ref(q, k, v, attention_mask, Wq, bq, Wk, bk, Wv, bv, Wo, bo):
        import jax, jax.numpy as jnp
        import numpy as np
        N_HEADS = 16
        D_MODEL = 128
        HEAD_DIM = D_MODEL // N_HEADS
        MASK_FILL = -100000000.0

        def _split_heads(x):
            B, S, _ = x.shape
            return x.reshape(B, S, N_HEADS, HEAD_DIM).transpose(0, 2, 1, 3)
        qm = _split_heads(q @ Wq.T + bq)
        km = _split_heads(k @ Wk.T + bk)
        vm = _split_heads(v @ Wv.T + bv)
        scores = jnp.einsum('bnlh,bnph->bnlp', qm, km) / np.sqrt(HEAD_DIM).astype(np.float32)
        mask = attention_mask[:, None, None, :]
        scores = jnp.where(mask, scores, MASK_FILL)
        attn = jax.nn.softmax(scores, axis=-1)
        out = jnp.einsum('bnlp,bnph->bnlh', attn, vm)
        B, _, L, _ = out.shape
        out = out.transpose(0, 2, 1, 3).reshape(B, L, D_MODEL)
        return out @ Wo.T + bo

    def _L0_ffn_ref(x, W1, b1, W2, b2, Wr, br):
        import jax, jax.numpy as jnp
        import numpy as np
        from jax import lax
        D = 128
        H = 512
        E = 8
        TOPK = 2
        B, S, _ = x.shape
        xf = x.reshape(-1, D)
        logits = xf @ Wr + br
        topv, _ = lax.top_k(logits, TOPK)
        thresh = topv[:, TOPK - 1:TOPK]
        masked = jnp.where(logits >= thresh, logits, -jnp.inf)
        weights = jax.nn.softmax(masked, axis=-1)
        h = jax.nn.gelu(jnp.einsum('td,edh->eth', xf, W1) + b1[:, None, :], approximate=False)
        expert_out = jnp.einsum('eth,ehd->etd', h, W2) + b2[:, None, :]
        out = jnp.einsum('etd,te->td', expert_out, weights)
        return out.reshape(B, S, D)

    def _L1_xattn_ref(inputs, context_sequence, Wk1, Wq1, Wv1, Wk2, Wq2, Wv2, W1, b1, W2, b2, gamma, beta):
        import jax, jax.numpy as jnp
        import numpy as np
        EPS = 0.001
        LEAKY_ALPHA = 0.2

        def layer_norm(x, gamma, beta):
            mu = jnp.mean(x, axis=-1, keepdims=True)
            var = jnp.mean(jnp.square(x - mu), axis=-1, keepdims=True)
            return (x - mu) * jax.lax.rsqrt(var + EPS) * gamma + beta

        def attention_head(x_k, x_v, x_q, Wk, Wq, Wv, use_mask):
            K = x_k @ Wk
            V = x_v @ Wv
            Q = x_q @ Wq
            Lq, Lk = (Q.shape[1], K.shape[1])
            score = jnp.einsum('bqd,bkd->bqk', Q, K) / jnp.sqrt(jnp.float32(Lk))
            if use_mask:
                mask = jnp.triu(jnp.full((Lq, Lk), -jnp.inf, dtype=score.dtype), k=1)
                score = score + mask
            return jax.nn.softmax(score, axis=-1) @ V
        att = attention_head(inputs, inputs, inputs, Wk1, Wq1, Wv1, use_mask=True)
        norm = layer_norm(att + inputs, gamma, beta)
        att2 = attention_head(context_sequence, context_sequence, att, Wk2, Wq2, Wv2, use_mask=False)
        norm2 = layer_norm(att2 + norm, gamma, beta)
        h = jax.nn.leaky_relu(norm2 @ W1 + b1, negative_slope=LEAKY_ALPHA)
        ff = h @ W2 + b2
        norm3 = layer_norm(ff + norm2, gamma, beta)
        return jax.nn.relu(norm3)

    def _L1_ffn_ref(x, gate_weight, e_score_correction_bias, experts_gate_up, experts_down, shared_gate_w, shared_up_w, shared_down_w):
        import jax, jax.numpy as jnp
        import numpy as np
        H = 128
        I = 64
        E = 32
        TOP_K = 6
        N_GROUP = 8
        TOPK_GROUP = 4
        SCALE = 2.5
        N_SHARED = 2
        SI = I * N_SHARED
        B, S = (2, 128)
        b, s, h = x.shape
        xf = x.reshape(-1, h)
        T = xf.shape[0]
        logits = xf.astype(jnp.float32) @ gate_weight.astype(jnp.float32).T
        scores = jax.nn.sigmoid(logits)
        sfc = scores + e_score_correction_bias[None, :]
        gs = E // N_GROUP
        group_scores = sfc.reshape(T, N_GROUP, gs).max(axis=-1)
        _, gidx = jax.lax.top_k(group_scores, TOPK_GROUP)
        gmask = jnp.zeros((T, N_GROUP), bool).at[jnp.arange(T)[:, None], gidx].set(True)
        smask = jnp.repeat(gmask, gs, axis=1)
        masked = jnp.where(smask, sfc, 0.0)
        _, topk_idx = jax.lax.top_k(masked, TOP_K)
        tw = jnp.take_along_axis(scores, topk_idx, axis=1)
        tw = tw / (tw.sum(-1, keepdims=True) + 1e-20)
        tw = (tw * SCALE).astype(xf.dtype)
        combine = jnp.zeros((T, E), xf.dtype).at[jnp.arange(T)[:, None], topk_idx].add(tw)

        def expert_step(acc, inp):
            gu, dn, c = inp
            g = xf @ gu[:I].T
            u = xf @ gu[I:].T
            o = jax.nn.silu(g) * u @ dn.T
            return (acc + c[:, None] * o, None)
        routed, _ = jax.lax.scan(expert_step, jnp.zeros_like(xf), (experts_gate_up, experts_down, combine.T))
        sh = jax.nn.silu(xf @ shared_gate_w.T) * (xf @ shared_up_w.T)
        shared_out = sh @ shared_down_w.T
        return (routed + shared_out).reshape(b, s, h)
    x = x + _L0_xattn_ref(_layernorm(x, axis=-1), ctx_1024, ctx_1024, mask_BxS2_bf1, L0_xattn_Wq, L0_xattn_bq, L0_xattn_Wk, L0_xattn_bk, L0_xattn_Wv, L0_xattn_bv, L0_xattn_Wo, L0_xattn_bo)
    x = x + _L0_ffn_ref(_layernorm(x, axis=-1), L0_ffn_W1, L0_ffn_b1, L0_ffn_W2, L0_ffn_b2, L0_ffn_Wr, L0_ffn_br)
    x = x + _L1_xattn_ref(_layernorm(x, axis=-1), ctx_1024, L1_xattn_Wk1, L1_xattn_Wq1, L1_xattn_Wv1, L1_xattn_Wk2, L1_xattn_Wq2, L1_xattn_Wv2, L1_xattn_W1, L1_xattn_b1, L1_xattn_W2, L1_xattn_b2, L1_xattn_gamma, L1_xattn_beta)
    x = x + _L1_ffn_ref(_layernorm(x, axis=-1), L1_ffn_gate_weight, L1_ffn_e_score_correction_bias, L1_ffn_experts_gate_up, L1_ffn_experts_down, L1_ffn_shared_gate_w, L1_ffn_shared_up_w, L1_ffn_shared_down_w)
    return x

_drawn_inputs = setup_inputs


def setup_inputs(seed=0):
    import zlib

    import numpy as np

    out = dict(_drawn_inputs(seed))
    spreads = {'L0_xattn_bq': (0.0, 0.324),
     'L0_xattn_bk': (0.0, 2.0),
     'L0_xattn_bv': (0.0, 0.1),
     'L0_xattn_bo': (0.0, 0.1),
     'L0_ffn_b1': (0.0, 0.53),
     'L0_ffn_b2': (0.0, 0.1),
     'L0_ffn_br': (0.0, 0.1),
     'L1_xattn_b1': (0.0, 0.355),
     'L1_xattn_b2': (0.0, 0.1),
     'L1_xattn_gamma': (1.0, 0.2),
     'L1_xattn_beta': (0.0, 0.1)}
    factors = {'L1_xattn_Wk1': 8.0,
     'L1_xattn_Wq1': 8.0,
     'L1_xattn_Wk2': 42.727,
     'L1_xattn_Wq2': 61.338,
     'L1_ffn_gate_weight': 8.0,
     'L1_ffn_e_score_correction_bias': 8.0,
     'L1_ffn_experts_gate_up': 8.0,
     'L1_ffn_experts_down': 8.0,
     'L1_ffn_shared_gate_w': 8.0,
     'L1_ffn_shared_up_w': 8.0,
     'L1_ffn_shared_down_w': 8.0}
    for name, (base, spread) in spreads.items():
        noise = np.random.default_rng([zlib.crc32(name.encode()), seed]).standard_normal(out[name].shape)
        drawn = base * np.exp(spread * noise) if base else spread * noise
        out[name] = jnp.asarray(drawn.astype(out[name].dtype))
    for name, factor in factors.items():
        out[name] = (out[name] * factor).astype(out[name].dtype)
    return out
```

```python
from contextlib import ExitStack
from itertools import chain

import numpy as np

import concourse.bass as bass
from concourse import mybir

F32 = mybir.dt.float32
F32R = mybir.dt.float32r
U8 = mybir.dt.uint8
ALU = mybir.AluOpType
ACT = mybir.ActivationFunctionType
AX = mybir.AxisListType

P = 128
NB, S, D = 4, 512, 128
NT = S // P
LK = 154
LT = LK - P
TP = 32
KW = P + TP
NH, HD = 16, 8
NG, HG = 4, 4
E0, H0 = 8, 512
NC0 = E0 * H0 // P
E1, I1 = 32, 64
NP1 = E1 * I1 // P
GRP, GS, TOPG, TOPK = 8, 4, 4, 6
CPAD = P + HG * TP
MASK_FILL = -1.0e8
BIG = 3.0e38
VST = P + HD


def f32r_parts(v):
    def rnd(u):
        m, e = np.frexp(np.float64(u))
        return float(np.ldexp(np.round(m * 4096.0) / 4096.0, e))
    hi = rnd(v)
    return hi, rnd(float(v) - hi)


class Signal:

    def __init__(self, sem, per):
        self.sem, self.per = sem, per

    def at(self, b, k):
        return b * self.per + k


def build_program(nc, a):
    ctx = ExitStack()

    def sb(name, shape, dt=F32):
        return ctx.enter_context(nc.sbuf_tensor(name, shape, dt))

    signals = []

    def sig(name, per):
        s = Signal(ctx.enter_context(nc.semaphore(name)), per)
        signals.append(s)
        return s

    def apart(eng, b):
        if not isinstance(b, int):
            eng.sem_inc(passed.sem, 1)

    ident = sb("ident", [P, P])
    trimask = sb("trimask", [P, P])
    valid = sb("valid", [P, 2])
    mhalf = sb("mhalf", [P, NT])
    w_in = {n: sb("w_" + n, [P, P]) for n in
            ("q", "k", "v", "k1", "q1", "v1", "k2", "q2", "v2", "f1", "f2")}
    w_o = sb("w_o", [P, 2, P])
    w_r = sb("w_r", [P, E0])
    w_gate = sb("w_gate", [P, E1])
    rows = {n: sb("row_" + n, [P, P]) for n in ("bq", "bk", "bv", "bo", "b2f", "gamma", "beta")}
    row_br = sb("row_br", [P, E0])
    row_gb = sb("row_gb", [P, E1])
    b1T = sb("b1T", [P, NC0])
    b1f = sb("b1f", [P, 1])
    b2dup = sb("b2dup", [2 * E0, P])
    pick0 = sb("pick0", [2 * E0, E0])
    pick1 = sb("pick1", [2 * E1, E1])
    pick0r = sb("pick0r", [2 * E0, E0], F32R)
    X2 = sb("X2", [P, NB, NT, P])

    ps = ctx.enter_context(nc.psum_tensor("ps", [P, 8, 512], F32))
    bank = [ps[:, i, :] for i in range(8)]
    RING, ACC, MISC = (bank[4], bank[5]), bank[6], bank[7]

    xn2 = sb("xn2", [P, NT, P])
    xT32 = sb("xT32", [P, S])
    xThi = sb("xThi", [P, S], F32R)
    xTlo = sb("xTlo", [P, S], F32R)
    h32 = sb("h32", [P, 2, S])
    hhi = sb("hhi", [P, 3, S], F32R)
    hlo = sb("hlo", [P, 3, S], F32R)
    ty = sb("ty", [P, 2, S])
    acc_o = sb("acc_o", [P, S])
    x1 = sb("x1", [P, NT, P])

    layer0 = ExitStack()

    def sb0(name, shape, dt=F32):
        return layer0.enter_context(nc.sbuf_tensor(name, shape, dt))

    w1s = sb0("w1s", [P, 2, NC0 * P], F32R)
    w2s = sb0("w2s", [P, 2, NC0 * P], F32R)
    x_in = sb0("x_in", [P, NT, P])
    xb = sb0("xb", [P, NT, P])
    xn = sb0("xn", [P, NT, P])
    xT = sb0("xT", [P, S])
    ctxA = sb0("ctxA", [P, CPAD])
    mask8 = sb0("mask8", [P, 2], U8)
    mk = sb0("mk", [P, 2])
    mkd = sb0("mkd", [P, 2])
    k32 = sb0("k32", [P, 2, P])
    km = sb0("km", [P, 2, P])
    v32 = sb0("v32", [P, 2, P])
    vtm = sb0("vtm", [P, P])
    KN = sb0("KN", [P, 2, NH, TP], F32R)
    KS = sb0("KS", [P, NG, HG, KW], F32R)
    KST = sb0("KST", [P, NG, HG * TP], F32R)
    VM = sb0("VM", [P, NG, HG * VST], F32R)
    VT = sb0("VT", [P, NG, P], F32R)
    q32 = sb0("q32", [P, NT, P])
    QN = sb0("QN", [P, NT, NH, TP], F32R)
    QS = sb0("QS", [P, NG, S], F32R)
    NM = sb0("NM", [P, NT, NH])
    P32 = sb0("P32", [P, 2, S])
    Phi = sb0("Phi", [P, 3, S], F32R)
    Plo = sb0("Plo", [P, 3, S], F32R)
    rz = sb0("rz", [64, S])
    OT = sb0("OT", [P, 2, S])
    lg = sb0("lg", [P, NT, E0])
    m8 = sb0("m8", [P, NT, 8])
    dl = sb0("dl", [P, NT, E0])
    sel = sb0("sel", [P, NT, E0])
    ex = sb0("ex", [P, NT, E0])
    wu = sb0("wu", [P, NT, E0])
    zr = sb0("zr", [P, NT])
    rr = sb0("rr", [P, NT])
    wn = sb0("wn", [P, NT, E0])
    WN = sb0("WN", [P, NT, 2 * E0], F32R)
    WT = sb0("WT", [2 * E0, S], F32R)
    WB = sb0("WB", [P, 2, S])
    layer0.close()

    gus = sb("gus", [P, 2, 2 * NP1 * P], F32R)
    dns = sb("dns", [P, 2, NP1 * P], F32R)
    shs = sb("shs", [P, 2, 3 * P], F32R)
    pick1r = sb("pick1r", [2 * E1, E1, I1], F32R)
    ctxC = sb("ctxC", [P, CPAD])
    xi = sb("xi", [P, NT, P])
    xiT = sb("xiT", [P, S])
    QT1 = sb("QT1", [P, S])
    KT1 = sb("KT1", [P, S])
    V1 = sb("V1", [P, NT, P])
    nm1 = sb("nm1", [P, NT])
    nb1 = sb("nb1", [P, NT])
    z1 = sb("z1", [P, NT])
    r1 = sb("r1", [P, NT])
    P1 = sb("P1", [P, 2, S])
    PN1 = sb("PN1", [P, 2, S])
    PT = sb("PT", [P, NT, S])
    att = sb("att", [P, NT, P])
    attT = sb("attT", [P, S])
    a1 = sb("a1", [P, NT, P])
    gn = sb("gn", [P, NT, P])
    normed = sb("normed", [P, NT, P])
    norm1 = sb("norm1", [P, NT, P])
    Q2T = sb("Q2T", [P, S])
    K2T = sb("K2T", [P, LK])
    V2m = sb("V2m", [P, P])
    V2t = sb("V2t", [TP, P])
    nm2 = sb("nm2", [P, NT])
    nb2 = sb("nb2", [P, NT])
    z2 = sb("z2", [P, NT])
    r2 = sb("r2", [P, NT])
    P2 = sb("P2", [P, NT, LK])
    PN2 = sb("PN2", [P, NT, LK])
    P2T = sb("P2T", [P, S])
    P2Tt = sb("P2Tt", [TP, S])
    a2 = sb("a2", [P, NT, P])
    norm2 = sb("norm2", [P, NT, P])
    norm2b = sb("norm2b", [P, NT, P])
    n2T = sb("n2T", [P, S])
    hu = sb("hu", [P, S])
    hT = sb("hT", [P, S])
    a3 = sb("a3", [P, NT, P])
    norm3 = sb("norm3", [P, NT, P])
    x3 = sb("x3", [P, NT, P])
    sc1 = sb("sc1", [P, NT, E1])
    sfc = sb("sfc", [P, NT, E1])
    gsc = sb("gsc", [P, NT, GRP + 8 - TOPG])
    gm8 = sb("gm8", [P, NT, 8])
    grp = sb("grp", [P, NT, GRP + 8 - TOPG])
    gmk = sb("gmk", [P, NT, GRP])
    mks = sb("mks", [P, NT, E1 + 8 - TOPK])
    em8 = sb("em8", [P, NT, 8])
    erp = sb("erp", [P, NT, E1 + 8 - TOPK])
    esl = sb("esl", [P, NT, E1])
    tw = sb("tw", [P, NT, E1])
    tz = sb("tz", [P, NT])
    tr = sb("tr", [P, NT])
    cw = sb("cw", [P, NT, E1])
    CN = sb("CN", [P, NT, 2 * E1], F32R)
    CT = sb("CT", [2 * E1, S], F32R)
    s32 = sb("s32", [P, 2, S])
    t32 = sb("t32", [P, 2, S])
    oT = sb("oT", [P, S])
    xo = sb("xo", [P, NT, P])

    class Norm:
        def __init__(self, name, eps):
            self.eps = eps
            self.st = sb(name + "_st", [P, NT, 6])
            self.mv = sb(name + "_mv", [P, NT, 2])
            self.ve = sb(name + "_ve", [P, NT])
            self.y0 = sb(name + "_y0", [P, NT])
            self.t = sb(name + "_t", [P, 4, NT])
            self.steps = sig(name + "_steps", 2 * NT + 4)
            self.power = sig(name + "_power", 2)
            self.out = sig(name + "_out", NT)

        def vector(self, eng, b, src, dst):
            for i in range(NT):
                nc.vector.bn_stats(self.st[:, i, :], src[:, i, :]).then_inc(self.steps.sem, 1)
            eng.wait_ge(self.steps.sem, self.steps.at(b, NT))
            apart(eng, b)
            for i in range(NT):
                nc.vector.bn_aggr(self.mv[:, i, :], self.st[:, i, :]).then_inc(self.steps.sem, 1)
            yield
            eng.wait_ge(self.power.sem, self.power.at(b, 2))
            y0, t, n = self.y0[:], self.t, self.steps
            nc.vector.tensor_tensor(t[:, 0, :], y0, y0, ALU.mult).then_inc(n.sem, 1)
            eng.wait_ge(n.sem, n.at(b, 2 * NT + 1))
            nc.vector.tensor_tensor(t[:, 1, :], t[:, 0, :], self.ve[:], ALU.mult).then_inc(n.sem, 1)
            eng.wait_ge(n.sem, n.at(b, 2 * NT + 2))
            nc.vector.tensor_scalar(t[:, 2, :], t[:, 1, :], -0.5, 1.5, ALU.mult, ALU.add).then_inc(n.sem, 1)
            eng.wait_ge(n.sem, n.at(b, 2 * NT + 3))
            nc.vector.tensor_tensor(t[:, 3, :], t[:, 2, :], y0, ALU.mult).then_inc(n.sem, 1)
            eng.wait_ge(n.sem, n.at(b, 2 * NT + 4))
            for i in range(NT):
                nc.vector.tensor_scalar(dst[:, i, :], src[:, i, :], self.mv[:, i, 0:1], t[:, 3, i:i + 1],
                                        ALU.subtract, ALU.mult).then_inc(self.out.sem, 1)

        def gpsimd(self, eng, b):
            eng.wait_ge(self.steps.sem, self.steps.at(b, 2 * NT))
            apart(eng, b)
            nc.gpsimd.tensor_scalar(self.ve[:], self.mv[:, :, 1], self.eps, None, ALU.add).then_inc(self.power.sem, 1)
            eng.wait_ge(self.power.sem, self.power.at(b, 1))
            nc.gpsimd.tensor_tensor(self.y0[:], self.ve[:], mhalf[:], ALU.pow).then_inc(self.power.sem, 1)

    ln_a, ln_b = Norm("ln_a", 1e-5), Norm("ln_b", 1e-5)
    ln_c, ln_d = Norm("ln_c", 1e-5), Norm("ln_d", 1e-5)
    ln_n1, ln_n2, ln_n3 = (Norm(n, 1e-3) for n in ("ln_n1", "ln_n2", "ln_n3"))

    small_loaded = sig("small_loaded", 0)
    passed = sig("passed", 0)
    const_set = sig("const_set", 0)
    raw_loaded = [sig(f"raw_loaded{i}", 0) for i in range(2)]
    raw_hi = sig("raw_hi", 0)
    raw_lo = sig("raw_lo", 0)
    layer0_done = sig("layer0_done", 0)
    a_x_in, a_ctx_in = sig("a_x_in", 16), sig("a_ctx_in", 32)
    a_xb = sig("a_xb", 1)
    a_kv_ps, a_kv = sig("a_kv_ps", 1), sig("a_kv", 2)
    a_mk, a_km, a_kn, a_vm = sig("a_mk", 2), sig("a_km", 2), sig("a_kn", 5), sig("a_vm", 2 + 2 * HG)
    a_kt_ps, a_ks, a_kst = sig("a_kt_ps", 2), sig("a_ks", 8), sig("a_kst", 1)
    a_xT_ps, a_xT, a_q_ps, a_q32, a_qn = (sig(n, k) for n, k in (
        ("a_xT_ps", 1), ("a_xT", 1), ("a_q_ps", 1), ("a_q32", 1), ("a_qn", 4)))
    a_qt_ps, a_qs = sig("a_qt_ps", NG), sig("a_qs", NG)
    NM_UNITS = NG * NT * 2
    a_m_ps, a_nm, a_nmq = sig("a_m_ps", NM_UNITS), sig("a_nm", NM_UNITS), sig("a_nmq", 2 * NG)
    a_q2_ps, a_q2s = sig("a_q2_ps", NG), sig("a_q2s", NG)
    NU = HG + 1
    a_s_ps, a_exp, a_phi = (sig(n, NG * NU) for n in ("a_s_ps", "a_exp", "a_phi"))
    PLO_G = (1, 3)
    a_plo_v, a_plo_g = sig("a_plo_v", NG * (NU - len(PLO_G))), sig("a_plo_g", NG * len(PLO_G))
    a_pv, a_rz, a_ot = sig("a_pv", NG * NU), sig("a_rz", NG), sig("a_ot", NG)
    a_y_ps, a_x1 = sig("a_y_ps", 1), sig("a_x1", 1)
    b_xT_ps, b_xT, b_xs, b_lg_ps, b_lg = (sig(n, k) for n, k in (
        ("b_xT_ps", 1), ("b_xT", 1), ("b_xs", 2), ("b_lg_ps", 1), ("b_lg", 1)))
    b_m8, b_sd, b_ex, b_w = sig("b_m8", NT), sig("b_sd", 2), sig("b_ex", 1), sig("b_w", 6)
    b_wt_ps, b_wt, b_base_ps, b_base = (sig(n, 1) for n in ("b_wt_ps", "b_wt", "b_base_ps", "b_base"))
    b_wb_ps, b_wb = sig("b_wb_ps", E0), sig("b_wb", E0)
    b_h_ps, b_gelu, b_hhi, b_hlo, b_y = (sig(n, NC0) for n in ("b_h_ps", "b_gelu", "b_hhi", "b_hlo", "b_y"))
    b_ty, b_acc = sig("b_ty", E0), sig("b_acc", E0)
    b_o_ps, b_x2 = sig("b_o_ps", 1), sig("b_x2", 1)
    c_ctx_in = sig("c_ctx_in", 16)
    c_kv2_ps, c_kv2, c_xT_ps, c_xT = sig("c_kv2_ps", 1), sig("c_kv2", 3), sig("c_xT_ps", 1), sig("c_xT", 1)
    c_qkv_ps, c_qv, c_k = sig("c_qkv_ps", 3), sig("c_qv", 2), sig("c_k", 1)
    c_s_ps, c_msk, c_nm, c_nb, c_p, c_r, c_pn, c_pt_ps, c_pt = (sig(n, NT) for n in (
        "c_s_ps", "c_msk", "c_nm", "c_nb", "c_p", "c_r", "c_pn", "c_pt_ps", "c_pt"))
    c_att_ps, c_att, c_attT_ps, c_attT, c_q2_ps, c_q2 = (sig(n, k) for n, k in (
        ("c_att_ps", 1), ("c_att", 2), ("c_attT_ps", 1), ("c_attT", 1), ("c_q2_ps", 1), ("c_q2", 1)))
    c_s2_ps, c_nm2, c_p2, c_pn2 = sig("c_s2_ps", 2), sig("c_nm2", 3), sig("c_p2", NT), sig("c_pn2", 2)
    c_p2t_ps, c_p2t, c_p2tt, c_att2_ps = (sig(n, 1) for n in ("c_p2t_ps", "c_p2t", "c_p2tt", "c_att2_ps"))
    c_n1, c_a2, c_n2, c_n2b, c_n2T_ps, c_n2T, c_h_ps, c_h, c_ff_ps, c_a3, c_n3, c_x3 = (sig(n, k) for n, k in (
        ("c_n1", 2), ("c_a2", 1), ("c_n2", 2), ("c_n2b", 1), ("c_n2T_ps", 1), ("c_n2T", 1), ("c_h_ps", 1),
        ("c_h", 2), ("c_ff_ps", 1), ("c_a3", 1), ("c_n3", 2), ("c_x3", 1)))
    ND = NP1 + 1
    d_xT_ps, d_xT, d_xs, d_lg_ps, d_sig = (sig(n, k) for n, k in (
        ("d_xT_ps", 1), ("d_xT", 1), ("d_xs", 2), ("d_lg_ps", 1), ("d_sig", 1)))
    d_r = sig("d_r", 12 + 4 * NT)
    d_ct_ps, d_ct = sig("d_ct_ps", 1), sig("d_ct", 1)
    d_g_ps, d_u_ps, d_silu, d_t, d_hi, d_lo, d_dn = (sig(n, ND) for n in (
        "d_g_ps", "d_u_ps", "d_silu", "d_t", "d_hi", "d_lo", "d_dn"))
    d_cb_ps, d_h = sig("d_cb_ps", NP1), sig("d_h", NP1)
    d_oT, d_o_ps, d_x4, d_out = sig("d_oT", 1), sig("d_o_ps", 1), sig("d_x4", 1), sig("d_out", 16)

    x_dram = a["x"].rearrange("b (i p) d -> b p i d", p=P)
    out_dram = a["out"].rearrange("b (i p) d -> b p i d", p=P)

    def four(bk):
        return bk.rearrange("p (i d) -> p i d", i=NT)

    def over_tiles(row, n=NT):
        return row.unsqueeze(1).to_broadcast([row.shape[0], n, row.shape[1]])

    def pieces(dram, split):
        w = dram.shape[1]
        return [(dram[:, c:c + min(1024, w - c)], min(1024, w - c), split, c) for c in range(0, w, 1024)]

    pieces0 = pieces(a["w1"], w1s) + pieces(a["w2"], w2s)
    pieces1 = pieces(a["sh"], shs) + pieces(a["gu"], gus) + pieces(a["dn"], dns)
    NP0, NPC = len(pieces0), len(pieces0) + len(pieces1)

    stage0 = [h32[:].rearrange("p a b -> p (a b)"), ty[:].rearrange("p a b -> p (a b)")]
    stage1 = [s32[:].rearrange("p a b -> p (a b)"), t32[:].rearrange("p a b -> p (a b)")]

    def staged(n):
        return stage0[n % 2] if n < NP0 else stage1[n % 2]

    all_pieces = pieces0 + pieces1
    small = [(ident, a["ident"]), (valid, a["valid"]), (pick0, a["pick0"]), (pick1, a["pick1"]), (trimask, a["trimask"]), (w_o, a["wo"]), (w_r, a["wr"]),
             (w_gate, a["wgate"]), (b1T, a["b1T"]), (b1f, a["b1f"]), (b2dup, a["b2dup"])]
    small += [(w_in[n], a["w_" + n]) for n in w_in]
    small_rows = [(rows[n], a["row_" + n]) for n in rows] + [(row_br, a["row_br"]), (row_gb, a["row_gb"])]
    NSMALL = 16 * (len(small) + len(small_rows))
    NCONST = 6
    NCONST_V = 2 + 2 * (1 + HG) + 1

    order = [("M", 0, m) for m in range(2 * NT)]
    for g in range(NG):
        m_next = [("M", g + 1, m) for m in range(2 * NT)] if g + 1 < NG else []
        s_now = [("S", g, u) for u in range(NU)]
        while m_next or s_now:
            order += m_next[:2]
            m_next = m_next[2:]
            order += s_now[:1]
            s_now = s_now[1:]
    s_slot = {}
    m_slot = {}
    for pos, (kind, g, u) in enumerate(order):
        if kind == "S":
            s_slot[g * NU + u] = pos % 2
        else:
            m_slot[g * 2 * NT + u] = pos % 2

    def prob_low(eng, b, n):
        if n < 0:
            eng.wait_ge(a_plo_v.sem, a_plo_v.at(b, 0))
            eng.wait_ge(a_plo_g.sem, a_plo_g.at(b, 0))
        elif n % NU in PLO_G:
            eng.wait_ge(a_plo_g.sem, a_plo_g.at(b, n // NU * len(PLO_G) + PLO_G.index(n % NU) + 1))
        else:
            rest = [u for u in range(NU) if u not in PLO_G]
            eng.wait_ge(a_plo_v.sem, a_plo_v.at(b, n // NU * len(rest) + rest.index(n % NU) + 1))

    block = ctx.enter_context(nc.Block())

    @block.sync
    def _(sp):
        def load_x(b):
            sp.wait_ge(a_xb.sem, a_xb.at(b, 0))
            apart(sp, b)
            sp.wait_ge(ln_a.out.sem, ln_a.out.at(b, 0))
            apart(sp, b)
            sp.dma_start(x_in[:], x_dram[b]).then_inc(a_x_in.sem, 16)
            sp.wait_ge(a_kv_ps.sem, a_kv_ps.at(b, 0))
            apart(sp, b)
            sp.wait_ge(a_mk.sem, a_mk.at(b, 0))
            apart(sp, b)
            sp.dma_start(ctxA[:], a["ctxT"][b]).then_inc(a_ctx_in.sem, 16)
            sp.dma_start(mask8[:], a["mask"][b]).then_inc(a_ctx_in.sem, 16)

        for t, d in small:
            sp.dma_start(t[:], d).then_inc(small_loaded.sem, 16)
        for t, d in small_rows:
            sp.dma_start(t[:], d.partition_broadcast(P)).then_inc(small_loaded.sem, 16)
        load_x(0)
        with sp.Fori(1, NB) as b:
            load_x(b)
        sp.wait_ge(layer0_done.sem, 4)

        def layer1(b):
            sp.wait_ge(c_kv2_ps.sem, c_kv2_ps.at(b, 0))
            apart(sp, b)
            sp.dma_start(ctxC[:], a["ctxT"][b]).then_inc(c_ctx_in.sem, 16)
            sp.wait_ge(d_x4.sem, d_x4.at(b, 1))
            apart(sp, b)
            sp.dma_start(out_dram[b], xo[:]).then_inc(d_out.sem, 16)

        layer1(0)
        with sp.Fori(1, NB) as b:
            layer1(b)
        sp.wait_ge(d_out.sem, d_out.at(NB - 1, 16))

    @block.gpsimd
    def _(pool):
        def load_piece(n):
            if n >= 2 and n != NP0 and n != NP0 + 1:
                pool.wait_ge(raw_lo.sem, n - 1)
            src, w, _, _ = all_pieces[n]
            pool.dma_start(staged(n)[:, 0:w], src).then_inc(raw_loaded[n % 2].sem, 16)

        def split(first, last):
            for n in range(first, min(first + 2, last)):
                load_piece(n)
            for n in range(first, last):
                _, w, dst, c = all_pieces[n]
                pool.wait_ge(raw_loaded[n % 2].sem, 16 * (n // 2 + 1))
                pool.wait_ge(raw_hi.sem, n + 1)
                nc.gpsimd.tensor_tensor(dst[:, 1, c:c + w], staged(n)[:, 0:w], dst[:, 0, c:c + w].bitcast(F32),
                                        ALU.subtract).then_inc(raw_lo.sem, 1)
                if n + 2 < last:
                    load_piece(n + 2)

        def stage_a(b):
            pool.wait_ge(a_x_in.sem, a_x_in.at(b, 16))
            pool.wait_ge(a_x1.sem, a_x1.at(b, 0))
            nc.gpsimd.tensor_tensor(xb[:], x_in[:], over_tiles(rows["bo"][:]), ALU.add).then_inc(a_xb.sem, 1)
            ln_a.gpsimd(pool, b)
            pool.wait_ge(a_ks.sem, a_ks.at(b, 2 * HG))
            pool.wait_ge(a_s_ps.sem, a_s_ps.at(b, 0))
            apart(pool, b)
            nc.gpsimd.tensor_copy(KST[:].rearrange("p g (j k) -> p g j k", j=HG), KS[:, :, :, P:KW].bitcast(F32)).then_inc(a_kst.sem, 1)
            for g in range(NG):
                for m, u in enumerate(PLO_G):
                    n = g * NU + u
                    pool.wait_ge(a_phi.sem, a_phi.at(b, n + 1))
                    pool.wait_ge(a_pv.sem, a_pv.at(b, max(0, n - 2)))
                    nc.gpsimd.tensor_tensor(Plo[:, n % 3, :], P32[:, n % 2, :], Phi[:, n % 3, :].bitcast(F32),
                                            ALU.subtract).then_inc(a_plo_g.sem, 1)
                    yield

        def stage_b(b):
            ln_b.gpsimd(pool, b)
            for e in range(E0):
                pool.wait_ge(b_ty.sem, b_ty.at(b, e + 1))
                pool.wait_ge(b_base.sem, b_base.at(b, 1))
                if e:
                    pool.wait_ge(b_acc.sem, b_acc.at(b, e))
                nc.gpsimd.tensor_tensor(acc_o[:], acc_o[:], ty[:, e % 2, :], ALU.add).then_inc(b_acc.sem, 1)
                yield

        def stage_c(b):
            ln_c.gpsimd(pool, b)
            ln_n1.gpsimd(pool, b)
            ln_n2.gpsimd(pool, b)
            pool.wait_ge(c_n2.sem, c_n2.at(b, 2))
            pool.wait_ge(c_a3.sem, c_a3.at(b, 0))
            nc.gpsimd.tensor_tensor(norm2b[:], norm2[:], over_tiles(rows["b2f"][:]), ALU.add).then_inc(c_n2b.sem, 1)
            ln_n3.gpsimd(pool, b)
            yield

        def stage_d(b):
            ln_d.gpsimd(pool, b)
            yield

        nc.gpsimd.memset(mhalf[:], -0.5).then_inc(const_set.sem, 1)
        nc.gpsimd.memset(KN[:].bitcast(F32), 0.0).then_inc(const_set.sem, 1)
        nc.gpsimd.memset(KS[:].bitcast(F32), 0.0).then_inc(const_set.sem, 1)
        nc.gpsimd.memset(VM[:].bitcast(F32), 0.0).then_inc(const_set.sem, 1)
        nc.gpsimd.memset(VT[:].bitcast(F32), 0.0).then_inc(const_set.sem, 1)
        nc.gpsimd.memset(QN[:].bitcast(F32), 0.0).then_inc(const_set.sem, 1)
        pool.wait_ge(const_set.sem, 1)
        split(0, NP0)
        for _ in chain(stage_a(0), stage_b(0)):
            pass
        with pool.Fori(1, NB) as b:
            for _ in chain(stage_a(b), stage_b(b)):
                pass
        pool.drain().then_inc(layer0_done.sem, 1)
        pool.wait_ge(layer0_done.sem, 4)
        split(NP0, NPC)
        for _ in chain(stage_c(0), stage_d(0)):
            pass
        with pool.Fori(1, NB) as b:
            for _ in chain(stage_c(b), stage_d(b)):
                pass

    @block.scalar
    def _(act):
        def copy(dst, src):
            return nc.scalar.activation(dst, src, ACT.Copy)

        def split(first, last):
            for n in range(first, last):
                _, w, dst, c = all_pieces[n]
                act.wait_ge(raw_loaded[n % 2].sem, 16 * (n // 2 + 1))
                copy(dst[:, 0, c:c + w], staged(n)[:, 0:w]).then_inc(raw_hi.sem, 1)

        def stage_a(b):
            for h in range(2):
                act.wait_ge(a_kt_ps.sem, a_kt_ps.at(b, h + 1))
                src = (RING[1] if h == 0 else ACC)[:, 0:2 * KW].rearrange("p (g k) -> p g k", g=2)
                act.wait_ge(a_s_ps.sem, a_s_ps.at(b, 0))
                for j in range(HG):
                    q = slice(TP * j, TP * j + TP)
                    copy(KS[q, 2 * h:2 * h + 2, j, :], src[q]).then_inc(a_ks.sem, 1)
            act.wait_ge(a_xT_ps.sem, a_xT_ps.at(b, 1))
            copy(xT[:], MISC).then_inc(a_xT.sem, 1)
            for g in range(NG):
                act.wait_ge(a_qt_ps.sem, a_qt_ps.at(b, g + 1))
                copy(QS[:, g, :], RING[g % 2]).then_inc(a_qs.sem, 1)
            yield
            for g in range(NG):
                act.wait_ge(a_q2_ps.sem, a_q2_ps.at(b, g + 1))
                copy(QS[:, g, :], MISC).then_inc(a_q2s.sem, 1)
                for u in range(NU):
                    n = g * NU + u
                    act.wait_ge(a_s_ps.sem, a_s_ps.at(b, n + 1))
                    prob_low(act, b, n - 2)
                    nc.scalar.activation(P32[:, n % 2, :], RING[s_slot[n]], ACT.Exp,
                                         scale=float(1 / np.sqrt(HD))).then_inc(a_exp.sem, 1)
                    act.wait_ge(a_exp.sem, a_exp.at(b, n + 1))
                    act.wait_ge(a_pv.sem, a_pv.at(b, max(0, n - 2)))
                    copy(Phi[:, n % 3, :], P32[:, n % 2, :]).then_inc(a_phi.sem, 1)
                yield

        def stage_b(b):
            act.wait_ge(b_xT_ps.sem, b_xT_ps.at(b, 1))
            copy(xT32[:], bank[3]).then_inc(b_xT.sem, 1)
            act.wait_ge(b_sd.sem, b_sd.at(b, 1))
            nc.scalar.activation(ex[:], dl[:], ACT.Exp).then_inc(b_ex.sem, 1)
            yield

            def spread(e):
                act.wait_ge(b_wb_ps.sem, b_wb_ps.at(b, e + 1))
                act.wait_ge(b_ty.sem, b_ty.at(b, max(0, e - 1)))
                copy(WB[:, e % 2, :], bank[3]).then_inc(b_wb.sem, 1)

            for c in range(NC0):
                act.wait_ge(b_h_ps.sem, b_h_ps.at(b, c + 1))
                act.wait_ge(b_hlo.sem, b_hlo.at(b, max(0, c - 1)))
                nc.scalar.activation(h32[:, c % 2, :], bank[c % 2], ACT.Gelu, bias=b1T[:, c:c + 1]).then_inc(b_gelu.sem, 1)
                act.wait_ge(b_gelu.sem, b_gelu.at(b, c + 1))
                act.wait_ge(b_y.sem, b_y.at(b, max(0, c - 2)))
                copy(hhi[:, c % 3, :], h32[:, c % 2, :]).then_inc(b_hhi.sem, 1)
                if c == 2:
                    act.wait_ge(b_wt_ps.sem, b_wt_ps.at(b, 1))
                    copy(WT[:], bank[3][0:2 * E0, :]).then_inc(b_wt.sem, 1)
                    act.wait_ge(b_base_ps.sem, b_base_ps.at(b, 1))
                    copy(acc_o[:], bank[3]).then_inc(b_base.sem, 1)
                if c % 4 == 3:
                    spread(c // 4)
                yield

        def stage_c(b):
            act.wait_ge(c_kv2_ps.sem, c_kv2_ps.at(b, 1))
            copy(K2T[:], RING[0][:, 0:LK]).then_inc(c_kv2.sem, 1)
            copy(V2m[:], RING[1][:, 0:P]).then_inc(c_kv2.sem, 1)
            copy(V2t[:], RING[1][0:TP, P:2 * P]).then_inc(c_kv2.sem, 1)
            act.wait_ge(c_xT_ps.sem, c_xT_ps.at(b, 1))
            copy(xiT[:], MISC).then_inc(c_xT.sem, 1)
            act.wait_ge(c_qkv_ps.sem, c_qkv_ps.at(b, 1))
            copy(QT1[:], RING[0]).then_inc(c_qv.sem, 1)
            act.wait_ge(c_qkv_ps.sem, c_qkv_ps.at(b, 3))
            copy(V1[:], four(ACC)).then_inc(c_qv.sem, 1)
            yield
            scale1 = float(1 / np.sqrt(np.float32(S)))
            scale2 = float(1 / np.sqrt(np.float32(LK)))
            for i in range(NT):
                w = (i + 1) * P
                act.wait_ge(c_nb.sem, c_nb.at(b, i + 1))
                act.wait_ge(c_pn.sem, c_pn.at(b, max(0, i - 1)))
                nc.scalar.activation(P1[:, i % 2, 0:w], RING[i % 2][:, 0:w], ACT.Exp, bias=nb1[:, i:i + 1],
                                     scale=scale1, accum_out=z1[:, i:i + 1]).then_inc(c_p.sem, 1)
                if i:
                    move_pt(b, i - 1)
            move_pt(b, NT - 1)
            act.wait_ge(c_attT_ps.sem, c_attT_ps.at(b, 1))
            copy(attT[:], MISC).then_inc(c_attT.sem, 1)
            act.wait_ge(c_q2_ps.sem, c_q2_ps.at(b, 1))
            copy(Q2T[:], RING[0]).then_inc(c_q2.sem, 1)
            act.wait_ge(c_nm2.sem, c_nm2.at(b, 3))
            yield
            for i in range(NT):
                src = (RING[1] if i < 2 else ACC)[:, 0:2 * KW].rearrange("p (i k) -> p i k", i=2)
                nc.scalar.activation(P2[:, i, :], src[:, i % 2, 0:LK], ACT.Exp, bias=nb2[:, i:i + 1],
                                     scale=scale2, accum_out=z2[:, i:i + 1]).then_inc(c_p2.sem, 1)
            act.wait_ge(c_p2t_ps.sem, c_p2t_ps.at(b, 1))
            copy(P2T[:], RING[0]).then_inc(c_p2t.sem, 1)
            act.wait_ge(c_n2T_ps.sem, c_n2T_ps.at(b, 1))
            copy(n2T[:], MISC).then_inc(c_n2T.sem, 1)
            yield

        def move_pt(b, i):
            act.wait_ge(c_pt_ps.sem, c_pt_ps.at(b, i + 1))
            copy(PT[:, 0:i + 1, i * P:(i + 1) * P], four(MISC)[:, 0:i + 1, :]).then_inc(c_pt.sem, 1)

        def stage_d(b):
            act.wait_ge(d_xT_ps.sem, d_xT_ps.at(b, 1))
            copy(xT32[:], bank[3]).then_inc(d_xT.sem, 1)
            act.wait_ge(d_lg_ps.sem, d_lg_ps.at(b, 1))
            nc.scalar.activation(sc1[:], bank[3][:, 0:NT * E1].rearrange("p (i e) -> p i e", i=NT),
                                 ACT.Sigmoid).then_inc(d_sig.sem, 1)
            yield

            def high(n):
                if n == 0:
                    act.wait_ge(d_t.sem, d_t.at(b, 1))
                else:
                    act.wait_ge(d_h.sem, d_h.at(b, n))
                act.wait_ge(d_dn.sem, d_dn.at(b, max(0, n - 2)))
                copy(hhi[:, n % 3, :], (t32 if n == 0 else h32)[:, n % 2, :]).then_inc(d_hi.sem, 1)

            for n in range(ND):
                act.wait_ge(d_g_ps.sem, d_g_ps.at(b, n + 1))
                act.wait_ge(d_t.sem, d_t.at(b, max(0, n - 1)))
                nc.scalar.activation(s32[:, n % 2, :], bank[0], ACT.Silu).then_inc(d_silu.sem, 1)
                if n == 1:
                    act.wait_ge(d_ct_ps.sem, d_ct_ps.at(b, 1))
                    copy(CT[:], bank[3][0:2 * E1, :]).then_inc(d_ct.sem, 1)
                if n:
                    high(n - 1)
                yield
            high(ND - 1)
            act.wait_ge(d_dn.sem, d_dn.at(b, ND))
            copy(oT[:], bank[2]).then_inc(d_oT.sem, 1)

        split(0, NP0)
        for _ in chain(stage_a(0), stage_b(0)):
            pass
        with act.Fori(1, NB) as b:
            for _ in chain(stage_a(b), stage_b(b)):
                pass
        act.drain().then_inc(layer0_done.sem, 1)
        act.wait_ge(layer0_done.sem, 4)
        split(NP0, NPC)
        for _ in chain(stage_c(0), stage_d(0)):
            pass
        with act.Fori(1, NB) as b:
            for _ in chain(stage_c(b), stage_d(b)):
                pass

    @block.vector
    def _(dve):
        V = nc.vector
        c_hi, c_lo = f32r_parts(-MASK_FILL * np.sqrt(HD))

        def stage_a(b):
            dve.wait_ge(a_ctx_in.sem, a_ctx_in.at(b, 32))
            V.tensor_copy(mk[:], mask8[:]).then_inc(a_mk.sem, 1)
            dve.wait_ge(a_mk.sem, a_mk.at(b, 1))
            V.tensor_tensor(mkd[:], mk[:], valid[:], ALU.subtract).then_inc(a_mk.sem, 1)
            dve.wait_ge(a_kv_ps.sem, a_kv_ps.at(b, 1))
            kps = RING[0][:, 0:2 * P].rearrange("p (t d) -> p t d", t=2)
            vps = RING[0][:, 2 * P:4 * P].rearrange("p (t d) -> p t d", t=2)
            V.tensor_tensor(k32[:], kps, over_tiles(rows["bk"][:], 2), ALU.add).then_inc(a_kv.sem, 1)
            V.tensor_tensor(v32[:], vps, over_tiles(rows["bv"][:], 2), ALU.add).then_inc(a_kv.sem, 1)
            dve.wait_ge(a_kv.sem, a_kv.at(b, 1))
            V.tensor_tensor(km[:], k32[:], mk[:].unsqueeze(2).to_broadcast([P, 2, P]), ALU.mult).then_inc(a_km.sem, 1)
            dve.wait_ge(a_kv.sem, a_kv.at(b, 2))
            V.tensor_scalar(vtm[:], v32[:, 1, :], valid[:, 1:2], None, ALU.mult).then_inc(a_km.sem, 1)
            dve.wait_ge(a_kt_ps.sem, a_kt_ps.at(b, 0))
            kh = km[:].rearrange("p t (h d) -> p t h d", d=HD)
            dve.wait_ge(a_km.sem, a_km.at(b, 1))
            V.tensor_copy(KN[:, :, :, 0:HD], kh).then_inc(a_kn.sem, 1)
            V.tensor_copy(KN[:, :, :, HD:2 * HD], kh).then_inc(a_kn.sem, 1)
            dve.wait_ge(a_mk.sem, a_mk.at(b, 2))
            pen = mkd[:].unsqueeze(2).unsqueeze(3).to_broadcast([P, 2, NH, 1])
            V.tensor_scalar(KN[:, :, :, 26:27], pen, c_hi, None, ALU.mult).then_inc(a_kn.sem, 1)
            V.tensor_scalar(KN[:, :, :, 27:28], pen, c_lo, None, ALU.mult).then_inc(a_kn.sem, 1)
            dve.wait_ge(a_kn.sem, a_kn.at(b, 1))
            V.tensor_tensor(KN[:, :, :, 2 * HD:3 * HD], kh, KN[:, :, :, 0:HD].bitcast(F32), ALU.subtract).then_inc(a_kn.sem, 1)
            yield
            dve.wait_ge(a_x_in.sem, a_x_in.at(b, 16))
            dve.wait_ge(a_xT_ps.sem, a_xT_ps.at(b, 0))
            yield from ln_a.vector(dve, b, x_in, xn)
            dve.wait_ge(a_pv.sem, a_pv.at(b, 0))
            vm = VM[:].rearrange("p g (j s) -> p g j s", s=VST)
            vh = v32[:, 0, :].rearrange("p (g j d) -> p g j d", j=HG, d=HD)
            V.tensor_copy(vm[:, :, :, 0:HD], vh).then_inc(a_vm.sem, 1)
            dve.wait_ge(a_km.sem, a_km.at(b, 2))
            vt = vtm[:].rearrange("p (g j d) -> p g j d", j=HG, d=HD)
            for j in range(HG):
                q, o = slice(TP * j, TP * j + TP), HD * j
                V.tensor_copy(VT[q, :, o:o + HD], vt[q, :, j, :]).then_inc(a_vm.sem, 1)
            dve.wait_ge(a_vm.sem, a_vm.at(b, 1))
            V.tensor_tensor(vm[:, :, :, 32:32 + HD], vh, vm[:, :, :, 0:HD].bitcast(F32), ALU.subtract).then_inc(a_vm.sem, 1)
            dve.wait_ge(a_vm.sem, a_vm.at(b, 1 + HG))
            for j in range(HG):
                q, o = slice(TP * j, TP * j + TP), HD * j
                V.tensor_tensor(VT[q, :, 32 + o:32 + o + HD], vt[q, :, j, :], VT[q, :, o:o + HD].bitcast(F32),
                                ALU.subtract).then_inc(a_vm.sem, 1)
            dve.wait_ge(a_q_ps.sem, a_q_ps.at(b, 1))
            V.tensor_tensor(q32[:], four(MISC), over_tiles(rows["bq"][:]), ALU.add).then_inc(a_q32.sem, 1)
            dve.wait_ge(a_q2_ps.sem, a_q2_ps.at(b, 0))
            dve.wait_ge(a_q32.sem, a_q32.at(b, 1))
            qh = q32[:].rearrange("p i (h d) -> p i h d", d=HD)
            V.tensor_copy(QN[:, :, :, 0:HD], qh).then_inc(a_qn.sem, 1)
            V.tensor_copy(QN[:, :, :, 2 * HD:3 * HD], qh).then_inc(a_qn.sem, 1)
            V.memset(QN[:, :, :, 24:26].bitcast(F32), 0.0).then_inc(a_qn.sem, 1)
            dve.wait_ge(a_qn.sem, a_qn.at(b, 1))
            V.tensor_tensor(QN[:, :, :, HD:2 * HD], qh, QN[:, :, :, 0:HD].bitcast(F32), ALU.subtract).then_inc(a_qn.sem, 1)
            yield

            def normalise(g):
                dve.wait_ge(a_pv.sem, a_pv.at(b, NU * (g + 1)))
                V.reciprocal(rz[:], ACC[64:128, :]).then_inc(a_rz.sem, 1)
                dve.wait_ge(a_rz.sem, a_rz.at(b, g + 1))
                if g == 0:
                    dve.wait_ge(a_y_ps.sem, a_y_ps.at(b, 0))
                o = 64 * (g % 2)
                V.tensor_tensor(OT[o:o + 64, g // 2, :], ACC[0:64, :], rz[:], ALU.mult).then_inc(a_ot.sem, 1)

            for kind, g, u in order:
                if kind == "M":
                    n = g * 2 * NT + u
                    i, half = divmod(u, 2)
                    dve.wait_ge(a_m_ps.sem, a_m_ps.at(b, n + 1))
                    src = RING[m_slot[n]][:, 0:2 * KW].rearrange("p (h k) -> p h k", h=2)[:, :, 0:LK]
                    h = HG * g + 2 * half
                    V.tensor_reduce(NM[:, i, h:h + 2], src, AX.X, ALU.max, negate=True).then_inc(a_nm.sem, 1)
                    if u == 2 * NT - 1:
                        dve.wait_ge(a_nm.sem, a_nm.at(b, n + 1))
                        nm = NM[:, :, HG * g:HG * g + HG].unsqueeze(3)
                        V.tensor_copy(QN[:, :, HG * g:HG * g + HG, 24:25], nm).then_inc(a_nmq.sem, 1)
                        dve.wait_ge(a_nmq.sem, a_nmq.at(b, 2 * g + 1))
                        V.tensor_tensor(QN[:, :, HG * g:HG * g + HG, 25:26], nm,
                                        QN[:, :, HG * g:HG * g + HG, 24:25].bitcast(F32), ALU.subtract).then_inc(a_nmq.sem, 1)
                else:
                    n = g * NU + u
                    if u not in PLO_G:
                        dve.wait_ge(a_phi.sem, a_phi.at(b, n + 1))
                        dve.wait_ge(a_pv.sem, a_pv.at(b, max(0, n - 2)))
                        V.tensor_tensor(Plo[:, n % 3, :], P32[:, n % 2, :], Phi[:, n % 3, :].bitcast(F32),
                                        ALU.subtract).then_inc(a_plo_v.sem, 1)
                    if u == 1 and g:
                        normalise(g - 1)
                    yield
            normalise(NG - 1)
            dve.wait_ge(b_x2.sem, b_x2.at(b, 0))
            dve.wait_ge(a_xb.sem, a_xb.at(b, 1))
            dve.wait_ge(a_y_ps.sem, a_y_ps.at(b, 1))
            V.tensor_tensor(x1[:], four(MISC), xb[:], ALU.add).then_inc(a_x1.sem, 1)
            yield

        def split_xT(b, ready, done):
            dve.wait_ge(ready.sem, ready.at(b, 1))
            V.tensor_copy(xThi[:], xT32[:]).then_inc(done.sem, 1)
            dve.wait_ge(done.sem, done.at(b, 1))
            V.tensor_tensor(xTlo[:], xT32[:], xThi[:].bitcast(F32), ALU.subtract).then_inc(done.sem, 1)

        def stage_b(b):
            dve.wait_ge(a_x1.sem, a_x1.at(b, 1))
            yield from ln_b.vector(dve, b, x1, xn2)
            split_xT(b, b_xT, b_xs)
            dve.wait_ge(b_lg_ps.sem, b_lg_ps.at(b, 1))
            V.tensor_tensor(lg[:], bank[3][:, 0:NT * E0].rearrange("p (i e) -> p i e", i=NT),
                            over_tiles(row_br[:]), ALU.add).then_inc(b_lg.sem, 1)
            dve.wait_ge(b_lg.sem, b_lg.at(b, 1))
            apart(dve, b)
            for i in range(NT):
                V.max(m8[:, i, :], lg[:, i, :]).then_inc(b_m8.sem, 1)
            dve.wait_ge(b_m8.sem, b_m8.at(b, NT))
            V.tensor_tensor(dl[:], lg[:], m8[:, :, 0:1].to_broadcast([P, NT, E0]), ALU.subtract).then_inc(b_sd.sem, 1)
            V.tensor_tensor(sel[:], lg[:], m8[:, :, 1:2].to_broadcast([P, NT, E0]), ALU.is_ge).then_inc(b_sd.sem, 1)
            dve.wait_ge(b_sd.sem, b_sd.at(b, 2))
            dve.wait_ge(b_ex.sem, b_ex.at(b, 1))
            V.tensor_tensor(wu[:], ex[:], sel[:], ALU.mult).then_inc(b_w.sem, 1)
            dve.wait_ge(b_w.sem, b_w.at(b, 1))
            V.reduce_sum(zr[:], wu[:], AX.X).then_inc(b_w.sem, 1)
            dve.wait_ge(b_w.sem, b_w.at(b, 2))
            V.reciprocal(rr[:], zr[:]).then_inc(b_w.sem, 1)
            dve.wait_ge(b_w.sem, b_w.at(b, 3))
            V.tensor_tensor(wn[:], wu[:], rr[:].unsqueeze(2).to_broadcast([P, NT, E0]), ALU.mult).then_inc(b_w.sem, 1)
            dve.wait_ge(b_w.sem, b_w.at(b, 4))
            V.tensor_copy(WN[:, :, 0:E0], wn[:]).then_inc(b_w.sem, 1)
            dve.wait_ge(b_w.sem, b_w.at(b, 5))
            V.tensor_tensor(WN[:, :, E0:2 * E0], wn[:], WN[:, :, 0:E0].bitcast(F32), ALU.subtract).then_inc(b_w.sem, 1)
            yield

            def weigh(e):
                dve.wait_ge(b_y.sem, b_y.at(b, 4 * e + 4))
                dve.wait_ge(b_wb.sem, b_wb.at(b, e + 1))
                dve.wait_ge(b_acc.sem, b_acc.at(b, max(0, e - 1)))
                V.tensor_tensor(ty[:, e % 2, :], bank[2], WB[:, e % 2, :], ALU.mult).then_inc(b_ty.sem, 1)

            for c in range(NC0):
                dve.wait_ge(b_hhi.sem, b_hhi.at(b, c + 1))
                dve.wait_ge(b_y.sem, b_y.at(b, max(0, c - 2)))
                V.tensor_tensor(hlo[:, c % 3, :], h32[:, c % 2, :], hhi[:, c % 3, :].bitcast(F32),
                                ALU.subtract).then_inc(b_hlo.sem, 1)
                if c % 4 == 1 and c > 4:
                    weigh(c // 4 - 1)
                yield
            weigh(E0 - 1)
            dve.wait_ge(b_o_ps.sem, b_o_ps.at(b, 1))
            V.tensor_tensor(X2[:, b, :, :], four(bank[3]), x1[:], ALU.add).then_inc(b_x2.sem, 1)

        def affine(src, dst, b, done):
            V.tensor_tensor(gn[:], src, over_tiles(rows["gamma"][:]), ALU.mult).then_inc(done.sem, 1)
            dve.wait_ge(done.sem, done.at(b, 1))
            V.tensor_tensor(dst[:], gn[:], over_tiles(rows["beta"][:]), ALU.add).then_inc(done.sem, 1)

        def stage_c(b):
            yield from ln_c.vector(dve, b, X2[:, b, :, :], xi)
            dve.wait_ge(c_qkv_ps.sem, c_qkv_ps.at(b, 2))
            V.tensor_copy(KT1[:], RING[1]).then_inc(c_k.sem, 1)
            scale1 = float(1 / np.sqrt(np.float32(S)))
            scale2 = float(1 / np.sqrt(np.float32(LK)))

            def scale_rows(i):
                w = (i + 1) * P
                dve.wait_ge(c_p.sem, c_p.at(b, i + 1))
                V.reciprocal(r1[:, i:i + 1], z1[:, i:i + 1]).then_inc(c_r.sem, 1)
                dve.wait_ge(c_r.sem, c_r.at(b, i + 1))
                dve.wait_ge(c_pt_ps.sem, c_pt_ps.at(b, max(0, i - 1)))
                V.tensor_scalar(PN1[:, i % 2, 0:w], P1[:, i % 2, 0:w], r1[:, i:i + 1], None, ALU.mult).then_inc(c_pn.sem, 1)

            for i in range(NT):
                w = (i + 1) * P
                dve.wait_ge(c_s_ps.sem, c_s_ps.at(b, i + 1))
                diag = RING[i % 2][:, i * P:w]
                V.tensor_tensor(diag, diag, trimask[:], ALU.add).then_inc(c_msk.sem, 1)
                dve.wait_ge(c_msk.sem, c_msk.at(b, i + 1))
                V.tensor_reduce(nm1[:, i:i + 1], RING[i % 2][:, 0:w], AX.X, ALU.max, negate=True).then_inc(c_nm.sem, 1)
                dve.wait_ge(c_nm.sem, c_nm.at(b, i + 1))
                V.tensor_scalar(nb1[:, i:i + 1], nm1[:, i:i + 1], scale1, None, ALU.mult).then_inc(c_nb.sem, 1)
                if i:
                    scale_rows(i - 1)
            scale_rows(NT - 1)
            yield
            dve.wait_ge(c_att_ps.sem, c_att_ps.at(b, 1))
            V.tensor_copy(att[:], four(ACC)).then_inc(c_att.sem, 1)
            V.tensor_tensor(a1[:], four(ACC), xi[:], ALU.add).then_inc(c_att.sem, 1)
            dve.wait_ge(c_att.sem, c_att.at(b, 2))
            yield from ln_n1.vector(dve, b, a1, normed)
            for h in range(2):
                src = (RING[1] if h == 0 else ACC)[:, 0:2 * KW].rearrange("p (i k) -> p i k", i=2)[:, :, 0:LK]
                dve.wait_ge(c_s2_ps.sem, c_s2_ps.at(b, h + 1))
                V.tensor_reduce(nm2[:, 2 * h:2 * h + 2], src, AX.X, ALU.max, negate=True).then_inc(c_nm2.sem, 1)
            dve.wait_ge(c_nm2.sem, c_nm2.at(b, 2))
            V.tensor_scalar(nb2[:], nm2[:], scale2, None, ALU.mult).then_inc(c_nm2.sem, 1)
            dve.wait_ge(ln_n1.out.sem, ln_n1.out.at(b, NT))
            affine(normed[:], norm1, b, c_n1)
            dve.wait_ge(c_p2.sem, c_p2.at(b, NT))
            V.reciprocal(r2[:], z2[:]).then_inc(c_pn2.sem, 1)
            dve.wait_ge(c_pn2.sem, c_pn2.at(b, 1))
            V.tensor_tensor(PN2[:], P2[:], r2[:].unsqueeze(2).to_broadcast([P, NT, LK]), ALU.mult).then_inc(c_pn2.sem, 1)
            dve.wait_ge(c_p2t_ps.sem, c_p2t_ps.at(b, 1))
            V.tensor_copy(P2Tt[0:LT, :], ACC[0:LT, :]).then_inc(c_p2tt.sem, 1)
            dve.wait_ge(c_att2_ps.sem, c_att2_ps.at(b, 1))
            dve.wait_ge(c_n1.sem, c_n1.at(b, 2))
            V.tensor_tensor(a2[:], four(RING[1]), norm1[:], ALU.add).then_inc(c_a2.sem, 1)
            dve.wait_ge(c_a2.sem, c_a2.at(b, 1))
            yield from ln_n2.vector(dve, b, a2, normed)
            dve.wait_ge(ln_n2.out.sem, ln_n2.out.at(b, NT))
            affine(normed[:], norm2, b, c_n2)
            dve.wait_ge(c_h_ps.sem, c_h_ps.at(b, 1))
            V.tensor_scalar(hu[:], RING[0], b1f[:, 0:1], None, ALU.add).then_inc(c_h.sem, 1)
            dve.wait_ge(c_h.sem, c_h.at(b, 1))
            V.scalar_tensor_tensor(hT[:], hu[:], 0.2, hu[:], ALU.mult, ALU.max).then_inc(c_h.sem, 1)
            dve.wait_ge(c_ff_ps.sem, c_ff_ps.at(b, 1))
            dve.wait_ge(c_n2b.sem, c_n2b.at(b, 1))
            V.tensor_tensor(a3[:], four(RING[1]), norm2b[:], ALU.add).then_inc(c_a3.sem, 1)
            dve.wait_ge(c_a3.sem, c_a3.at(b, 1))
            yield from ln_n3.vector(dve, b, a3, normed)
            dve.wait_ge(ln_n3.out.sem, ln_n3.out.at(b, NT))
            affine(normed[:], norm3, b, c_n3)
            dve.wait_ge(c_n3.sem, c_n3.at(b, 2))
            dve.wait_ge(d_x4.sem, d_x4.at(b, 0))
            V.scalar_tensor_tensor(x3[:].rearrange("p i d -> p (i d)"), norm3[:].rearrange("p i d -> p (i d)"), 0.0,
                                   X2[:, b, :, :].rearrange("p i d -> p (i d)"), ALU.max, ALU.add).then_inc(c_x3.sem, 1)

        def stage_d(b):
            dve.wait_ge(c_x3.sem, c_x3.at(b, 1))
            yield from ln_d.vector(dve, b, x3, xn2)
            split_xT(b, d_xT, d_xs)
            k = 0

            def step(ins):
                nonlocal k
                k += 1
                ins.then_inc(d_r.sem, 1)
                dve.wait_ge(d_r.sem, d_r.at(b, k))
                apart(dve, b)

            dve.wait_ge(d_sig.sem, d_sig.at(b, 1))
            step(V.tensor_tensor(sfc[:], sc1[:], over_tiles(row_gb[:]), ALU.add))
            step(V.tensor_reduce(gsc[:, :, 0:GRP], sfc[:].rearrange("p i (g s) -> p i g s", s=GS), AX.X, ALU.max))
            for i in range(NT):
                step(V.max(gm8[:, i, :], gsc[:, i, :]))
            for i in range(NT):
                step(V.match_replace(grp[:, i, :], gm8[:, i, :], gsc[:, i, :], -BIG))
            step(V.tensor_scalar(gmk[:], grp[:, :, 0:GRP], -BIG, None, ALU.is_equal))
            step(V.tensor_tensor(mks[:, :, 0:E1].rearrange("p i (g s) -> p i g s", s=GS),
                                 sfc[:].rearrange("p i (g s) -> p i g s", s=GS),
                                 gmk[:].unsqueeze(3).to_broadcast([P, NT, GRP, GS]), ALU.mult))
            for i in range(NT):
                step(V.max(em8[:, i, :], mks[:, i, :]))
            for i in range(NT):
                step(V.match_replace(erp[:, i, :], em8[:, i, :], mks[:, i, :], -BIG))
            step(V.tensor_scalar(esl[:], erp[:, :, 0:E1], -BIG, None, ALU.is_equal))
            step(V.tensor_tensor(tw[:], sc1[:], esl[:], ALU.mult))
            step(V.reduce_sum(tz[:], tw[:], AX.X))
            step(V.tensor_scalar(tz[:], tz[:], 1e-20, None, ALU.add))
            step(V.reciprocal(tr[:], tz[:]))
            step(V.scalar_tensor_tensor(cw[:], tw[:], 2.5, tr[:].unsqueeze(2).to_broadcast([P, NT, E1]), ALU.mult, ALU.mult))
            step(V.tensor_copy(CN[:, :, 0:E1], cw[:]))
            V.tensor_tensor(CN[:, :, E1:2 * E1], cw[:], CN[:, :, 0:E1].bitcast(F32), ALU.subtract).then_inc(d_r.sem, 1)
            yield

            def low(n):
                dve.wait_ge(d_hi.sem, d_hi.at(b, n + 1))
                dve.wait_ge(d_dn.sem, d_dn.at(b, max(0, n - 2)))
                V.tensor_tensor(hlo[:, n % 3, :], (t32 if n == 0 else h32)[:, n % 2, :], hhi[:, n % 3, :].bitcast(F32),
                                ALU.subtract).then_inc(d_lo.sem, 1)

            for n in range(ND):
                dve.wait_ge(d_silu.sem, d_silu.at(b, n + 1))
                dve.wait_ge(d_u_ps.sem, d_u_ps.at(b, n + 1))
                dve.wait_ge(d_lo.sem, d_lo.at(b, max(0, n - 1)))
                V.tensor_tensor(t32[:, n % 2, :], s32[:, n % 2, :], bank[1], ALU.mult).then_inc(d_t.sem, 1)
                if n:
                    dve.wait_ge(d_t.sem, d_t.at(b, n + 1))
                    dve.wait_ge(d_cb_ps.sem, d_cb_ps.at(b, n))
                    V.tensor_tensor(h32[:, n % 2, :], t32[:, n % 2, :], bank[3], ALU.mult).then_inc(d_h.sem, 1)
                    low(n - 1)
                yield
            low(ND - 1)
            dve.wait_ge(d_o_ps.sem, d_o_ps.at(b, 1))
            dve.wait_ge(d_out.sem, d_out.at(b, 0))
            V.tensor_tensor(xo[:], four(bank[3]), x3[:], ALU.add).then_inc(d_x4.sem, 1)

        dve.wait_ge(small_loaded.sem, NSMALL)
        dve.wait_ge(const_set.sem, NCONST)
        V.tensor_copy(KN[:, :, :, 24:26], valid[:].unsqueeze(2).unsqueeze(3).to_broadcast([P, 2, NH, 2])).then_inc(const_set.sem, 1)
        V.memset(QN[:, :, :, 26:28].bitcast(F32), 1.0).then_inc(const_set.sem, 1)
        vm = VM[:].rearrange("p g (j s) -> p g j s", s=VST)
        for o in (64, 96):
            V.memset(vm[:, :, :, o:o + HD].bitcast(F32), 1.0).then_inc(const_set.sem, 1)
            for j in range(HG):
                q, c = slice(TP * j, TP * j + TP), o + HD * j
                V.tensor_copy(VT[q, :, c:c + HD], valid[q, 1:2].unsqueeze(2).to_broadcast([TP, NG, HD])).then_inc(const_set.sem, 1)
        V.tensor_copy(pick0r[:], pick0[:]).then_inc(const_set.sem, 1)
        dve.wait_ge(const_set.sem, NCONST + NCONST_V)
        for _ in chain(stage_a(0), stage_b(0)):
            pass
        with dve.Fori(1, NB) as b:
            for _ in chain(stage_a(b), stage_b(b)):
                pass
        dve.drain().then_inc(layer0_done.sem, 1)
        dve.wait_ge(layer0_done.sem, 4)
        V.memset(gsc[:, :, GRP:], BIG).then_inc(const_set.sem, 1)
        V.tensor_copy(pick1r[:], pick1[:].unsqueeze(2).to_broadcast([2 * E1, E1, I1])).then_inc(const_set.sem, 1)
        V.memset(mks[:, :, E1:], BIG).then_inc(const_set.sem, 1)
        dve.wait_ge(const_set.sem, NCONST + NCONST_V + 3)
        for _ in chain(stage_c(0), stage_d(0)):
            pass
        with dve.Fori(1, NB) as b:
            for _ in chain(stage_c(b), stage_d(b)):
                pass

    @block.tensor
    def _(pe):
        M = nc.tensor.matmul

        def transpose4(dst, src):
            for i in range(NT):
                last = nc.tensor.transpose(dst[:, i * P:(i + 1) * P], src[:, i, :], ident[:])
            return last

        def product3(dst, w, x_hi, x_lo, start, stop):
            M(dst, w[0], x_hi, start=start, stop=False)
            M(dst, w[1], x_hi, start=False, stop=False)
            return M(dst, w[0], x_lo, start=False, stop=stop)

        def stage_a(b):
            pe.wait_ge(a_ctx_in.sem, a_ctx_in.at(b, 32))
            pe.wait_ge(a_exp.sem, a_exp.at(b, 0))
            for t in range(2):
                M(RING[0][:, t * P:(t + 1) * P], ctxA[:, t * P:(t + 1) * P], w_in["k"][:], start=True, stop=True)
            for t in range(2):
                last = M(RING[0][:, (2 + t) * P:(3 + t) * P], ctxA[:, t * P:(t + 1) * P], w_in["v"][:], start=True, stop=True)
            last.then_inc(a_kv_ps.sem, 1)
            yield
            pe.wait_ge(a_kn.sem, a_kn.at(b, 5))
            pe.wait_ge(a_ot.sem, a_ot.at(b, 0))
            for h in range(2):
                dst = (RING[1] if h == 0 else ACC)[:, 0:2 * KW].rearrange("p (g k) -> p g k", g=2)
                for gg in range(2):
                    g = 2 * h + gg
                    src = KN[:, :, HG * g:HG * g + HG, :].rearrange("p t h c -> p t (h c)").bitcast(F32)
                    nc.tensor.transpose(dst[:, gg, 0:P], src[:, 0, :], ident[:])
                    last = nc.tensor.transpose(dst[:, gg, P:KW], src[0:TP, 1, :], ident[0:TP, 0:TP])
                last.then_inc(a_kt_ps.sem, 1)
            pe.wait_ge(ln_a.out.sem, ln_a.out.at(b, NT))
            pe.wait_ge(a_x1.sem, a_x1.at(b, 0))
            transpose4(MISC, xn).then_inc(a_xT_ps.sem, 1)
            pe.wait_ge(a_xT.sem, a_xT.at(b, 1))
            for i in range(NT):
                last = M(four(MISC)[:, i, :], xT[:, i * P:(i + 1) * P], w_in["q"][:], start=True, stop=True)
            last.then_inc(a_q_ps.sem, 1)
            yield
            pe.wait_ge(a_qn.sem, a_qn.at(b, 4))

            def query_stack(dst, g):
                for i in range(NT):
                    src = QN[:, i, HG * g:HG * g + HG, :].rearrange("p h c -> p (h c)").bitcast(F32)
                    last = nc.tensor.transpose(dst[:, i * P:(i + 1) * P], src, ident[:])
                return last

            for g in range(NG):
                if g == 0:
                    pe.wait_ge(a_kv.sem, a_kv.at(b, 2))
                elif g == 1:
                    pe.wait_ge(a_ks.sem, a_ks.at(b, HG))
                else:
                    pe.wait_ge(a_qs.sem, a_qs.at(b, g - 1))
                query_stack(RING[g % 2], g).then_inc(a_qt_ps.sem, 1)
            pe.wait_ge(a_qs.sem, a_qs.at(b, NG))
            pe.wait_ge(a_ks.sem, a_ks.at(b, 2 * HG))
            pe.wait_ge(a_vm.sem, a_vm.at(b, 2 + 2 * HG))
            pe.wait_ge(a_kst.sem, a_kst.at(b, 1))

            def released(pos):
                if pos < 2:
                    return
                kind, g, u = order[pos - 2]
                if kind == "M":
                    pe.wait_ge(a_nm.sem, a_nm.at(b, g * 2 * NT + u + 1))
                else:
                    pe.wait_ge(a_exp.sem, a_exp.at(b, g * NU + u + 1))

            def weighted_values(n):
                g, u = divmod(n, NU)
                v = VM[:, g, P * u:P * u + P] if u < HG else VT[:, g, :]
                if u == 0:
                    pe.wait_ge(a_ot.sem, a_ot.at(b, g))
                pe.wait_ge(a_phi.sem, a_phi.at(b, n + 1))
                M(ACC, v, Phi[:, n % 3, :], start=(u == 0), stop=False)
                prob_low(pe, b, n)
                M(ACC, v, Plo[:, n % 3, :], start=False, stop=(u == NU - 1)).then_inc(a_pv.sem, 1)

            for pos, (kind, g, u) in enumerate(order):
                if kind == "M":
                    released(pos)
                    i, half = divmod(u, 2)
                    M(RING[pos % 2][:, 0:2 * KW], QS[:, g, i * P:(i + 1) * P],
                      KS[:, g, 2 * half:2 * half + 2, :].rearrange("p h k -> p (h k)"), start=True, stop=True).then_inc(a_m_ps.sem, 1)
                else:
                    n = g * NU + u
                    if u == 0:
                        pe.wait_ge(a_nmq.sem, a_nmq.at(b, 2 * g + 2))
                        pe.wait_ge(a_q2s.sem, a_q2s.at(b, g))
                        query_stack(MISC, g).then_inc(a_q2_ps.sem, 1)
                        pe.wait_ge(a_q2s.sem, a_q2s.at(b, g + 1))
                    released(pos)
                    keys = KS[:, g, u, 0:P] if u < HG else KST[:, g, :]
                    M(RING[pos % 2], keys, QS[:, g, :], start=True, stop=True).then_inc(a_s_ps.sem, 1)
                    if n >= 2:
                        weighted_values(n - 2)
                    yield
            weighted_values(NG * NU - 2)
            weighted_values(NG * NU - 1)
            pe.wait_ge(a_ot.sem, a_ot.at(b, NG))
            pe.wait_ge(a_q2s.sem, a_q2s.at(b, NG))
            for i in range(NT):
                for h in range(2):
                    last = M(four(MISC)[:, i, :], OT[:, h, i * P:(i + 1) * P], w_o[:, h, :], start=(h == 0), stop=(h == 1))
            last.then_inc(a_y_ps.sem, 1)
            yield

        def parts(w, c):
            return w[:, 0, c * P:(c + 1) * P], w[:, 1, c * P:(c + 1) * P]

        def stage_b(b):
            pe.wait_ge(ln_b.out.sem, ln_b.out.at(b, NT))
            pe.wait_ge(b_x2.sem, b_x2.at(b, 0))
            transpose4(bank[3], xn2).then_inc(b_xT_ps.sem, 1)
            pe.wait_ge(b_xT.sem, b_xT.at(b, 1))
            pe.wait_ge(b_xs.sem, b_xs.at(b, 2))
            for i in range(NT):
                last = M(bank[3][:, i * E0:(i + 1) * E0], xT32[:, i * P:(i + 1) * P], w_r[:], start=True, stop=True)
            last.then_inc(b_lg_ps.sem, 1)

            def second(c):
                if c % 4 == 0:
                    pe.wait_ge(b_ty.sem, b_ty.at(b, c // 4))
                pe.wait_ge(b_hhi.sem, b_hhi.at(b, c + 1))
                pe.wait_ge(b_hlo.sem, b_hlo.at(b, c + 1))
                product3(bank[2], parts(w2s, c), hhi[:, c % 3, :], hlo[:, c % 3, :], c % 4 == 0, c % 4 == 3).then_inc(b_y.sem, 1)

            for c in range(NC0):
                pe.wait_ge(b_gelu.sem, b_gelu.at(b, max(0, c - 1)))
                product3(bank[c % 2], parts(w1s, c), xThi[:], xTlo[:], True, True).then_inc(b_h_ps.sem, 1)
                if c == 2:
                    pe.wait_ge(b_w.sem, b_w.at(b, 6))
                    for i in range(NT):
                        last = nc.tensor.transpose(bank[3][0:2 * E0, i * P:(i + 1) * P], WN[:, i, :].bitcast(F32), ident[:])
                    last.then_inc(b_wt_ps.sem, 1)
                    pe.wait_ge(b_wt.sem, b_wt.at(b, 1))
                    M(bank[3], b2dup[:], WT[:].bitcast(F32), start=True, stop=True).then_inc(b_base_ps.sem, 1)
                if c % 4 == 3:
                    e = c // 4
                    if e == 0:
                        pe.wait_ge(b_base.sem, b_base.at(b, 1))
                    else:
                        pe.wait_ge(b_wb.sem, b_wb.at(b, e))
                    M(bank[3], spread0(e), WT[:], start=True, stop=True).then_inc(b_wb_ps.sem, 1)
                if c >= 2:
                    second(c - 2)
                yield
            second(NC0 - 2)
            second(NC0 - 1)
            pe.wait_ge(b_acc.sem, b_acc.at(b, E0))
            pe.wait_ge(b_wb.sem, b_wb.at(b, E0))
            transpose4(bank[3], acc_o[:].rearrange("p (i d) -> p i d", i=NT)).then_inc(b_o_ps.sem, 1)

        def spread0(e):
            return pick0r[:, e:e + 1].to_broadcast([2 * E0, P])

        def spread1(e):
            return pick1r[:, e:e + 2, :].rearrange("k e i -> k (e i)")

        def stage_c(b):
            pe.wait_ge(c_ctx_in.sem, c_ctx_in.at(b, 16))
            pe.wait_ge(c_a3.sem, c_a3.at(b, 0))
            M(RING[0][:, 0:LK], w_in["k2"][:], ctxC[:, 0:LK], start=True, stop=True)
            M(RING[1][:, 0:P], ctxC[:, 0:P], w_in["v2"][:], start=True, stop=True)
            M(RING[1][0:TP, P:2 * P], ctxC[:, P:KW], w_in["v2"][:], start=True, stop=True).then_inc(c_kv2_ps.sem, 1)
            pe.wait_ge(ln_c.out.sem, ln_c.out.at(b, NT))
            pe.wait_ge(c_n2T.sem, c_n2T.at(b, 0))
            transpose4(MISC, xi).then_inc(c_xT_ps.sem, 1)
            pe.wait_ge(c_xT.sem, c_xT.at(b, 1))
            pe.wait_ge(c_kv2.sem, c_kv2.at(b, 3))
            M(RING[0], w_in["q1"][:], xiT[:], start=True, stop=True).then_inc(c_qkv_ps.sem, 1)
            M(RING[1], w_in["k1"][:], xiT[:], start=True, stop=True).then_inc(c_qkv_ps.sem, 1)
            pe.wait_ge(c_p2tt.sem, c_p2tt.at(b, 0))
            for i in range(NT):
                last = M(four(ACC)[:, i, :], xiT[:, i * P:(i + 1) * P], w_in["v1"][:], start=True, stop=True)
            last.then_inc(c_qkv_ps.sem, 1)
            pe.wait_ge(c_qv.sem, c_qv.at(b, 1))
            pe.wait_ge(c_k.sem, c_k.at(b, 1))

            def turn(i):
                pe.wait_ge(c_pn.sem, c_pn.at(b, i + 1))
                pe.wait_ge(c_pt.sem, c_pt.at(b, i))
                for kc in range(i + 1):
                    last = nc.tensor.transpose(MISC[:, kc * P:(kc + 1) * P], PN1[:, i % 2, kc * P:(kc + 1) * P], ident[:])
                last.then_inc(c_pt_ps.sem, 1)

            def attend(i):
                pe.wait_ge(c_pt.sem, c_pt.at(b, i + 1))
                for kc in range(i + 1):
                    last = M(four(ACC)[:, i, :], PT[:, kc, i * P:(i + 1) * P], V1[:, kc, :], start=(kc == 0), stop=(kc == i))
                return last

            for i in range(NT):
                w = (i + 1) * P
                pe.wait_ge(c_p.sem, c_p.at(b, max(0, i - 1)))
                M(RING[i % 2][:, 0:w], QT1[:, i * P:w], KT1[:, 0:w], start=True, stop=True).then_inc(c_s_ps.sem, 1)
                if i == 1:
                    pe.wait_ge(c_qv.sem, c_qv.at(b, 2))
                if i:
                    turn(i - 1)
                    attend(i - 1)
            turn(NT - 1)
            attend(NT - 1).then_inc(c_att_ps.sem, 1)
            yield
            pe.wait_ge(c_att.sem, c_att.at(b, 1))
            transpose4(MISC, att).then_inc(c_attT_ps.sem, 1)
            pe.wait_ge(c_attT.sem, c_attT.at(b, 1))
            M(RING[0], w_in["q2"][:], attT[:], start=True, stop=True).then_inc(c_q2_ps.sem, 1)
            pe.wait_ge(c_q2.sem, c_q2.at(b, 1))
            pe.wait_ge(c_p.sem, c_p.at(b, NT))
            pe.wait_ge(c_att.sem, c_att.at(b, 2))
            for i in range(NT):
                dst = (RING[1] if i < 2 else ACC)[:, 0:2 * KW].rearrange("p (i k) -> p i k", i=2)
                last = M(dst[:, i % 2, 0:LK], Q2T[:, i * P:(i + 1) * P], K2T[:], start=True, stop=True)
                if i % 2:
                    last.then_inc(c_s2_ps.sem, 1)
            yield
            pe.wait_ge(c_pn2.sem, c_pn2.at(b, 2))
            for i in range(NT):
                nc.tensor.transpose(RING[0][:, i * P:(i + 1) * P], PN2[:, i, 0:P], ident[:])
            for i in range(NT):
                last = nc.tensor.transpose(ACC[0:LT, i * P:(i + 1) * P], PN2[:, i, P:LK], ident[:])
            last.then_inc(c_p2t_ps.sem, 1)
            pe.wait_ge(c_p2t.sem, c_p2t.at(b, 1))
            pe.wait_ge(c_p2tt.sem, c_p2tt.at(b, 1))
            for i in range(NT):
                M(four(RING[1])[:, i, :], P2T[:, i * P:(i + 1) * P], V2m[:], start=True, stop=False)
                last = M(four(RING[1])[:, i, :], P2Tt[0:LT, i * P:(i + 1) * P], V2t[0:LT, :], start=False, stop=True)
            last.then_inc(c_att2_ps.sem, 1)
            yield
            pe.wait_ge(c_n2.sem, c_n2.at(b, 2))
            transpose4(MISC, norm2).then_inc(c_n2T_ps.sem, 1)
            pe.wait_ge(c_n2T.sem, c_n2T.at(b, 1))
            M(RING[0], w_in["f1"][:], n2T[:], start=True, stop=True).then_inc(c_h_ps.sem, 1)
            pe.wait_ge(c_h.sem, c_h.at(b, 2))
            for i in range(NT):
                last = M(four(RING[1])[:, i, :], hT[:, i * P:(i + 1) * P], w_in["f2"][:], start=True, stop=True)
            last.then_inc(c_ff_ps.sem, 1)
            yield

        def stage_d(b):
            pe.wait_ge(ln_d.out.sem, ln_d.out.at(b, NT))
            pe.wait_ge(d_x4.sem, d_x4.at(b, 0))
            transpose4(bank[3], xn2).then_inc(d_xT_ps.sem, 1)
            pe.wait_ge(d_xT.sem, d_xT.at(b, 1))
            pe.wait_ge(d_xs.sem, d_xs.at(b, 2))
            for i in range(NT):
                last = M(bank[3][:, i * E1:(i + 1) * E1], xT32[:, i * P:(i + 1) * P], w_gate[:], start=True, stop=True)
            last.then_inc(d_lg_ps.sem, 1)

            def gate_up(n, k):
                return parts(shs, k) if n == 0 else parts(gus, 2 * (n - 1) + k)

            def down(n):
                pe.wait_ge(d_hi.sem, d_hi.at(b, n + 1))
                pe.wait_ge(d_lo.sem, d_lo.at(b, n + 1))
                w = parts(shs, 2) if n == 0 else parts(dns, n - 1)
                product3(bank[2], w, hhi[:, n % 3, :], hlo[:, n % 3, :], n == 0, n == ND - 1).then_inc(d_dn.sem, 1)

            pe.wait_ge(d_oT.sem, d_oT.at(b, 0))
            for n in range(ND):
                pe.wait_ge(d_silu.sem, d_silu.at(b, n))
                product3(bank[0], gate_up(n, 0), xThi[:], xTlo[:], True, True).then_inc(d_g_ps.sem, 1)
                pe.wait_ge(d_t.sem, d_t.at(b, n))
                product3(bank[1], gate_up(n, 1), xThi[:], xTlo[:], True, True).then_inc(d_u_ps.sem, 1)
                if n == 1:
                    pe.wait_ge(d_r.sem, d_r.at(b, d_r.per))
                    apart(pe, b)
                    for i in range(NT):
                        last = nc.tensor.transpose(bank[3][0:2 * E1, i * P:(i + 1) * P], CN[:, i, :].bitcast(F32), ident[:])
                    last.then_inc(d_ct_ps.sem, 1)
                    pe.wait_ge(d_ct.sem, d_ct.at(b, 1))
                if n:
                    pe.wait_ge(d_h.sem, d_h.at(b, n - 1))
                    M(bank[3], spread1(2 * (n - 1)), CT[:], start=True, stop=True).then_inc(d_cb_ps.sem, 1)
                if n >= 2:
                    down(n - 2)
                yield
            down(ND - 2)
            down(ND - 1)
            pe.wait_ge(d_oT.sem, d_oT.at(b, 1))
            pe.wait_ge(d_h.sem, d_h.at(b, NP1))
            transpose4(bank[3], oT[:].rearrange("p (i d) -> p i d", i=NT)).then_inc(d_o_ps.sem, 1)

        pe.wait_ge(small_loaded.sem, NSMALL)
        pe.wait_ge(const_set.sem, NCONST + NCONST_V)
        pe.wait_ge(raw_hi.sem, NP0)
        pe.wait_ge(raw_lo.sem, NP0)
        for _ in chain(stage_a(0), stage_b(0)):
            pass
        with pe.Fori(1, NB) as b:
            for _ in chain(stage_a(b), stage_b(b)):
                pass
        pe.drain().then_inc(layer0_done.sem, 1)
        pe.wait_ge(layer0_done.sem, 4)
        pe.wait_ge(const_set.sem, NCONST + NCONST_V + 3)
        pe.wait_ge(raw_hi.sem, NPC)
        pe.wait_ge(raw_lo.sem, NPC)
        for _ in chain(stage_c(0), stage_d(0)):
            pass
        with pe.Fori(1, NB) as b:
            for _ in chain(stage_c(b), stage_d(b)):
                pass

    ctx.close()


def kernel(**inputs):
    import concourse.bacc as bacc
    from concourse.bass_utils import run_bass_kernel_spmd

    i = {n: np.asarray(v) for n, v in inputs.items()}
    ctxT = np.zeros((NB, D, CPAD), np.float32)
    ctx_t = i["ctx_1024"].transpose(0, 2, 1)
    mask = np.zeros((NB, CPAD), bool)
    mask_in = i["mask_BxS2_bf1"]
    valid = np.zeros((CPAD,), np.float32)
    ctxT[:, :, 0:P], mask[:, 0:P], valid[0:P] = ctx_t[:, :, 0:P], mask_in[:, 0:P], 1.0
    for j in range(HG):
        o = P + TP * j
        ctxT[:, :, o:o + LT], mask[:, o:o + LT], valid[o:o + LT] = ctx_t[:, :, P:LK], mask_in[:, P:LK], 1.0
    woT = i["L0_xattn_Wo"].T
    wo = np.zeros((P, 2, D), np.float32)
    for g in range(NG):
        for part in range(2):
            o = 64 * (g % 2) + 32 * part
            wo[o:o + 32, g // 2] = woT[32 * g:32 * g + 32]
    gu = i["L1_ffn_experts_gate_up"].reshape(NP1, 2, 2, I1, D)
    arrays = {
        "x": i["x"],
        "ctxT": ctxT,
        "mask": mask.reshape(NB, 2, P).transpose(0, 2, 1),
        "valid": valid.reshape(2, P).T,
        "ident": np.eye(P, dtype=np.float32),
        "trimask": np.triu(np.full((P, P), -BIG, np.float32), k=1),
        "pick0": np.tile(np.eye(E0, dtype=np.float32), (2, 1)),
        "pick1": np.tile(np.eye(E1, dtype=np.float32), (2, 1)),
        "w_q": i["L0_xattn_Wq"].T, "w_k": i["L0_xattn_Wk"].T, "w_v": i["L0_xattn_Wv"].T, "wo": wo,
        "row_bq": i["L0_xattn_bq"], "row_bk": i["L0_xattn_bk"], "row_bv": i["L0_xattn_bv"], "row_bo": i["L0_xattn_bo"],
        "wr": i["L0_ffn_Wr"], "row_br": i["L0_ffn_br"],
        "w1": i["L0_ffn_W1"].transpose(1, 0, 2).reshape(D, E0 * H0),
        "b1T": i["L0_ffn_b1"].reshape(NC0, P).T,
        "w2": i["L0_ffn_W2"].reshape(NC0, P, D).transpose(1, 0, 2).reshape(P, NC0 * D),
        "b2dup": np.tile(i["L0_ffn_b2"], (2, 1)),
        "w_k1": i["L1_xattn_Wk1"], "w_q1": i["L1_xattn_Wq1"], "w_v1": i["L1_xattn_Wv1"],
        "w_k2": i["L1_xattn_Wk2"], "w_q2": i["L1_xattn_Wq2"], "w_v2": i["L1_xattn_Wv2"],
        "w_f1": i["L1_xattn_W1"], "b1f": i["L1_xattn_b1"].reshape(D, 1), "w_f2": i["L1_xattn_W2"],
        "row_b2f": i["L1_xattn_b2"], "row_gamma": i["L1_xattn_gamma"], "row_beta": i["L1_xattn_beta"],
        "wgate": i["L1_ffn_gate_weight"].T, "row_gb": i["L1_ffn_e_score_correction_bias"],
        "gu": gu.transpose(4, 0, 2, 1, 3).reshape(D, 2 * NP1 * P),
        "dn": i["L1_ffn_experts_down"].reshape(NP1, 2, D, I1).transpose(1, 3, 0, 2).reshape(P, NP1 * D),
        "sh": np.concatenate([i["L1_ffn_shared_gate_w"].T, i["L1_ffn_shared_up_w"].T, i["L1_ffn_shared_down_w"].T], 1),
    }
    arrays = {n: np.ascontiguousarray(v) for n, v in arrays.items()}
    nc = bacc.Bacc("TRN2", target_bir_lowering=False, num_devices=1)
    aps = {n: nc.dram_tensor(n + "_dram", v.shape, mybir.dt.from_np(v.dtype), kind="ExternalInput").ap()
           for n, v in arrays.items()}
    aps["out"] = nc.dram_tensor("out_dram", (NB, S, D), F32, kind="ExternalOutput").ap()
    build_program(nc, aps)
    r = run_bass_kernel_spmd(nc, [{n + "_dram": v for n, v in arrays.items()}], core_ids=[0])
    return r.results[0]["out_dram"]
```

```python
from contextlib import ExitStack

import numpy as np

import concourse.bass as bass
from concourse import mybir

F32 = mybir.dt.float32
F32R = mybir.dt.float32r
U8 = mybir.dt.uint8
ALU = mybir.AluOpType
ACT = mybir.ActivationFunctionType
AX = mybir.AxisListType

P = 128
NB, S, D = 4, 512, 128
NT = S // P
LK = 154
LT = LK - P
TP = 32
KW = P + TP
NH, HD = 16, 8
NG, HG = 4, 4
E0, H0 = 8, 512
NC0 = E0 * H0 // P
E1, I1 = 32, 64
NP1 = E1 * I1 // P
GRP, GS, TOPG, TOPK = 8, 4, 4, 6
NRAW1 = 3
CPAD = P + HG * TP
MASK_FILL = -1.0e8
BIG = 3.0e38
VST = P + HD


EARLY = [("w_k", P, P), ("w_v", P, P), ("w_q", P, P), ("ident", P, P), ("valid", P, 2), ("wo", P, 2 * P),
         ("wr", P, E0), ("b1T", P, NC0), ("b2dup", 2 * E0, P), ("pick0", 2 * E0, E0)]
LATE = [(n, P, P) for n in ("w_k1", "w_q1", "w_v1", "w_k2", "w_q2", "w_v2", "w_f1", "w_f2", "trimask")]
LATE += [("wgate", P, E1), ("b1f", P, 1), ("pick1", 2 * E1, E1)]
EARLY_ROWS = [("row_bk", 1, P), ("row_bv", 1, P), ("row_bq", 1, P), ("row_bo", 1, P), ("row_br", 1, E0)]
LATE_ROWS = [("row_b2f", 1, P), ("row_gamma", 1, P), ("row_beta", 1, P), ("row_gb", 1, E1)]


def width(pack):
    return sum(columns for _, _, columns in pack)


def f32r_parts(v):
    def rnd(u):
        m, e = np.frexp(np.float64(u))
        return float(np.ldexp(np.round(m * 4096.0) / 4096.0, e))
    hi = rnd(v)
    return hi, rnd(float(v) - hi)


def by_time(*parts):
    heads = [[next(p), k, p] for k, p in enumerate(parts)]
    while heads:
        head = min(heads, key=lambda h: h[:2])
        yield head[0]
        time = next(head[2], None)
        if time is None:
            heads.remove(head)
        else:
            assert time >= head[0]
            head[0] = time


def merged(*stages):
    for _ in by_time(*stages):
        pass


class Signal:

    def __init__(self, sem, per):
        self.sem, self.per = sem, per

    def at(self, b, k):
        return b * self.per + k


def build_program(nc, a):
    ctx = ExitStack()

    def sb(name, shape, dt=F32):
        return ctx.enter_context(nc.sbuf_tensor(name, shape, dt))

    def sb_right(name, shape, dt=F32):
        return ctx.enter_context(nc.sbuf_tensor(name, shape, dt, side="right"))

    signals = []

    def sig(name, per):
        s = Signal(ctx.enter_context(nc.semaphore(name)), per)
        signals.append(s)
        return s

    def apart(eng, b):
        if not isinstance(b, int):
            eng.sem_inc(passed.sem, 1)

    small = {}

    def packed(name, pack, broadcast=False):
        whole = sb(name, [P, width(pack)])
        at = 0
        for n, partitions, columns in pack:
            small[n] = whole[0:P if broadcast else partitions, at:at + columns]
            at += columns
        return whole

    early, late = packed("early", EARLY), packed("late", LATE)
    early_rows, late_rows = packed("early_rows", EARLY_ROWS, True), packed("late_rows", LATE_ROWS, True)
    mhalf = sb("mhalf", [P, NT])
    ident, trimask, valid = small["ident"], small["trimask"], small["valid"]
    w_in = {n: small["w_" + n] for n in ("q", "k", "v", "k1", "q1", "v1", "k2", "q2", "v2", "f1", "f2")}
    w_o = small["wo"].rearrange("p (h d) -> p h d", h=2)
    w_r, w_gate, b1T, b1f = small["wr"], small["wgate"], small["b1T"], small["b1f"]
    b2dup, pick0, pick1 = small["b2dup"], small["pick0"], small["pick1"]
    rows = {n: small["row_" + n] for n in ("bq", "bk", "bv", "bo", "b2f", "gamma", "beta")}
    row_br, row_gb = small["row_br"], small["row_gb"]
    pick0r = sb("pick0r", [2 * E0, E0], F32R)
    X2 = sb("X2", [P, NB, NT, P])

    ps = ctx.enter_context(nc.psum_tensor("ps", [P, 8, 512], F32))
    bank = [ps[:, i, :] for i in range(8)]
    RING, ACC, MISC = (bank[4], bank[5]), bank[6], bank[7]

    xn2 = sb("xn2", [P, NT, P])
    xT32 = sb("xT32", [P, S])
    xThi = sb("xThi", [P, S], F32R)
    xTlo = sb("xTlo", [P, S], F32R)
    h32 = sb("h32", [P, 3, S])
    hhi = sb("hhi", [P, 3, S], F32R)
    hlo = sb("hlo", [P, 3, S], F32R)
    ty = sb("ty", [P, 2, S])
    acc_o = sb("acc_o", [P, S])

    class Norm:
        def __init__(self, name, eps):
            self.eps = eps
            self.st = sb(name + "_st", [P, NT, 6])
            self.mv = sb(name + "_mv", [P, NT, 2])
            self.ve = sb(name + "_ve", [P, NT])
            self.y0 = sb(name + "_y0", [P, NT])
            self.t = sb(name + "_t", [P, 4, NT])
            self.steps = sig(name + "_steps", 2 * NT + 4)
            self.power = sig(name + "_power", 2)
            self.out = sig(name + "_out", NT)

        def vector(self, eng, b, src, dst, time):
            yield time
            for i in range(NT):
                nc.vector.bn_stats(self.st[:, i, :], src[:, i, :]).then_inc(self.steps.sem, 1)
            eng.wait_ge(self.steps.sem, self.steps.at(b, NT))
            apart(eng, b)
            for i in range(NT):
                nc.vector.bn_aggr(self.mv[:, i, :], self.st[:, i, :]).then_inc(self.steps.sem, 1)
            yield time + 1
            eng.wait_ge(self.power.sem, self.power.at(b, 2))
            y0, t, n = self.y0[:], self.t, self.steps
            nc.vector.tensor_tensor(t[:, 0, :], y0, y0, ALU.mult).then_inc(n.sem, 1)
            eng.wait_ge(n.sem, n.at(b, 2 * NT + 1))
            nc.vector.tensor_tensor(t[:, 1, :], t[:, 0, :], self.ve[:], ALU.mult).then_inc(n.sem, 1)
            eng.wait_ge(n.sem, n.at(b, 2 * NT + 2))
            nc.vector.tensor_scalar(t[:, 2, :], t[:, 1, :], -0.5, 1.5, ALU.mult, ALU.add).then_inc(n.sem, 1)
            eng.wait_ge(n.sem, n.at(b, 2 * NT + 3))
            nc.vector.tensor_tensor(t[:, 3, :], t[:, 2, :], y0, ALU.mult).then_inc(n.sem, 1)
            eng.wait_ge(n.sem, n.at(b, 2 * NT + 4))
            for i in range(NT):
                nc.vector.tensor_scalar(dst[:, i, :], src[:, i, :], self.mv[:, i, 0:1], t[:, 3, i:i + 1],
                                        ALU.subtract, ALU.mult).then_inc(self.out.sem, 1)

        def gpsimd(self, eng, b):
            eng.wait_ge(self.steps.sem, self.steps.at(b, 2 * NT))
            apart(eng, b)
            nc.gpsimd.tensor_scalar(self.ve[:], self.mv[:, :, 1], self.eps, None, ALU.add).then_inc(self.power.sem, 1)
            eng.wait_ge(self.power.sem, self.power.at(b, 1))
            nc.gpsimd.tensor_tensor(self.y0[:], self.ve[:], mhalf[:], ALU.pow).then_inc(self.power.sem, 1)

    ln_a, ln_b = Norm("ln_a", 1e-5), Norm("ln_b", 1e-5)
    ln_c, ln_d = Norm("ln_c", 1e-5), Norm("ln_d", 1e-5)
    ln_n1, ln_n2, ln_n3 = (Norm(n, 1e-3) for n in ("ln_n1", "ln_n2", "ln_n3"))

    own_a = ExitStack()

    def sb_a(name, shape, dt=F32):
        return own_a.enter_context(nc.sbuf_tensor(name, shape, dt))

    x_in = sb_a("x_in", [P, NT, P])
    xn = sb_a("xn", [P, NT, P])
    xT = sb_a("xT", [P, S])
    ctxA = sb_a("ctxA", [P, CPAD])
    mask8 = sb_a("mask8", [P, 2], U8)
    mk = sb_a("mk", [P, 2])
    mkd = sb_a("mkd", [P, 2])
    k32 = sb_a("k32", [P, 2, P])
    km = sb_a("km", [P, 2, P])
    v32 = sb_a("v32", [P, 2, P])
    vtm = sb_a("vtm", [P, P])
    KN = sb_a("KN", [P, 2, NH, TP], F32R)
    KS = sb_a("KS", [P, NG, HG, KW], F32R)
    KST = sb_a("KST", [P, NG, HG * TP], F32R)
    VM = sb_a("VM", [P, NG, HG * VST], F32R)
    VT = sb_a("VT", [P, NG, P], F32R)
    QN = sb_a("QN", [P, NT, NH, TP], F32R)
    QS = sb_a("QS", [P, NG, S], F32R)
    NM = sb_a("NM", [P, NT, NH])
    P32 = sb_a("P32", [P, 4, S])
    Phi = sb_a("Phi", [P, 4, S], F32R)
    Plo = sb_a("Plo", [P, 4, S], F32R)
    q32, OZ, OT = xn, xT, P32[:, 0:2, :]
    rz = sb_a("rz", [P, NT, 2 * HG])
    ON = sb_a("ON", [P, NT, NG, 2 * HG * HD])
    own_a.close()

    ctxC = sb("ctxC", [P, CPAD])
    xi = sb("xi", [P, NT, P])
    xiT = sb("xiT", [P, S])
    QT1 = sb("QT1", [P, S])
    KT1 = sb("KT1", [P, S])
    V1 = sb("V1", [P, NT, P])
    nm1 = sb("nm1", [P, NT])
    nb1 = sb("nb1", [P, NT])
    z1 = sb("z1", [P, NT])
    r1 = sb("r1", [P, NT])
    P1 = sb("P1", [P, 2, S])
    PN1 = sb("PN1", [P, 2, S])
    PT = sb("PT", [P, NT, S])
    att = sb("att", [P, NT, P])
    attT = sb("attT", [P, S])
    a1 = sb("a1", [P, NT, P])
    gn = sb("gn", [P, NT, P])
    normed = sb("normed", [P, NT, P])
    norm1 = sb("norm1", [P, NT, P])
    Q2T = sb("Q2T", [P, S])
    K2T = sb("K2T", [P, LK])
    V2m = sb("V2m", [P, P])
    V2t = sb("V2t", [TP, P])
    nm2 = sb("nm2", [P, NT])
    nb2 = sb("nb2", [P, NT])
    z2 = sb("z2", [P, NT])
    r2 = sb("r2", [P, NT])
    P2 = sb("P2", [P, NT, LK])
    PN2 = sb("PN2", [P, NT, LK])
    P2T = sb("P2T", [P, S])
    P2Tt = sb("P2Tt", [TP, S])
    norm2 = sb("norm2", [P, NT, P])
    norm2b = sb("norm2b", [P, NT, P])
    n2T = sb("n2T", [P, S])
    hu = sb("hu", [P, S])
    hT = sb("hT", [P, S])
    norm3 = sb("norm3", [P, NT, P])
    raw1 = sb("raw1", [P, NRAW1, 1024])

    own_b = ExitStack()

    def sb_b(name, shape, dt=F32):
        return own_b.enter_context(nc.sbuf_tensor(name, shape, dt, side="right"))

    w1s = sb_b("w1s", [P, 2, NC0 * P], F32R)
    w2s = sb_b("w2s", [P, 2, NC0 * P], F32R)
    lg = sb_b("lg", [P, NT, E0])
    m8 = sb_b("m8", [P, NT, 8])
    dl = sb_b("dl", [P, NT, E0])
    sel = sb_b("sel", [P, NT, E0])
    ex = sb_b("ex", [P, NT, E0])
    wu = sb_b("wu", [P, NT, E0])
    zr = sb_b("zr", [P, NT])
    rr = sb_b("rr", [P, NT])
    wn = sb_b("wn", [P, NT, E0])
    WN = sb_b("WN", [P, NT, 2 * E0], F32R)
    WT = sb_b("WT", [2 * E0, S], F32R)
    WB = sb_b("WB", [P, 2, S])
    own_b.close()

    gus = sb_right("gus", [P, 2, 2 * NP1 * P], F32R)
    dns = sb_right("dns", [P, 2, NP1 * P], F32R)
    shs = sb_right("shs", [P, 2, 3 * P], F32R)
    pick1r = sb_right("pick1r", [2 * E1, E1, I1], F32R)
    sc1 = sb_right("sc1", [P, NT, E1])
    sfc = sb_right("sfc", [P, NT, E1])
    gsc = sb_right("gsc", [P, NT, GRP + 8 - TOPG])
    gm8 = sb_right("gm8", [P, NT, 8])
    grp = sb_right("grp", [P, NT, GRP + 8 - TOPG])
    gmk = sb_right("gmk", [P, NT, GRP])
    mks = sb_right("mks", [P, NT, E1 + 8 - TOPK])
    em8 = sb_right("em8", [P, NT, 8])
    erp = sb_right("erp", [P, NT, E1 + 8 - TOPK])
    esl = sb_right("esl", [P, NT, E1])
    tw = sb_right("tw", [P, NT, E1])
    tz = sb_right("tz", [P, NT])
    tr = sb_right("tr", [P, NT])
    cw = sb_right("cw", [P, NT, E1])
    CN = sb_right("CN", [P, NT, 2 * E1], F32R)
    CT = sb_right("CT", [2 * E1, S], F32R)
    s32 = sb_right("s32", [P, 2, S])
    t32 = sb_right("t32", [P, 2, S])
    oT = acc_o
    xo = ty[:, 0, :].rearrange("p (i d) -> p i d", i=NT)

    early_loaded, late_loaded = sig("early_loaded", 0), sig("late_loaded", 0)
    passed = sig("passed", 0)
    const_set = sig("const_set", 0)
    raw_loaded = [sig(f"raw_loaded{i}", 0) for i in range(max(2, NRAW1))]
    raw_hi = sig("raw_hi", 0)
    raw_lo = sig("raw_lo", 0)
    layer0_done = sig("layer0_done", 0)
    a_x_in, a_ctx_in = sig("a_x_in", 16), sig("a_ctx_in", 32)
    a_xb = sig("a_xb", 1)
    a_kv_ps, a_kv = sig("a_kv_ps", 1), sig("a_kv", 2)
    a_mk, a_km, a_kn, a_vtail = sig("a_mk", 2), sig("a_km", 2), sig("a_kn", 5), sig("a_vtail", 2 * HG)
    a_vmain = sig("a_vmain", 2)
    a_kt_ps, a_ks, a_kst = sig("a_kt_ps", 2), sig("a_ks", 8), sig("a_kst", 1)
    a_xT_ps, a_xT, a_q_ps, a_q32, a_qn = (sig(n, k) for n, k in (
        ("a_xT_ps", 1), ("a_xT", 1), ("a_q_ps", 1), ("a_q32", 1), ("a_qn", 4)))
    a_qt_ps, a_qs = sig("a_qt_ps", NG), sig("a_qs", NG)
    NM_UNITS = NG * NT * 2
    a_m_ps, a_nm, a_nmq = sig("a_m_ps", NM_UNITS), sig("a_nm", NM_UNITS), sig("a_nmq", 2 * NG)
    a_q2_ps, a_q2s = sig("a_q2_ps", NG), sig("a_q2s", NG)
    NU = HG + 1
    a_s_ps, a_exp, a_phi = (sig(n, NG * NU) for n in ("a_s_ps", "a_exp", "a_phi"))
    PLO_G = (1, 3)
    PR = P32.shape[1]
    a_plo_v, a_plo_g = sig("a_plo_v", NG * (NU - len(PLO_G))), sig("a_plo_g", NG * len(PLO_G))
    a_pv, a_oz, a_ozt_ps, a_on = sig("a_pv", NG * NU), sig("a_oz", NG), sig("a_ozt_ps", NG), sig("a_on", 2 * NG)
    a_ot_ps, a_ot = sig("a_ot_ps", 2), sig("a_ot", 2)
    a_y_ps, a_x1 = sig("a_y_ps", 1), sig("a_x1", 1)
    b_xT_ps, b_xT, b_xs, b_lg_ps = (sig(n, k) for n, k in (
        ("b_xT_ps", 1), ("b_xT", 1), ("b_xs", 2), ("b_lg_ps", 1)))
    b_lg, b_sd, b_ex, b_w = sig("b_lg", 1 + NT), sig("b_sd", 2), sig("b_ex", 1), sig("b_w", 6)
    b_wt_ps, b_wt, b_base_ps, b_base = (sig(n, 1) for n in ("b_wt_ps", "b_wt", "b_base_ps", "b_base"))
    b_wb_ps, b_wb = sig("b_wb_ps", E0), sig("b_wb", E0)
    b_h_ps, b_gelu, b_y = (sig(n, NC0) for n in ("b_h_ps", "b_gelu", "b_y"))
    b_hhi_s, b_hhi_v, b_hlo_v, b_hlo_g = (sig(n, NC0 // 2) for n in ("b_hhi_s", "b_hhi_v", "b_hlo_v", "b_hlo_g"))
    HR = h32.shape[1]
    b_ty, b_acc = sig("b_ty", E0), sig("b_acc", E0)
    b_o_ps, b_x2 = sig("b_o_ps", 1), sig("b_x2", 1)
    c_ctx_in = sig("c_ctx_in", 16)
    c_kv2_ps, c_kv2, c_xT_ps, c_xT = sig("c_kv2_ps", 1), sig("c_kv2", 3), sig("c_xT_ps", 1), sig("c_xT", 1)
    c_qkv_ps, c_qv, c_k = sig("c_qkv_ps", 3), sig("c_qv", 2), sig("c_k", 1)
    c_mx = sig("c_mx", 2 * NT)
    c_s_ps, c_nb, c_p, c_r, c_pn, c_pt_ps, c_pt = (sig(n, NT) for n in (
        "c_s_ps", "c_nb", "c_p", "c_r", "c_pn", "c_pt_ps", "c_pt"))
    c_att_ps, c_att, c_attT_ps, c_attT, c_q2_ps, c_q2 = (sig(n, k) for n, k in (
        ("c_att_ps", 1), ("c_att", 2), ("c_attT_ps", 1), ("c_attT", 1), ("c_q2_ps", 1), ("c_q2", 1)))
    c_s2_ps, c_nm2, c_p2, c_pn2 = sig("c_s2_ps", 2), sig("c_nm2", 3), sig("c_p2", NT), sig("c_pn2", 2)
    c_p2t_ps, c_p2t, c_p2tt, c_att2_ps = (sig(n, 1) for n in ("c_p2t_ps", "c_p2t", "c_p2tt", "c_att2_ps"))
    c_n1, c_a2, c_n2, c_n2b, c_n2T_ps, c_n2T, c_h_ps, c_h, c_ff_ps, c_a3, c_n3, c_x3 = (sig(n, k) for n, k in (
        ("c_n1", 2), ("c_a2", 1), ("c_n2", 2), ("c_n2b", 1), ("c_n2T_ps", 1), ("c_n2T", 1), ("c_h_ps", 1),
        ("c_h", 2), ("c_ff_ps", 1), ("c_a3", 1), ("c_n3", 2), ("c_x3", 1)))
    ND = NP1 + 1
    d_xT_ps, d_xT, d_xs, d_lg_ps, d_sig = (sig(n, k) for n, k in (
        ("d_xT_ps", 1), ("d_xT", 1), ("d_xs", 2), ("d_lg_ps", 1), ("d_sig", 1)))
    d_r = sig("d_r", 12 + 4 * NT)
    d_ct_ps, d_ct = sig("d_ct_ps", 1), sig("d_ct", 1)
    d_g_ps, d_u_ps, d_silu, d_t, d_hi, d_lo, d_dn = (sig(n, ND) for n in (
        "d_g_ps", "d_u_ps", "d_silu", "d_t", "d_hi", "d_lo", "d_dn"))
    d_cb_ps, d_h = sig("d_cb_ps", NP1), sig("d_h", NP1)
    d_oT, d_o_ps, d_x4, d_out = sig("d_oT", 1), sig("d_o_ps", 1), sig("d_x4", 1), sig("d_out", 16)

    x_dram = a["x"].rearrange("b (i p) d -> b p i d", p=P)
    out_dram = a["out"].rearrange("b (i p) d -> b p i d", p=P)

    def four(bk):
        return bk.rearrange("p (i d) -> p i d", i=NT)

    def over_tiles(row, n=NT):
        return row.unsqueeze(1).to_broadcast([row.shape[0], n, row.shape[1]])

    def pieces(dram, split):
        w = dram.shape[1]
        return [(dram[:, c:c + min(1024, w - c)], min(1024, w - c), split, c) for c in range(0, w, 1024)]

    def alternate(p, q):
        return [piece for pair in zip(p, q) for piece in pair]

    pieces0 = alternate(pieces(a["w1"], w1s), pieces(a["w2"], w2s))
    gu_pieces, dn_pieces = pieces(a["gu"], gus), pieces(a["dn"], dns)
    pieces1 = pieces(a["sh"], shs) + [gu_pieces[0], dn_pieces[0], gu_pieces[1], gu_pieces[2], dn_pieces[1], gu_pieces[3]]
    NP0, NPC = len(pieces0), len(pieces0) + len(pieces1)
    piece_times = (-3, -2, -1, 3, 11, 12, 19)

    stage0 = [h32[:, 0:2, :].rearrange("p a b -> p (a b)"), ty[:].rearrange("p a b -> p (a b)")]

    def staged(n):
        return stage0[n % 2] if n < NP0 else raw1[:, (n - NP0) % NRAW1, :]

    def piece_loaded(eng, n):
        if n < NP0:
            eng.wait_ge(raw_loaded[n % 2].sem, 16 * (n // 2 + 1))
        else:
            slot, turn = (n - NP0) % NRAW1, (n - NP0) // NRAW1
            eng.wait_ge(raw_loaded[slot].sem, 16 * ((NP0 // 2 if slot < 2 else 0) + turn + 1))

    all_pieces = pieces0 + pieces1
    NCONST = 6
    NCONST_V = 2 + 2 * (1 + HG) + 1

    def b_time(c):
        return 0.8 + 1.25 * c

    def d_time(n):
        return 1 + 2 * n

    def c_time(pair):
        return 6 + 3 * pair

    def s_time(g, u):
        return b_time(5 + 7 * g) + 0.66 + (0, 0, 0.9, 0.95, 1)[u]

    def m_time(b, g, m):
        step = 0.45 if isinstance(b, int) and b == 0 else 0.9
        return s_time(g - 1, 0) + 0.3 + step * m if g else 4.4 + 0.3 * m

    def low_time(g, u):
        return s_time(g, 0) + 0.3 + 0.4 * u

    def pv_time(g, u):
        return s_time(g, 0) + 1.2 + 0.5 * u

    piece0_times = [3, 4.2] + [s_time(g, 0) + 2.3 + 2.5 * k for g in range(NG - 1) for k in range(2)]
    assert len(piece0_times) == NP0

    def norm_time(g):
        return pv_time(g, NU) + 0.4

    def m_bank(g, m):
        return ACC if g == 0 and m % 2 else MISC

    X1_TIME = norm_time(NG - 1) + 2

    def prob_low(eng, b, n):
        if n < 0:
            eng.wait_ge(a_plo_v.sem, a_plo_v.at(b, 0))
            eng.wait_ge(a_plo_g.sem, a_plo_g.at(b, 0))
        elif n % NU in PLO_G:
            eng.wait_ge(a_plo_g.sem, a_plo_g.at(b, n // NU * len(PLO_G) + PLO_G.index(n % NU) + 1))
        else:
            rest = [u for u in range(NU) if u not in PLO_G]
            eng.wait_ge(a_plo_v.sem, a_plo_v.at(b, n // NU * len(rest) + rest.index(n % NU) + 1))

    block = ctx.enter_context(nc.Block())

    def hidden_high(eng, b, c):
        done = b_hhi_v if c % 2 else b_hhi_s
        eng.wait_ge(done.sem, done.at(b, c // 2 + 1))

    def hidden_low(eng, b, c):
        done = b_hlo_g if c % 2 else b_hlo_v
        eng.wait_ge(done.sem, done.at(b, c // 2 + 1 if c >= 0 else 0))

    @block.sync
    def _(sp):
        def load_context(b):
            sp.wait_ge(a_kv_ps.sem, a_kv_ps.at(b, 0))
            apart(sp, b)
            sp.wait_ge(a_mk.sem, a_mk.at(b, 0))
            apart(sp, b)
            sp.dma_start(ctxA[:], a["ctxT"][b]).then_inc(a_ctx_in.sem, 16)
            sp.dma_start(mask8[:], a["mask"][b]).then_inc(a_ctx_in.sem, 16)

        def load_x(b):
            sp.wait_ge(a_xb.sem, a_xb.at(b, 0))
            apart(sp, b)
            sp.wait_ge(ln_a.out.sem, ln_a.out.at(b, 0))
            apart(sp, b)
            sp.dma_start(x_in[:], x_dram[b]).then_inc(a_x_in.sem, 16)

        load_context(0)
        load_x(0)
        sp.dma_start(early[:], a["early"]).then_inc(early_loaded.sem, 16)
        sp.dma_start(early_rows[:], a["early_rows"].partition_broadcast(P)).then_inc(early_loaded.sem, 16)
        for n in range(NP0):
            src, w, _, _ = all_pieces[n]
            if n >= 2:
                sp.wait_ge(raw_lo.sem, n - 1)
            sp.dma_start(staged(n)[:, 0:w], src).then_inc(raw_loaded[n % 2].sem, 16)
        sp.dma_start(late[:], a["late"]).then_inc(late_loaded.sem, 16)
        sp.dma_start(late_rows[:], a["late_rows"].partition_broadcast(P)).then_inc(late_loaded.sem, 16)
        with sp.Fori(1, NB) as b:
            load_x(b)
            load_context(b)

        def load_context1(b):
            sp.wait_ge(c_kv2_ps.sem, c_kv2_ps.at(b, 0))
            apart(sp, b)
            sp.dma_start(ctxC[:], a["ctxT"][b]).then_inc(c_ctx_in.sem, 16)

        def store(b):
            sp.wait_ge(d_x4.sem, d_x4.at(b, 1))
            apart(sp, b)
            sp.dma_start(out_dram[b], xo).then_inc(d_out.sem, 16)

        sp.wait_ge(layer0_done.sem, 4)
        load_context1(0)
        for n in range(NP0, NPC):
            src, w, _, _ = all_pieces[n]
            if n == NP0 + NRAW1:
                load_context1(1)
            if n >= NP0 + NRAW1:
                sp.wait_ge(raw_lo.sem, n - NRAW1 + 1)
            sp.dma_start(staged(n)[:, 0:w], src).then_inc(raw_loaded[(n - NP0) % NRAW1].sem, 16)
        with sp.Fori(2, NB) as b:
            load_context1(b)
            store(b - 2)
        store(NB - 2)
        store(NB - 1)
        sp.wait_ge(d_out.sem, d_out.at(NB - 1, 16))

    @block.gpsimd
    def _(pool):
        def split(first, times):
            for n, time in enumerate(times, first):
                yield time
                _, w, dst, c = all_pieces[n]
                piece_loaded(pool, n)
                pool.wait_ge(raw_hi.sem, n + 1)
                nc.gpsimd.tensor_tensor(dst[:, 1, c:c + w], staged(n)[:, 0:w], dst[:, 0, c:c + w].bitcast(F32),
                                        ALU.subtract).then_inc(raw_lo.sem, 1)

        def stage_a(b):
            yield 0.2
            pool.wait_ge(a_x_in.sem, a_x_in.at(b, 16))
            nc.gpsimd.tensor_tensor(X2[:, b, :, :], x_in[:], over_tiles(rows["bo"]), ALU.add).then_inc(a_xb.sem, 1)
            yield 0.5
            ln_a.gpsimd(pool, b)
            yield 2.6
            pool.wait_ge(a_pv.sem, a_pv.at(b, 0))
            apart(pool, b)
            pool.wait_ge(a_km.sem, a_km.at(b, 2))
            apart(pool, b)
            vm = VM[:].rearrange("p g (j s) -> p g j s", s=VST)
            vh = v32[:, 0, :].rearrange("p (g j d) -> p g j d", j=HG, d=HD)
            nc.gpsimd.tensor_copy(vm[:, :, :, 0:HD], vh).then_inc(a_vmain.sem, 1)
            pool.wait_ge(a_vmain.sem, a_vmain.at(b, 1))
            nc.gpsimd.tensor_tensor(vm[:, :, :, 32:32 + HD], vh, vm[:, :, :, 0:HD].bitcast(F32), ALU.subtract).then_inc(a_vmain.sem, 1)
            yield 4.4
            pool.wait_ge(a_ks.sem, a_ks.at(b, 2 * HG))
            pool.wait_ge(a_s_ps.sem, a_s_ps.at(b, 0))
            apart(pool, b)
            nc.gpsimd.tensor_copy(KST[:].rearrange("p g (j k) -> p g j k", j=HG), KS[:, :, :, P:KW].bitcast(F32)).then_inc(a_kst.sem, 1)
            for g in range(NG):
                for u in PLO_G:
                    n = g * NU + u
                    yield low_time(g, u)
                    pool.wait_ge(a_phi.sem, a_phi.at(b, n + 1))
                    pool.wait_ge(a_pv.sem, a_pv.at(b, max(0, n - PR + 1)))
                    nc.gpsimd.tensor_tensor(Plo[:, n % PR, :], P32[:, n % PR, :], Phi[:, n % PR, :].bitcast(F32),
                                            ALU.subtract).then_inc(a_plo_g.sem, 1)
            yield X1_TIME + 0.8
            ln_b.gpsimd(pool, b)

        def stage_b(b):
            for c in range(1, NC0 + 3):
                if c % 2 and c < NC0:
                    yield b_time(c) + 1.9
                    hidden_high(pool, b, c)
                    pool.wait_ge(b_y.sem, b_y.at(b, max(0, c - HR + 1)))
                    nc.gpsimd.tensor_tensor(hlo[:, c % HR, :], h32[:, c % HR, :], hhi[:, c % HR, :].bitcast(F32),
                                            ALU.subtract).then_inc(b_hlo_g.sem, 1)
                if c % 4 == 2 and c > 4:
                    e = c // 4 - 1
                    yield b_time(c) + 2
                    pool.wait_ge(b_ty.sem, b_ty.at(b, e + 1))
                    pool.wait_ge(b_base.sem, b_base.at(b, 1))
                    if e:
                        pool.wait_ge(b_acc.sem, b_acc.at(b, e))
                    nc.gpsimd.tensor_tensor(acc_o[:], acc_o[:], ty[:, e % 2, :], ALU.add).then_inc(b_acc.sem, 1)

        def stage_c(b):
            yield 0.2
            ln_c.gpsimd(pool, b)
            yield 15.7
            ln_n1.gpsimd(pool, b)
            yield 25.7
            ln_n2.gpsimd(pool, b)
            yield 28.4
            pool.wait_ge(c_n2.sem, c_n2.at(b, 2))
            pool.wait_ge(c_a3.sem, c_a3.at(b, 0))
            nc.gpsimd.tensor_tensor(norm2b[:], norm2[:], over_tiles(rows["b2f"]), ALU.add).then_inc(c_n2b.sem, 1)
            yield 33.4
            ln_n3.gpsimd(pool, b)
            yield 36.5
            ln_d.gpsimd(pool, b)

        def stage_d(b):
            for n in range(ND):
                yield d_time(n) + 2.8
                pool.wait_ge(d_hi.sem, d_hi.at(b, n + 1))
                pool.wait_ge(d_dn.sem, d_dn.at(b, max(0, n - HR + 1)))
                nc.gpsimd.tensor_tensor(hlo[:, n % HR, :], (t32[:, n % 2, :] if n == 0 else h32[:, n % HR, :]),
                                        hhi[:, n % HR, :].bitcast(F32), ALU.subtract).then_inc(d_lo.sem, 1)

        nc.gpsimd.memset(mhalf[:], -0.5).then_inc(const_set.sem, 1)
        nc.gpsimd.memset(KN[:].bitcast(F32), 0.0).then_inc(const_set.sem, 1)
        nc.gpsimd.memset(KS[:].bitcast(F32), 0.0).then_inc(const_set.sem, 1)
        nc.gpsimd.memset(VM[:].bitcast(F32), 0.0).then_inc(const_set.sem, 1)
        nc.gpsimd.memset(VT[:].bitcast(F32), 0.0).then_inc(const_set.sem, 1)
        nc.gpsimd.memset(QN[:].bitcast(F32), 0.0).then_inc(const_set.sem, 1)
        pool.wait_ge(const_set.sem, 1)
        pool.wait_ge(early_loaded.sem, 32)
        merged(stage_a(0), split(0, piece0_times))
        merged(stage_b(0), stage_a(1))
        with pool.Fori(2, NB) as b:
            merged(stage_b(b - 1), stage_a(b))
        pool.drain().then_inc(layer0_done.sem, 1)
        pool.wait_ge(layer0_done.sem, 4)
        pool.wait_ge(late_loaded.sem, 32)
        merged(stage_b(NB - 1), stage_c(0))
        pool.drain().then_inc(layer0_done.sem, 1)
        pool.wait_ge(layer0_done.sem, 8)
        merged(split(NP0, piece_times), stage_d(0), stage_c(1))
        with pool.Fori(2, NB) as b:
            merged(stage_d(b - 1), stage_c(b))
        merged(stage_d(NB - 1))

    @block.scalar
    def _(act):
        def copy(dst, src):
            return nc.scalar.activation(dst, src, ACT.Copy)

        def split(first, times):
            for n, time in enumerate(times, first):
                yield time
                _, w, dst, c = all_pieces[n]
                piece_loaded(act, n)
                copy(dst[:, 0, c:c + w], staged(n)[:, 0:w]).then_inc(raw_hi.sem, 1)

        def stage_a(b):
            yield 1.6
            act.wait_ge(a_xT_ps.sem, a_xT_ps.at(b, 1))
            copy(xT[:], MISC).then_inc(a_xT.sem, 1)
            for g in range(NG):
                yield 2.7 + 0.2 * g
                act.wait_ge(a_qt_ps.sem, a_qt_ps.at(b, g + 1))
                copy(QS[:, g, :], RING[g % 2]).then_inc(a_qs.sem, 1)
            yield 3.5
            for h in range(2):
                act.wait_ge(a_kt_ps.sem, a_kt_ps.at(b, h + 1))
                src = (RING[1] if h == 0 else ACC)[:, 0:2 * KW].rearrange("p (g k) -> p g k", g=2)
                act.wait_ge(a_s_ps.sem, a_s_ps.at(b, 0))
                for j in range(HG):
                    q = slice(TP * j, TP * j + TP)
                    copy(KS[q, 2 * h:2 * h + 2, j, :], src[q]).then_inc(a_ks.sem, 1)
            for g in range(NG):
                yield s_time(g, 0) - 1
                act.wait_ge(a_q2_ps.sem, a_q2_ps.at(b, g + 1))
                copy(QS[:, g, :], MISC).then_inc(a_q2s.sem, 1)
                for u in range(NU):
                    yield s_time(g, u)
                    n = g * NU + u
                    act.wait_ge(a_s_ps.sem, a_s_ps.at(b, n + 1))
                    prob_low(act, b, n - PR)
                    if n < 2:
                        act.wait_ge(a_y_ps.sem, a_y_ps.at(b, 0))
                    nc.scalar.activation(P32[:, n % PR, :], RING[n % 2], ACT.Exp,
                                         scale=float(1 / np.sqrt(HD))).then_inc(a_exp.sem, 1)
                yield pv_time(g, NU)
                act.wait_ge(a_pv.sem, a_pv.at(b, NU * (g + 1)))
                act.wait_ge(a_ozt_ps.sem, a_ozt_ps.at(b, g))
                copy(OZ[:], ACC).then_inc(a_oz.sem, 1)
            yield norm_time(NG - 1) + 1
            for h in range(2):
                act.wait_ge(a_ot_ps.sem, a_ot_ps.at(b, h + 1))
                act.wait_ge(a_y_ps.sem, a_y_ps.at(b, 0))
                copy(OT[:, h, :], RING[h]).then_inc(a_ot.sem, 1)

        def stage_b(b):
            yield 0.2
            act.wait_ge(b_xT_ps.sem, b_xT_ps.at(b, 1))
            copy(xT32[:], bank[3]).then_inc(b_xT.sem, 1)
            yield 1.3
            act.wait_ge(b_sd.sem, b_sd.at(b, 1))
            nc.scalar.activation(ex[:], dl[:], ACT.Exp).then_inc(b_ex.sem, 1)

            def spread(e):
                act.wait_ge(b_wb_ps.sem, b_wb_ps.at(b, e + 1))
                act.wait_ge(b_ty.sem, b_ty.at(b, max(0, e - 1)))
                copy(WB[:, e % 2, :], bank[3]).then_inc(b_wb.sem, 1)

            for c in range(NC0 + 1):
                if c < NC0:
                    yield b_time(c) + 0.6
                    act.wait_ge(b_h_ps.sem, b_h_ps.at(b, c + 1))
                    hidden_low(act, b, c - HR)
                    nc.scalar.activation(h32[:, c % HR, :], bank[c % 2], ACT.Gelu, bias=b1T[:, c:c + 1]).then_inc(b_gelu.sem, 1)
                if c % 2:
                    yield b_time(c) + 0.65
                    act.wait_ge(b_gelu.sem, b_gelu.at(b, c))
                    act.wait_ge(b_y.sem, b_y.at(b, max(0, c - HR)))
                    copy(hhi[:, (c - 1) % HR, :], h32[:, (c - 1) % HR, :]).then_inc(b_hhi_s.sem, 1)
                if c == 3:
                    yield b_time(c) + 0.7
                    act.wait_ge(b_wt_ps.sem, b_wt_ps.at(b, 1))
                    copy(WT[:], bank[3][0:2 * E0, :]).then_inc(b_wt.sem, 1)
                if c == 4:
                    yield b_time(c) + 0.61
                    act.wait_ge(b_base_ps.sem, b_base_ps.at(b, 1))
                    copy(acc_o[:], bank[3]).then_inc(b_base.sem, 1)
                if c == 4 or c % 4 == 3 and c > 4:
                    yield b_time(c) + 0.7
                    spread((c - 3) // 4)

        def stage_c(b):
            yield 0.6
            act.wait_ge(c_kv2_ps.sem, c_kv2_ps.at(b, 1))
            copy(K2T[:], RING[0][:, 0:LK]).then_inc(c_kv2.sem, 1)
            copy(V2m[:], RING[1][:, 0:P]).then_inc(c_kv2.sem, 1)
            copy(V2t[:], RING[1][0:TP, P:2 * P]).then_inc(c_kv2.sem, 1)
            yield 3.4
            act.wait_ge(c_xT_ps.sem, c_xT_ps.at(b, 1))
            copy(xiT[:], MISC).then_inc(c_xT.sem, 1)
            yield 5.05
            act.wait_ge(c_qkv_ps.sem, c_qkv_ps.at(b, 1))
            copy(QT1[:], RING[0]).then_inc(c_qv.sem, 1)
            yield 5.7
            act.wait_ge(c_qkv_ps.sem, c_qkv_ps.at(b, 3))
            copy(V1[:], four(ACC)).then_inc(c_qv.sem, 1)
            scale1 = float(1 / np.sqrt(np.float32(S)))
            scale2 = float(1 / np.sqrt(np.float32(LK)))

            def move_pt(i):
                act.wait_ge(c_pt_ps.sem, c_pt_ps.at(b, i + 1))
                copy(PT[:, 0:i + 1, i * P:(i + 1) * P], four(MISC)[:, 0:i + 1, :]).then_inc(c_pt.sem, 1)

            for pair in range(2):
                yield c_time(pair) + 1.8
                for i in (2 * pair, 2 * pair + 1):
                    w = (i + 1) * P
                    act.wait_ge(c_nb.sem, c_nb.at(b, i + 1))
                    act.wait_ge(c_pn.sem, c_pn.at(b, max(0, i - 1)))
                    nc.scalar.activation(P1[:, i % 2, 0:w], RING[i % 2][:, 0:w], ACT.Exp, bias=nb1[:, i:i + 1],
                                         scale=scale1, accum_out=z1[:, i:i + 1]).then_inc(c_p.sem, 1)
                yield c_time(pair) + 3.7
                move_pt(2 * pair)
                yield c_time(pair) + 4.6
                move_pt(2 * pair + 1)
            yield 16.2
            act.wait_ge(c_attT_ps.sem, c_attT_ps.at(b, 1))
            copy(attT[:], MISC).then_inc(c_attT.sem, 1)
            yield 18
            act.wait_ge(c_q2_ps.sem, c_q2_ps.at(b, 1))
            copy(Q2T[:], RING[0]).then_inc(c_q2.sem, 1)
            yield 21.2
            act.wait_ge(c_nm2.sem, c_nm2.at(b, 3))
            for i in range(NT):
                src = (RING[1] if i < 2 else ACC)[:, 0:2 * KW].rearrange("p (i k) -> p i k", i=2)
                nc.scalar.activation(P2[:, i, :], src[:, i % 2, 0:LK], ACT.Exp, bias=nb2[:, i:i + 1],
                                     scale=scale2, accum_out=z2[:, i:i + 1]).then_inc(c_p2.sem, 1)
            yield 22.6
            act.wait_ge(c_p2t_ps.sem, c_p2t_ps.at(b, 1))
            copy(P2T[:], RING[0]).then_inc(c_p2t.sem, 1)
            yield 29
            act.wait_ge(c_n2T_ps.sem, c_n2T_ps.at(b, 1))
            copy(n2T[:], MISC).then_inc(c_n2T.sem, 1)

        def stage_d(b):
            yield 0.3
            act.wait_ge(d_xT_ps.sem, d_xT_ps.at(b, 1))
            copy(xT32[:], bank[3]).then_inc(d_xT.sem, 1)
            yield 1
            act.wait_ge(d_lg_ps.sem, d_lg_ps.at(b, 1))
            nc.scalar.activation(sc1[:], bank[3][:, 0:NT * E1].rearrange("p (i e) -> p i e", i=NT),
                                 ACT.Sigmoid).then_inc(d_sig.sem, 1)

            def high(n):
                if n == 0:
                    act.wait_ge(d_t.sem, d_t.at(b, 1))
                else:
                    act.wait_ge(d_h.sem, d_h.at(b, n))
                act.wait_ge(d_dn.sem, d_dn.at(b, max(0, n - HR + 1)))
                copy(hhi[:, n % HR, :], (t32[:, n % 2, :] if n == 0 else h32[:, n % HR, :])).then_inc(d_hi.sem, 1)

            for n in range(ND):
                yield d_time(n) + 0.3
                act.wait_ge(d_g_ps.sem, d_g_ps.at(b, n + 1))
                act.wait_ge(d_t.sem, d_t.at(b, max(0, n - 1)))
                nc.scalar.activation(s32[:, n % 2, :], bank[0], ACT.Silu).then_inc(d_silu.sem, 1)
                if n:
                    yield d_time(n) + 0.4
                    high(n - 1)
                if n == 1:
                    yield d_time(n) + 0.95
                    act.wait_ge(d_ct_ps.sem, d_ct_ps.at(b, 1))
                    copy(CT[:], bank[3][0:2 * E1, :]).then_inc(d_ct.sem, 1)
            yield d_time(ND) + 0.4
            high(ND - 1)
            yield d_time(ND) + 3.6
            act.wait_ge(d_dn.sem, d_dn.at(b, ND))
            copy(oT[:], bank[2]).then_inc(d_oT.sem, 1)

        merged(stage_a(0), split(0, piece0_times))
        merged(stage_b(0), stage_a(1))
        with act.Fori(2, NB) as b:
            merged(stage_b(b - 1), stage_a(b))
        act.drain().then_inc(layer0_done.sem, 1)
        act.wait_ge(layer0_done.sem, 4)
        merged(stage_b(NB - 1), stage_c(0))
        act.drain().then_inc(layer0_done.sem, 1)
        act.wait_ge(layer0_done.sem, 8)
        merged(split(NP0, piece_times), stage_d(0), stage_c(1))
        with act.Fori(2, NB) as b:
            merged(stage_d(b - 1), stage_c(b))
        merged(stage_d(NB - 1))

    @block.vector
    def _(dve):
        V = nc.vector
        c_hi, c_lo = f32r_parts(-MASK_FILL * np.sqrt(HD))

        def stage_a(b):
            yield 0
            dve.wait_ge(a_ctx_in.sem, a_ctx_in.at(b, 32))
            V.tensor_copy(mk[:], mask8[:]).then_inc(a_mk.sem, 1)
            dve.wait_ge(a_mk.sem, a_mk.at(b, 1))
            V.tensor_tensor(mkd[:], mk[:], valid, ALU.subtract).then_inc(a_mk.sem, 1)
            dve.wait_ge(a_x_in.sem, a_x_in.at(b, 16))
            dve.wait_ge(a_xT_ps.sem, a_xT_ps.at(b, 0))
            yield from ln_a.vector(dve, b, x_in, xn, 0)
            yield 1.2
            dve.wait_ge(a_kv_ps.sem, a_kv_ps.at(b, 1))
            kps = RING[0][:, 0:2 * P].rearrange("p (t d) -> p t d", t=2)
            vps = RING[0][:, 2 * P:4 * P].rearrange("p (t d) -> p t d", t=2)
            V.tensor_tensor(k32[:], kps, over_tiles(rows["bk"], 2), ALU.add).then_inc(a_kv.sem, 1)
            V.tensor_tensor(v32[:], vps, over_tiles(rows["bv"], 2), ALU.add).then_inc(a_kv.sem, 1)
            yield 2.2
            dve.wait_ge(a_q_ps.sem, a_q_ps.at(b, 1))
            V.tensor_tensor(q32[:], four(MISC), over_tiles(rows["bq"]), ALU.add).then_inc(a_q32.sem, 1)
            dve.wait_ge(a_q2_ps.sem, a_q2_ps.at(b, 0))
            dve.wait_ge(a_q32.sem, a_q32.at(b, 1))
            qh = q32[:].rearrange("p i (h d) -> p i h d", d=HD)
            V.tensor_copy(QN[:, :, :, 0:HD], qh).then_inc(a_qn.sem, 1)
            V.tensor_copy(QN[:, :, :, 2 * HD:3 * HD], qh).then_inc(a_qn.sem, 1)
            V.memset(QN[:, :, :, 24:26].bitcast(F32), 0.0).then_inc(a_qn.sem, 1)
            dve.wait_ge(a_qn.sem, a_qn.at(b, 1))
            V.tensor_tensor(QN[:, :, :, HD:2 * HD], qh, QN[:, :, :, 0:HD].bitcast(F32), ALU.subtract).then_inc(a_qn.sem, 1)
            yield 2.25
            dve.wait_ge(a_kv.sem, a_kv.at(b, 1))
            V.tensor_tensor(km[:], k32[:], mk[:].unsqueeze(2).to_broadcast([P, 2, P]), ALU.mult).then_inc(a_km.sem, 1)
            dve.wait_ge(a_kv.sem, a_kv.at(b, 2))
            V.tensor_scalar(vtm[:], v32[:, 1, :], valid[:, 1:2], None, ALU.mult).then_inc(a_km.sem, 1)
            dve.wait_ge(a_kt_ps.sem, a_kt_ps.at(b, 0))
            kh = km[:].rearrange("p t (h d) -> p t h d", d=HD)
            dve.wait_ge(a_km.sem, a_km.at(b, 1))
            V.tensor_copy(KN[:, :, :, 0:HD], kh).then_inc(a_kn.sem, 1)
            V.tensor_copy(KN[:, :, :, HD:2 * HD], kh).then_inc(a_kn.sem, 1)
            dve.wait_ge(a_mk.sem, a_mk.at(b, 2))
            pen = mkd[:].unsqueeze(2).unsqueeze(3).to_broadcast([P, 2, NH, 1])
            V.tensor_scalar(KN[:, :, :, 26:27], pen, c_hi, None, ALU.mult).then_inc(a_kn.sem, 1)
            V.tensor_scalar(KN[:, :, :, 27:28], pen, c_lo, None, ALU.mult).then_inc(a_kn.sem, 1)
            dve.wait_ge(a_kn.sem, a_kn.at(b, 1))
            V.tensor_tensor(KN[:, :, :, 2 * HD:3 * HD], kh, KN[:, :, :, 0:HD].bitcast(F32), ALU.subtract).then_inc(a_kn.sem, 1)
            yield 4
            dve.wait_ge(a_pv.sem, a_pv.at(b, 0))
            dve.wait_ge(a_km.sem, a_km.at(b, 2))
            vt = vtm[:].rearrange("p (g j d) -> p g j d", j=HG, d=HD)
            for j in range(HG):
                q, o = slice(TP * j, TP * j + TP), HD * j
                V.tensor_copy(VT[q, :, o:o + HD], vt[q, :, j, :]).then_inc(a_vtail.sem, 1)
            dve.wait_ge(a_vtail.sem, a_vtail.at(b, HG))
            for j in range(HG):
                q, o = slice(TP * j, TP * j + TP), HD * j
                V.tensor_tensor(VT[q, :, 32 + o:32 + o + HD], vt[q, :, j, :], VT[q, :, o:o + HD].bitcast(F32),
                                ALU.subtract).then_inc(a_vtail.sem, 1)

            def normalise(g):
                yield norm_time(g) + 0.3
                src = four(ACC)
                dve.wait_ge(a_ozt_ps.sem, a_ozt_ps.at(b, g + 1))
                dve.wait_ge(a_on.sem, a_on.at(b, 2 * g))
                V.reciprocal(rz[:], src[:, :, 64::HD]).then_inc(a_on.sem, 1)
                dve.wait_ge(a_on.sem, a_on.at(b, 2 * g + 1))
                dve.wait_ge(a_ot_ps.sem, a_ot_ps.at(b, 0))
                V.tensor_tensor(ON[:, :, g, :].rearrange("p i (h d) -> p i h d", d=HD),
                                src[:, :, 0:64].rearrange("p i (h d) -> p i h d", d=HD),
                                rz[:].unsqueeze(3).to_broadcast([P, NT, 2 * HG, HD]), ALU.mult).then_inc(a_on.sem, 1)

            def maxima(g):
                for u in range(2 * NT):
                    yield m_time(b, g, u) + 0.2
                    n = g * 2 * NT + u
                    i, half = divmod(u, 2)
                    dve.wait_ge(a_m_ps.sem, a_m_ps.at(b, n + 1))
                    src = m_bank(g, u)[:, 0:2 * KW].rearrange("p (h k) -> p h k", h=2)[:, :, 0:LK]
                    h = HG * g + 2 * half
                    V.tensor_reduce(NM[:, i, h:h + 2], src, AX.X, ALU.max, negate=True).then_inc(a_nm.sem, 1)
                dve.wait_ge(a_nm.sem, a_nm.at(b, (g + 1) * 2 * NT))
                nm = NM[:, :, HG * g:HG * g + HG].unsqueeze(3)
                V.tensor_copy(QN[:, :, HG * g:HG * g + HG, 24:25], nm).then_inc(a_nmq.sem, 1)
                dve.wait_ge(a_nmq.sem, a_nmq.at(b, 2 * g + 1))
                V.tensor_tensor(QN[:, :, HG * g:HG * g + HG, 25:26], nm,
                                QN[:, :, HG * g:HG * g + HG, 24:25].bitcast(F32), ALU.subtract).then_inc(a_nmq.sem, 1)

            def low_parts(g):
                for u in range(NU):
                    yield low_time(g, u)
                    n = g * NU + u
                    dve.wait_ge(a_exp.sem, a_exp.at(b, n + 1))
                    dve.wait_ge(a_pv.sem, a_pv.at(b, max(0, n - PR + 1)))
                    V.tensor_copy(Phi[:, n % PR, :], P32[:, n % PR, :]).then_inc(a_phi.sem, 1)
                    if u not in PLO_G:
                        dve.wait_ge(a_phi.sem, a_phi.at(b, n + 1))
                        V.tensor_tensor(Plo[:, n % PR, :], P32[:, n % PR, :], Phi[:, n % PR, :].bitcast(F32),
                                        ALU.subtract).then_inc(a_plo_v.sem, 1)

            parts = [maxima(g) for g in range(NG)] + [low_parts(g) for g in range(NG)] + [normalise(g) for g in range(NG)]
            yield from by_time(*parts)
            yield X1_TIME
            dve.wait_ge(a_xb.sem, a_xb.at(b, 1))
            dve.wait_ge(a_y_ps.sem, a_y_ps.at(b, 1))
            V.tensor_tensor(X2[:, b, :, :], four(MISC), X2[:, b, :, :], ALU.add).then_inc(a_x1.sem, 1)
            dve.wait_ge(b_xT_ps.sem, b_xT_ps.at(b, 0))
            dve.wait_ge(a_x1.sem, a_x1.at(b, 1))
            apart(dve, b)
            yield from ln_b.vector(dve, b, X2[:, b, :, :], xn2, X1_TIME + 0.3)

        def split_xT(b, ready, done):
            dve.wait_ge(ready.sem, ready.at(b, 1))
            V.tensor_copy(xThi[:], xT32[:]).then_inc(done.sem, 1)
            dve.wait_ge(done.sem, done.at(b, 1))
            V.tensor_tensor(xTlo[:], xT32[:], xThi[:].bitcast(F32), ALU.subtract).then_inc(done.sem, 1)

        def stage_b(b):
            x1 = X2[:, b, :, :]
            yield 0.4
            split_xT(b, b_xT, b_xs)
            yield 0.7
            dve.wait_ge(b_lg_ps.sem, b_lg_ps.at(b, 1))
            V.tensor_tensor(lg[:], bank[3][:, 0:NT * E0].rearrange("p (i e) -> p i e", i=NT),
                            over_tiles(row_br), ALU.add).then_inc(b_lg.sem, 1)
            dve.wait_ge(b_lg.sem, b_lg.at(b, 1))
            apart(dve, b)
            for i in range(NT):
                V.max(m8[:, i, :], lg[:, i, :]).then_inc(b_lg.sem, 1)
            dve.wait_ge(b_lg.sem, b_lg.at(b, 1 + NT))
            V.tensor_tensor(dl[:], lg[:], m8[:, :, 0:1].to_broadcast([P, NT, E0]), ALU.subtract).then_inc(b_sd.sem, 1)
            V.tensor_tensor(sel[:], lg[:], m8[:, :, 1:2].to_broadcast([P, NT, E0]), ALU.is_ge).then_inc(b_sd.sem, 1)
            yield 1.35
            dve.wait_ge(b_sd.sem, b_sd.at(b, 2))
            dve.wait_ge(b_ex.sem, b_ex.at(b, 1))
            V.tensor_tensor(wu[:], ex[:], sel[:], ALU.mult).then_inc(b_w.sem, 1)
            dve.wait_ge(b_w.sem, b_w.at(b, 1))
            V.reduce_sum(zr[:], wu[:], AX.X).then_inc(b_w.sem, 1)
            dve.wait_ge(b_w.sem, b_w.at(b, 2))
            V.reciprocal(rr[:], zr[:]).then_inc(b_w.sem, 1)
            dve.wait_ge(b_w.sem, b_w.at(b, 3))
            V.tensor_tensor(wn[:], wu[:], rr[:].unsqueeze(2).to_broadcast([P, NT, E0]), ALU.mult).then_inc(b_w.sem, 1)
            dve.wait_ge(b_w.sem, b_w.at(b, 4))
            V.tensor_copy(WN[:, :, 0:E0], wn[:]).then_inc(b_w.sem, 1)
            dve.wait_ge(b_w.sem, b_w.at(b, 5))
            V.tensor_tensor(WN[:, :, E0:2 * E0], wn[:], WN[:, :, 0:E0].bitcast(F32), ALU.subtract).then_inc(b_w.sem, 1)

            def weigh(e):
                dve.wait_ge(b_y.sem, b_y.at(b, 4 * e + 4))
                dve.wait_ge(b_wb.sem, b_wb.at(b, e + 1))
                dve.wait_ge(b_acc.sem, b_acc.at(b, max(0, e - 1)))
                V.tensor_tensor(ty[:, e % 2, :], bank[2], WB[:, e % 2, :], ALU.mult).then_inc(b_ty.sem, 1)

            for c in range(NC0 + 3):
                if c % 2 and c < NC0:
                    yield b_time(c) + 0.85
                    dve.wait_ge(b_gelu.sem, b_gelu.at(b, c + 1))
                    dve.wait_ge(b_y.sem, b_y.at(b, max(0, c - HR + 1)))
                    V.tensor_copy(hhi[:, c % HR, :], h32[:, c % HR, :]).then_inc(b_hhi_v.sem, 1)
                if c % 2 and c <= NC0:
                    yield b_time(c) + 1.6
                    hidden_high(dve, b, c - 1)
                    dve.wait_ge(b_y.sem, b_y.at(b, max(0, c - HR)))
                    V.tensor_tensor(hlo[:, (c - 1) % HR, :], h32[:, (c - 1) % HR, :], hhi[:, (c - 1) % HR, :].bitcast(F32),
                                    ALU.subtract).then_inc(b_hlo_v.sem, 1)
                if c % 4 == 2 and c > 4:
                    yield b_time(c) + 1
                    weigh(c // 4 - 1)
            yield b_time(NC0) + 5
            dve.wait_ge(b_o_ps.sem, b_o_ps.at(b, 1))
            V.tensor_tensor(x1, four(bank[3]), x1, ALU.add).then_inc(b_x2.sem, 1)

        def affine(src, dst, b, done):
            V.tensor_tensor(gn[:], src, over_tiles(rows["gamma"]), ALU.mult).then_inc(done.sem, 1)
            dve.wait_ge(done.sem, done.at(b, 1))
            V.tensor_tensor(dst[:], gn[:], over_tiles(rows["beta"]), ALU.add).then_inc(done.sem, 1)

        def stage_c(b):
            yield 0
            dve.wait_ge(b_x2.sem, b_x2.at(b, 1))
            yield from ln_c.vector(dve, b, X2[:, b, :, :], xi, 0)
            yield 4.6
            dve.wait_ge(c_qkv_ps.sem, c_qkv_ps.at(b, 2))
            V.tensor_copy(KT1[:], RING[1]).then_inc(c_k.sem, 1)
            scale1 = float(1 / np.sqrt(np.float32(S)))
            scale2 = float(1 / np.sqrt(np.float32(LK)))

            def scale_rows(i):
                w = (i + 1) * P
                dve.wait_ge(c_p.sem, c_p.at(b, i + 1))
                V.reciprocal(r1[:, i:i + 1], z1[:, i:i + 1]).then_inc(c_r.sem, 1)
                dve.wait_ge(c_r.sem, c_r.at(b, i + 1))
                dve.wait_ge(c_pt_ps.sem, c_pt_ps.at(b, max(0, i - 1)))
                V.tensor_scalar(PN1[:, i % 2, 0:w], P1[:, i % 2, 0:w], r1[:, i:i + 1], None, ALU.mult).then_inc(c_pn.sem, 1)

            for pair in range(2):
                yield c_time(pair) + 0.8
                for i in (2 * pair, 2 * pair + 1):
                    w = (i + 1) * P
                    dve.wait_ge(c_s_ps.sem, c_s_ps.at(b, i + 1))
                    diag = RING[i % 2][:, i * P:w]
                    V.tensor_tensor(diag, diag, trimask, ALU.add).then_inc(c_mx.sem, 1)
                    dve.wait_ge(c_mx.sem, c_mx.at(b, 2 * i + 1))
                    V.tensor_reduce(nm1[:, i:i + 1], RING[i % 2][:, 0:w], AX.X, ALU.max, negate=True).then_inc(c_mx.sem, 1)
                    dve.wait_ge(c_mx.sem, c_mx.at(b, 2 * i + 2))
                    V.tensor_scalar(nb1[:, i:i + 1], nm1[:, i:i + 1], scale1, None, ALU.mult).then_inc(c_nb.sem, 1)
                yield c_time(pair) + 2.5
                scale_rows(2 * pair)
                scale_rows(2 * pair + 1)
            yield 15
            dve.wait_ge(c_att_ps.sem, c_att_ps.at(b, 1))
            V.tensor_copy(att[:], four(ACC)).then_inc(c_att.sem, 1)
            V.tensor_tensor(a1[:], four(ACC), xi[:], ALU.add).then_inc(c_att.sem, 1)
            dve.wait_ge(c_att.sem, c_att.at(b, 2))
            yield from ln_n1.vector(dve, b, a1, normed, 15.5)
            yield 19.8
            for h in range(2):
                src = (RING[1] if h == 0 else ACC)[:, 0:2 * KW].rearrange("p (i k) -> p i k", i=2)[:, :, 0:LK]
                dve.wait_ge(c_s2_ps.sem, c_s2_ps.at(b, h + 1))
                V.tensor_reduce(nm2[:, 2 * h:2 * h + 2], src, AX.X, ALU.max, negate=True).then_inc(c_nm2.sem, 1)
            dve.wait_ge(c_nm2.sem, c_nm2.at(b, 2))
            V.tensor_scalar(nb2[:], nm2[:], scale2, None, ALU.mult).then_inc(c_nm2.sem, 1)
            yield 20
            dve.wait_ge(ln_n1.out.sem, ln_n1.out.at(b, NT))
            affine(normed[:], norm1, b, c_n1)
            yield 21.6
            dve.wait_ge(c_p2.sem, c_p2.at(b, NT))
            V.reciprocal(r2[:], z2[:]).then_inc(c_pn2.sem, 1)
            dve.wait_ge(c_pn2.sem, c_pn2.at(b, 1))
            V.tensor_tensor(PN2[:], P2[:], r2[:].unsqueeze(2).to_broadcast([P, NT, LK]), ALU.mult).then_inc(c_pn2.sem, 1)
            yield 22.6
            dve.wait_ge(c_p2t_ps.sem, c_p2t_ps.at(b, 1))
            V.tensor_copy(P2Tt[0:LT, :], ACC[0:LT, :]).then_inc(c_p2tt.sem, 1)
            yield 25
            dve.wait_ge(c_att2_ps.sem, c_att2_ps.at(b, 1))
            dve.wait_ge(c_n1.sem, c_n1.at(b, 2))
            V.tensor_tensor(a1[:], four(RING[1]), norm1[:], ALU.add).then_inc(c_a2.sem, 1)
            dve.wait_ge(c_a2.sem, c_a2.at(b, 1))
            yield from ln_n2.vector(dve, b, a1, normed, 25.5)
            yield 27
            dve.wait_ge(ln_n2.out.sem, ln_n2.out.at(b, NT))
            affine(normed[:], norm2, b, c_n2)
            yield 31.2
            dve.wait_ge(c_h_ps.sem, c_h_ps.at(b, 1))
            V.tensor_scalar(hu[:], RING[0], b1f[:, 0:1], None, ALU.add).then_inc(c_h.sem, 1)
            dve.wait_ge(c_h.sem, c_h.at(b, 1))
            V.scalar_tensor_tensor(hT[:], hu[:], 0.2, hu[:], ALU.mult, ALU.max).then_inc(c_h.sem, 1)
            yield 33
            dve.wait_ge(c_ff_ps.sem, c_ff_ps.at(b, 1))
            dve.wait_ge(c_n2b.sem, c_n2b.at(b, 1))
            V.tensor_tensor(a1[:], four(RING[1]), norm2b[:], ALU.add).then_inc(c_a3.sem, 1)
            dve.wait_ge(c_a3.sem, c_a3.at(b, 1))
            yield from ln_n3.vector(dve, b, a1, normed, 33.2)
            yield 35.2
            dve.wait_ge(ln_n3.out.sem, ln_n3.out.at(b, NT))
            affine(normed[:], norm3, b, c_n3)
            dve.wait_ge(c_n3.sem, c_n3.at(b, 2))
            x2 = X2[:, b, :, :].rearrange("p i d -> p (i d)")
            V.scalar_tensor_tensor(x2, norm3[:].rearrange("p i d -> p (i d)"), 0.0, x2, ALU.max, ALU.add).then_inc(c_x3.sem, 1)
            dve.wait_ge(d_xT_ps.sem, d_xT_ps.at(b, 0))
            dve.wait_ge(c_x3.sem, c_x3.at(b, 1))
            apart(dve, b)
            yield from ln_d.vector(dve, b, X2[:, b, :, :], xn2, 36)

        def stage_d(b):
            x3 = X2[:, b, :, :]
            yield 0.6
            split_xT(b, d_xT, d_xs)
            def router():
                yield d_time(0) + 1.1
                k = 0

                def step(*writes):
                    nonlocal k
                    for ins in writes:
                        k += 1
                        ins.then_inc(d_r.sem, 1)
                    dve.wait_ge(d_r.sem, d_r.at(b, k))
                    apart(dve, b)

                dve.wait_ge(d_sig.sem, d_sig.at(b, 1))
                step(V.tensor_tensor(sfc[:], sc1[:], over_tiles(row_gb), ALU.add))
                step(V.tensor_reduce(gsc[:, :, 0:GRP], sfc[:].rearrange("p i (g s) -> p i g s", s=GS), AX.X, ALU.max))
                step(*[V.max(gm8[:, i, :], gsc[:, i, :]) for i in range(NT)])
                step(*[V.match_replace(grp[:, i, :], gm8[:, i, :], gsc[:, i, :], -BIG) for i in range(NT)])
                step(V.tensor_scalar(gmk[:], grp[:, :, 0:GRP], -BIG, None, ALU.is_equal))
                step(V.tensor_tensor(mks[:, :, 0:E1].rearrange("p i (g s) -> p i g s", s=GS),
                                     sfc[:].rearrange("p i (g s) -> p i g s", s=GS),
                                     gmk[:].unsqueeze(3).to_broadcast([P, NT, GRP, GS]), ALU.mult))
                step(*[V.max(em8[:, i, :], mks[:, i, :]) for i in range(NT)])
                step(*[V.match_replace(erp[:, i, :], em8[:, i, :], mks[:, i, :], -BIG) for i in range(NT)])
                step(V.tensor_scalar(esl[:], erp[:, :, 0:E1], -BIG, None, ALU.is_equal))
                step(V.tensor_tensor(tw[:], sc1[:], esl[:], ALU.mult))
                step(V.reduce_sum(tz[:], tw[:], AX.X))
                step(V.tensor_scalar(tz[:], tz[:], 1e-20, None, ALU.add))
                step(V.reciprocal(tr[:], tz[:]))
                step(V.scalar_tensor_tensor(cw[:], tw[:], 2.5, tr[:].unsqueeze(2).to_broadcast([P, NT, E1]), ALU.mult, ALU.mult))
                step(V.tensor_copy(CN[:, :, 0:E1], cw[:]))
                V.tensor_tensor(CN[:, :, E1:2 * E1], cw[:], CN[:, :, 0:E1].bitcast(F32), ALU.subtract).then_inc(d_r.sem, 1)

            def units():
                for n in range(ND):
                    yield d_time(n) + 1
                    dve.wait_ge(d_silu.sem, d_silu.at(b, n + 1))
                    dve.wait_ge(d_u_ps.sem, d_u_ps.at(b, n + 1))
                    if n == 2:
                        dve.wait_ge(d_lo.sem, d_lo.at(b, 1))
                    elif n > 2:
                        dve.wait_ge(d_h.sem, d_h.at(b, n - 2))
                    V.tensor_tensor(t32[:, n % 2, :], s32[:, n % 2, :], bank[1], ALU.mult).then_inc(d_t.sem, 1)
                    if n:
                        yield d_time(n) + 1.4
                        dve.wait_ge(d_t.sem, d_t.at(b, n + 1))
                        dve.wait_ge(d_cb_ps.sem, d_cb_ps.at(b, n))
                        dve.wait_ge(d_lo.sem, d_lo.at(b, max(0, n - HR + 1)))
                        V.tensor_tensor(h32[:, n % HR, :], t32[:, n % 2, :], bank[3], ALU.mult).then_inc(d_h.sem, 1)

            yield from by_time(units(), router())
            yield d_time(ND) + 5
            dve.wait_ge(d_o_ps.sem, d_o_ps.at(b, 1))
            dve.wait_ge(d_out.sem, d_out.at(b, 0))
            V.tensor_tensor(xo, four(bank[3]), x3, ALU.add).then_inc(d_x4.sem, 1)

        dve.wait_ge(early_loaded.sem, 32)
        dve.wait_ge(const_set.sem, NCONST)
        V.tensor_copy(KN[:, :, :, 24:26], valid.unsqueeze(2).unsqueeze(3).to_broadcast([P, 2, NH, 2])).then_inc(const_set.sem, 1)
        V.memset(QN[:, :, :, 26:28].bitcast(F32), 1.0).then_inc(const_set.sem, 1)
        vm = VM[:].rearrange("p g (j s) -> p g j s", s=VST)
        for o in (64, 96):
            V.memset(vm[:, :, :, o:o + HD].bitcast(F32), 1.0).then_inc(const_set.sem, 1)
            for j in range(HG):
                q, c = slice(TP * j, TP * j + TP), o + HD * j
                V.tensor_copy(VT[q, :, c:c + HD], valid[q, 1:2].unsqueeze(2).to_broadcast([TP, NG, HD])).then_inc(const_set.sem, 1)
        V.tensor_copy(pick0r[:], pick0).then_inc(const_set.sem, 1)
        dve.wait_ge(const_set.sem, NCONST + NCONST_V)
        merged(stage_a(0))
        merged(stage_b(0), stage_a(1))
        with dve.Fori(2, NB) as b:
            merged(stage_b(b - 1), stage_a(b))
        dve.drain().then_inc(layer0_done.sem, 1)
        dve.wait_ge(layer0_done.sem, 4)
        dve.wait_ge(late_loaded.sem, 32)
        merged(stage_b(NB - 1), stage_c(0))
        dve.drain().then_inc(layer0_done.sem, 1)
        dve.wait_ge(layer0_done.sem, 8)
        V.memset(gsc[:, :, GRP:], BIG).then_inc(const_set.sem, 1)
        V.tensor_copy(pick1r[:], pick1.unsqueeze(2).to_broadcast([2 * E1, E1, I1])).then_inc(const_set.sem, 1)
        V.memset(mks[:, :, E1:], BIG).then_inc(const_set.sem, 1)
        dve.wait_ge(const_set.sem, NCONST + NCONST_V + 3)
        merged(stage_d(0), stage_c(1))
        with dve.Fori(2, NB) as b:
            merged(stage_d(b - 1), stage_c(b))
        merged(stage_d(NB - 1))

    @block.tensor
    def _(pe):
        M = nc.tensor.matmul

        def transpose4(dst, src):
            for i in range(NT):
                last = nc.tensor.transpose(dst[:, i * P:(i + 1) * P], src[:, i, :], ident)
            return last

        def product3(dst, w, x_hi, x_lo, start, stop):
            M(dst, w[0], x_hi, start=start, stop=False)
            M(dst, w[1], x_hi, start=False, stop=False)
            return M(dst, w[0], x_lo, start=False, stop=stop)

        def stage_a(b):
            yield 0
            pe.wait_ge(a_ctx_in.sem, a_ctx_in.at(b, 32))
            pe.wait_ge(a_exp.sem, a_exp.at(b, 0))
            for t in range(2):
                M(RING[0][:, t * P:(t + 1) * P], ctxA[:, t * P:(t + 1) * P], w_in["k"], start=True, stop=True)
            for t in range(2):
                last = M(RING[0][:, (2 + t) * P:(3 + t) * P], ctxA[:, t * P:(t + 1) * P], w_in["v"], start=True, stop=True)
            last.then_inc(a_kv_ps.sem, 1)
            yield 1.4
            pe.wait_ge(ln_a.out.sem, ln_a.out.at(b, NT))
            pe.wait_ge(a_x1.sem, a_x1.at(b, 0))
            transpose4(MISC, xn).then_inc(a_xT_ps.sem, 1)
            yield 1.9
            pe.wait_ge(a_xT.sem, a_xT.at(b, 1))
            for i in range(NT):
                last = M(four(MISC)[:, i, :], xT[:, i * P:(i + 1) * P], w_in["q"], start=True, stop=True)
            last.then_inc(a_q_ps.sem, 1)
            yield 2.5
            pe.wait_ge(a_qn.sem, a_qn.at(b, 4))

            def query_stack(dst, g):
                for i in range(NT):
                    src = QN[:, i, HG * g:HG * g + HG, :].rearrange("p h c -> p (h c)").bitcast(F32)
                    last = nc.tensor.transpose(dst[:, i * P:(i + 1) * P], src, ident)
                return last

            for g in range(NG):
                if g:
                    yield 2.5 + 0.2 * g
                if g == 0:
                    pe.wait_ge(a_kv.sem, a_kv.at(b, 2))
                elif g >= 2:
                    pe.wait_ge(a_qs.sem, a_qs.at(b, g - 1))
                query_stack(RING[g % 2], g).then_inc(a_qt_ps.sem, 1)
            yield 3.2
            pe.wait_ge(a_kn.sem, a_kn.at(b, 5))
            pe.wait_ge(a_on.sem, a_on.at(b, 0))
            pe.wait_ge(a_qs.sem, a_qs.at(b, NG))
            for h in range(2):
                dst = (RING[1] if h == 0 else ACC)[:, 0:2 * KW].rearrange("p (g k) -> p g k", g=2)
                for gg in range(2):
                    g = 2 * h + gg
                    src = KN[:, :, HG * g:HG * g + HG, :].rearrange("p t h c -> p t (h c)").bitcast(F32)
                    nc.tensor.transpose(dst[:, gg, 0:P], src[:, 0, :], ident)
                    last = nc.tensor.transpose(dst[:, gg, P:KW], src[0:TP, 1, :], ident[0:TP, 0:TP])
                last.then_inc(a_kt_ps.sem, 1)
            yield 4.3
            pe.wait_ge(a_qs.sem, a_qs.at(b, NG))
            pe.wait_ge(a_ks.sem, a_ks.at(b, 2 * HG))

            def weighted_values(g):
                for u in range(NU):
                    yield pv_time(g, u)
                    n = g * NU + u
                    v = VM[:, g, P * u:P * u + P] if u < HG else VT[:, g, :]
                    if u == 0:
                        pe.wait_ge(a_on.sem, a_on.at(b, 2 * g))
                        pe.wait_ge(a_nm.sem, a_nm.at(b, 2 * NT))
                    if n == 0:
                        pe.wait_ge(a_vmain.sem, a_vmain.at(b, 2))
                        pe.wait_ge(a_vtail.sem, a_vtail.at(b, 2 * HG))
                    pe.wait_ge(a_phi.sem, a_phi.at(b, n + 1))
                    M(ACC, v, Phi[:, n % PR, :], start=(u == 0), stop=False)
                    prob_low(pe, b, n)
                    M(ACC, v, Plo[:, n % PR, :], start=False, stop=(u == NU - 1)).then_inc(a_pv.sem, 1)
                yield norm_time(g)
                pe.wait_ge(a_oz.sem, a_oz.at(b, g + 1))
                transpose4(ACC, OZ[:].rearrange("p (i t) -> p i t", i=NT)).then_inc(a_ozt_ps.sem, 1)

            def maxima(g):
                for u in range(2 * NT):
                    yield m_time(b, g, u)
                    if u == 0:
                        pe.wait_ge(a_q2s.sem, a_q2s.at(b, g))
                    pe.wait_ge(a_nm.sem, a_nm.at(b, max(0, u - 1) if g == 0 else g * 2 * NT + u))
                    i, half = divmod(u, 2)
                    M(m_bank(g, u)[:, 0:2 * KW], QS[:, g, i * P:(i + 1) * P],
                      KS[:, g, 2 * half:2 * half + 2, :].rearrange("p h k -> p (h k)"), start=True, stop=True).then_inc(a_m_ps.sem, 1)

            def scores(g):
                yield s_time(g, 0) - 1.2
                pe.wait_ge(a_nmq.sem, a_nmq.at(b, 2 * g + 2))
                query_stack(MISC, g).then_inc(a_q2_ps.sem, 1)
                for u in range(NU):
                    yield s_time(g, u)
                    n = g * NU + u
                    pe.wait_ge(a_q2s.sem, a_q2s.at(b, g + 1))
                    pe.wait_ge(a_exp.sem, a_exp.at(b, max(0, n - 1)))
                    if n == HG:
                        pe.wait_ge(a_kst.sem, a_kst.at(b, 1))
                    keys = KS[:, g, u, 0:P] if u < HG else KST[:, g, :]
                    M(RING[n % 2], keys, QS[:, g, :], start=True, stop=True).then_inc(a_s_ps.sem, 1)

            yield from by_time(*[maxima(g) for g in range(NG)], *[scores(g) for g in range(NG)],
                               *[weighted_values(g) for g in range(NG)])
            yield norm_time(NG - 1) + 0.7
            pe.wait_ge(a_on.sem, a_on.at(b, 2 * NG))
            pe.wait_ge(a_exp.sem, a_exp.at(b, NG * NU))
            for h in range(2):
                for i in range(NT):
                    src = ON[:, i, 2 * h:2 * h + 2, :].rearrange("p g c -> p (g c)")
                    last = nc.tensor.transpose(RING[h][:, i * P:(i + 1) * P], src, ident)
                last.then_inc(a_ot_ps.sem, 1)
            yield norm_time(NG - 1) + 1.5
            pe.wait_ge(a_ot.sem, a_ot.at(b, 2))
            for i in range(NT):
                for h in range(2):
                    last = M(four(MISC)[:, i, :], OT[:, h, i * P:(i + 1) * P], w_o[:, h, :], start=(h == 0), stop=(h == 1))
            last.then_inc(a_y_ps.sem, 1)

        def parts(w, c):
            return w[:, 0, c * P:(c + 1) * P], w[:, 1, c * P:(c + 1) * P]

        def stage_b(b):
            yield 0
            pe.wait_ge(ln_b.out.sem, ln_b.out.at(b, NT))
            pe.wait_ge(b_x2.sem, b_x2.at(b, 0))
            transpose4(bank[3], xn2).then_inc(b_xT_ps.sem, 1)
            yield 0.4
            pe.wait_ge(b_xT.sem, b_xT.at(b, 1))
            for i in range(NT):
                last = M(bank[3][:, i * E0:(i + 1) * E0], xT32[:, i * P:(i + 1) * P], w_r, start=True, stop=True)
            last.then_inc(b_lg_ps.sem, 1)

            def second(c):
                if c % 4 == 0:
                    pe.wait_ge(b_ty.sem, b_ty.at(b, c // 4))
                hidden_high(pe, b, c)
                hidden_low(pe, b, c)
                product3(bank[2], parts(w2s, c), hhi[:, c % HR, :], hlo[:, c % HR, :], c % 4 == 0, c % 4 == 3).then_inc(b_y.sem, 1)

            for c in range(NC0):
                yield b_time(c) + 0.3
                if c == 0:
                    pe.wait_ge(b_xs.sem, b_xs.at(b, 2))
                pe.wait_ge(b_gelu.sem, b_gelu.at(b, max(0, c - 1)))
                product3(bank[c % 2], parts(w1s, c), xThi[:], xTlo[:], True, True).then_inc(b_h_ps.sem, 1)
                if c == 3:
                    yield b_time(c) + 0.5
                    pe.wait_ge(b_w.sem, b_w.at(b, 6))
                    for i in range(NT):
                        last = nc.tensor.transpose(bank[3][0:2 * E0, i * P:(i + 1) * P], WN[:, i, :].bitcast(F32), ident)
                    last.then_inc(b_wt_ps.sem, 1)
                if c == 4:
                    yield b_time(c) + 0.4
                    pe.wait_ge(b_wt.sem, b_wt.at(b, 1))
                    M(bank[3], b2dup, WT[:].bitcast(F32), start=True, stop=True).then_inc(b_base_ps.sem, 1)
                if c == 4 or c % 4 == 3 and c > 4:
                    yield b_time(c) + 0.65
                    e = (c - 3) // 4
                    if e == 0:
                        pe.wait_ge(b_base.sem, b_base.at(b, 1))
                    else:
                        pe.wait_ge(b_wb.sem, b_wb.at(b, e))
                    M(bank[3], spread0(e), WT[:], start=True, stop=True).then_inc(b_wb_ps.sem, 1)
                if c >= 3 and (c - 3) % 4 == 0:
                    yield b_time(c) + 0.7
                    second(c - 3)
                if c >= 2 and (c - 2) % 4:
                    yield b_time(c) + 1.25
                    second(c - 2)
            yield b_time(NC0) + 0.75
            second(NC0 - 2)
            yield b_time(NC0 + 1) + 0.75
            second(NC0 - 1)
            yield b_time(NC0) + 4.5
            pe.wait_ge(b_acc.sem, b_acc.at(b, E0))
            pe.wait_ge(b_wb.sem, b_wb.at(b, E0))
            transpose4(bank[3], acc_o[:].rearrange("p (i d) -> p i d", i=NT)).then_inc(b_o_ps.sem, 1)

        def spread0(e):
            return pick0r[:, e:e + 1].to_broadcast([2 * E0, P])

        def spread1(e):
            return pick1r[:, e:e + 2, :].rearrange("k e i -> k (e i)")

        def stage_c(b):
            yield 0.5
            pe.wait_ge(c_ctx_in.sem, c_ctx_in.at(b, 16))
            pe.wait_ge(c_a3.sem, c_a3.at(b, 0))
            M(RING[0][:, 0:LK], w_in["k2"], ctxC[:, 0:LK], start=True, stop=True)
            M(RING[1][:, 0:P], ctxC[:, 0:P], w_in["v2"], start=True, stop=True)
            M(RING[1][0:TP, P:2 * P], ctxC[:, P:KW], w_in["v2"], start=True, stop=True).then_inc(c_kv2_ps.sem, 1)
            yield 2
            pe.wait_ge(ln_c.out.sem, ln_c.out.at(b, NT))
            pe.wait_ge(c_n2T.sem, c_n2T.at(b, 0))
            transpose4(MISC, xi).then_inc(c_xT_ps.sem, 1)
            yield 3.6
            pe.wait_ge(c_xT.sem, c_xT.at(b, 1))
            pe.wait_ge(c_kv2.sem, c_kv2.at(b, 3))
            M(RING[0], w_in["q1"], xiT[:], start=True, stop=True).then_inc(c_qkv_ps.sem, 1)
            M(RING[1], w_in["k1"], xiT[:], start=True, stop=True).then_inc(c_qkv_ps.sem, 1)
            pe.wait_ge(c_p2tt.sem, c_p2tt.at(b, 0))
            for i in range(NT):
                last = M(four(ACC)[:, i, :], xiT[:, i * P:(i + 1) * P], w_in["v1"], start=True, stop=True)
            last.then_inc(c_qkv_ps.sem, 1)
            yield 5.6
            pe.wait_ge(c_qv.sem, c_qv.at(b, 1))
            pe.wait_ge(c_k.sem, c_k.at(b, 1))

            def turn(i):
                pe.wait_ge(c_pn.sem, c_pn.at(b, i + 1))
                pe.wait_ge(c_pt.sem, c_pt.at(b, i))
                for kc in range(i + 1):
                    last = nc.tensor.transpose(MISC[:, kc * P:(kc + 1) * P], PN1[:, i % 2, kc * P:(kc + 1) * P], ident)
                last.then_inc(c_pt_ps.sem, 1)

            def attend(i):
                pe.wait_ge(c_pt.sem, c_pt.at(b, i + 1))
                for kc in range(i + 1):
                    last = M(four(ACC)[:, i, :], PT[:, kc, i * P:(i + 1) * P], V1[:, kc, :], start=(kc == 0), stop=(kc == i))
                return last

            def tiles(pair):
                for i in (2 * pair, 2 * pair + 1):
                    yield c_time(pair) + 0.1 * (i % 2)
                    w = (i + 1) * P
                    pe.wait_ge(c_p.sem, c_p.at(b, max(0, i - 1)))
                    M(RING[i % 2][:, 0:w], QT1[:, i * P:w], KT1[:, 0:w], start=True, stop=True).then_inc(c_s_ps.sem, 1)
                for i in (2 * pair, 2 * pair + 1):
                    yield c_time(pair) + 3.3 + 0.9 * (i % 2)
                    turn(i)
                for i in (2 * pair, 2 * pair + 1):
                    yield c_time(pair) + 4.7 + 0.5 * (i % 2)
                    if i == 0:
                        pe.wait_ge(c_qv.sem, c_qv.at(b, 2))
                    last = attend(i)
                if pair == 1:
                    last.then_inc(c_att_ps.sem, 1)

            yield from by_time(tiles(0), tiles(1))
            yield 15.5
            pe.wait_ge(c_att.sem, c_att.at(b, 1))
            transpose4(MISC, att).then_inc(c_attT_ps.sem, 1)
            yield 17
            pe.wait_ge(c_attT.sem, c_attT.at(b, 1))
            M(RING[0], w_in["q2"], attT[:], start=True, stop=True).then_inc(c_q2_ps.sem, 1)
            yield 19
            pe.wait_ge(c_q2.sem, c_q2.at(b, 1))
            pe.wait_ge(c_p.sem, c_p.at(b, NT))
            pe.wait_ge(c_att.sem, c_att.at(b, 2))
            for i in range(NT):
                dst = (RING[1] if i < 2 else ACC)[:, 0:2 * KW].rearrange("p (i k) -> p i k", i=2)
                last = M(dst[:, i % 2, 0:LK], Q2T[:, i * P:(i + 1) * P], K2T[:], start=True, stop=True)
                if i % 2:
                    last.then_inc(c_s2_ps.sem, 1)
            yield 22.4
            pe.wait_ge(c_pn2.sem, c_pn2.at(b, 2))
            for i in range(NT):
                nc.tensor.transpose(RING[0][:, i * P:(i + 1) * P], PN2[:, i, 0:P], ident)
            for i in range(NT):
                last = nc.tensor.transpose(ACC[0:LT, i * P:(i + 1) * P], PN2[:, i, P:LK], ident)
            last.then_inc(c_p2t_ps.sem, 1)
            yield 24
            pe.wait_ge(c_p2t.sem, c_p2t.at(b, 1))
            pe.wait_ge(c_p2tt.sem, c_p2tt.at(b, 1))
            for i in range(NT):
                M(four(RING[1])[:, i, :], P2T[:, i * P:(i + 1) * P], V2m[:], start=True, stop=False)
                last = M(four(RING[1])[:, i, :], P2Tt[0:LT, i * P:(i + 1) * P], V2t[0:LT, :], start=False, stop=True)
            last.then_inc(c_att2_ps.sem, 1)
            yield 29
            pe.wait_ge(c_n2.sem, c_n2.at(b, 2))
            transpose4(MISC, norm2).then_inc(c_n2T_ps.sem, 1)
            yield 30.3
            pe.wait_ge(c_n2T.sem, c_n2T.at(b, 1))
            M(RING[0], w_in["f1"], n2T[:], start=True, stop=True).then_inc(c_h_ps.sem, 1)
            yield 32.4
            pe.wait_ge(c_h.sem, c_h.at(b, 2))
            for i in range(NT):
                last = M(four(RING[1])[:, i, :], hT[:, i * P:(i + 1) * P], w_in["f2"], start=True, stop=True)
            last.then_inc(c_ff_ps.sem, 1)

        def stage_d(b):
            yield 0
            pe.wait_ge(ln_d.out.sem, ln_d.out.at(b, NT))
            pe.wait_ge(d_x4.sem, d_x4.at(b, 0))
            transpose4(bank[3], xn2).then_inc(d_xT_ps.sem, 1)
            yield 0.6
            pe.wait_ge(d_xT.sem, d_xT.at(b, 1))
            for i in range(NT):
                last = M(bank[3][:, i * E1:(i + 1) * E1], xT32[:, i * P:(i + 1) * P], w_gate, start=True, stop=True)
            last.then_inc(d_lg_ps.sem, 1)

            def gate_up(n, k):
                return parts(shs, k) if n == 0 else parts(gus, 2 * (n - 1) + k)

            def first_use(n):
                if isinstance(b, int) and b == 0:
                    pe.wait_ge(raw_lo.sem, NP0 + n + 1)

            def down(n):
                if n == 1:
                    first_use(2)
                elif n == 1 + NP1 // 2:
                    first_use(5)
                pe.wait_ge(d_hi.sem, d_hi.at(b, n + 1))
                pe.wait_ge(d_lo.sem, d_lo.at(b, n + 1))
                w = parts(shs, 2) if n == 0 else parts(dns, n - 1)
                product3(bank[2], w, hhi[:, n % HR, :], hlo[:, n % HR, :], n == 0, n == ND - 1).then_inc(d_dn.sem, 1)

            for n in range(ND):
                yield d_time(n)
                if n == 0:
                    pe.wait_ge(d_xs.sem, d_xs.at(b, 2))
                    pe.wait_ge(d_oT.sem, d_oT.at(b, 0))
                    first_use(0)
                elif n % 4 == 1:
                    first_use((1, 3, 4, 6)[n // 4])
                pe.wait_ge(d_silu.sem, d_silu.at(b, n))
                product3(bank[0], gate_up(n, 0), xThi[:], xTlo[:], True, True).then_inc(d_g_ps.sem, 1)
                yield d_time(n) + 0.6
                pe.wait_ge(d_t.sem, d_t.at(b, n))
                product3(bank[1], gate_up(n, 1), xThi[:], xTlo[:], True, True).then_inc(d_u_ps.sem, 1)
                if n == 1:
                    yield d_time(n) + 0.9
                    pe.wait_ge(d_r.sem, d_r.at(b, d_r.per))
                    apart(pe, b)
                    for i in range(NT):
                        last = nc.tensor.transpose(bank[3][0:2 * E1, i * P:(i + 1) * P], CN[:, i, :].bitcast(F32), ident)
                    last.then_inc(d_ct_ps.sem, 1)
                if n:
                    yield d_time(n) + 1
                    if n == 1:
                        pe.wait_ge(d_ct.sem, d_ct.at(b, 1))
                    pe.wait_ge(d_h.sem, d_h.at(b, n - 1))
                    M(bank[3], spread1(2 * (n - 1)), CT[:], start=True, stop=True).then_inc(d_cb_ps.sem, 1)
                if n >= 2:
                    yield d_time(n) + 1.6
                    down(n - 2)
            yield d_time(ND) + 1.3
            down(ND - 2)
            yield d_time(ND) + 3.3
            down(ND - 1)
            yield d_time(ND) + 4.5
            pe.wait_ge(d_oT.sem, d_oT.at(b, 1))
            pe.wait_ge(d_h.sem, d_h.at(b, NP1))
            transpose4(bank[3], oT[:].rearrange("p (i d) -> p i d", i=NT)).then_inc(d_o_ps.sem, 1)

        pe.wait_ge(early_loaded.sem, 32)
        pe.wait_ge(const_set.sem, NCONST + NCONST_V)
        merged(stage_a(0))
        pe.wait_ge(raw_lo.sem, NP0)
        merged(stage_b(0), stage_a(1))
        with pe.Fori(2, NB) as b:
            merged(stage_b(b - 1), stage_a(b))
        pe.drain().then_inc(layer0_done.sem, 1)
        pe.wait_ge(layer0_done.sem, 4)
        pe.wait_ge(late_loaded.sem, 32)
        merged(stage_b(NB - 1), stage_c(0))
        pe.drain().then_inc(layer0_done.sem, 1)
        pe.wait_ge(layer0_done.sem, 8)
        pe.wait_ge(const_set.sem, NCONST + NCONST_V + 3)
        merged(stage_d(0), stage_c(1))
        with pe.Fori(2, NB) as b:
            merged(stage_d(b - 1), stage_c(b))
        merged(stage_d(NB - 1))

    ctx.close()


def kernel(**inputs):
    import concourse.bacc as bacc
    from concourse.bass_utils import run_bass_kernel_spmd

    i = {n: np.asarray(v) for n, v in inputs.items()}
    ctxT = np.zeros((NB, D, CPAD), np.float32)
    ctx_t = i["ctx_1024"].transpose(0, 2, 1)
    mask = np.zeros((NB, CPAD), bool)
    mask_in = i["mask_BxS2_bf1"]
    valid = np.zeros((CPAD,), np.float32)
    ctxT[:, :, 0:P], mask[:, 0:P], valid[0:P] = ctx_t[:, :, 0:P], mask_in[:, 0:P], 1.0
    for j in range(HG):
        o = P + TP * j
        ctxT[:, :, o:o + LT], mask[:, o:o + LT], valid[o:o + LT] = ctx_t[:, :, P:LK], mask_in[:, P:LK], 1.0
    woT = i["L0_xattn_Wo"].T
    wo = np.zeros((P, 2, D), np.float32)
    for g in range(NG):
        for part in range(2):
            o = 64 * (g % 2) + 32 * part
            wo[o:o + 32, g // 2] = woT[32 * g:32 * g + 32]
    gu = i["L1_ffn_experts_gate_up"].reshape(NP1, 2, 2, I1, D)
    arrays = {
        "x": i["x"],
        "ctxT": ctxT,
        "mask": mask.reshape(NB, 2, P).transpose(0, 2, 1),
        "valid": valid.reshape(2, P).T,
        "ident": np.eye(P, dtype=np.float32),
        "trimask": np.triu(np.full((P, P), -BIG, np.float32), k=1),
        "pick0": np.tile(np.eye(E0, dtype=np.float32), (2, 1)),
        "pick1": np.tile(np.eye(E1, dtype=np.float32), (2, 1)),
        "w_q": i["L0_xattn_Wq"].T, "w_k": i["L0_xattn_Wk"].T, "w_v": i["L0_xattn_Wv"].T, "wo": wo,
        "row_bq": i["L0_xattn_bq"], "row_bk": i["L0_xattn_bk"], "row_bv": i["L0_xattn_bv"], "row_bo": i["L0_xattn_bo"],
        "wr": i["L0_ffn_Wr"], "row_br": i["L0_ffn_br"],
        "w1": i["L0_ffn_W1"].transpose(1, 0, 2).reshape(D, E0 * H0),
        "b1T": i["L0_ffn_b1"].reshape(NC0, P).T,
        "w2": i["L0_ffn_W2"].reshape(NC0, P, D).transpose(1, 0, 2).reshape(P, NC0 * D),
        "b2dup": np.tile(i["L0_ffn_b2"], (2, 1)),
        "w_k1": i["L1_xattn_Wk1"], "w_q1": i["L1_xattn_Wq1"], "w_v1": i["L1_xattn_Wv1"],
        "w_k2": i["L1_xattn_Wk2"], "w_q2": i["L1_xattn_Wq2"], "w_v2": i["L1_xattn_Wv2"],
        "w_f1": i["L1_xattn_W1"], "b1f": i["L1_xattn_b1"].reshape(D, 1), "w_f2": i["L1_xattn_W2"],
        "row_b2f": i["L1_xattn_b2"], "row_gamma": i["L1_xattn_gamma"], "row_beta": i["L1_xattn_beta"],
        "wgate": i["L1_ffn_gate_weight"].T, "row_gb": i["L1_ffn_e_score_correction_bias"],
        "gu": gu.transpose(4, 0, 2, 1, 3).reshape(D, 2 * NP1 * P),
        "dn": i["L1_ffn_experts_down"].reshape(NP1, 2, D, I1).transpose(1, 3, 0, 2).reshape(P, NP1 * D),
        "sh": np.concatenate([i["L1_ffn_shared_gate_w"].T, i["L1_ffn_shared_up_w"].T, i["L1_ffn_shared_down_w"].T], 1),
    }

    def pack(parts):
        out = np.zeros((max(n for _, n, _ in parts), width(parts)), np.float32)
        at = 0
        for name, partitions, columns in parts:
            out[0:partitions, at:at + columns] = arrays.pop(name).reshape(partitions, columns)
            at += columns
        return out

    arrays["early"], arrays["late"] = pack(EARLY), pack(LATE)
    arrays["early_rows"], arrays["late_rows"] = pack(EARLY_ROWS)[0], pack(LATE_ROWS)[0]
    arrays = {n: np.ascontiguousarray(v) for n, v in arrays.items()}
    nc = bacc.Bacc("TRN2", target_bir_lowering=False, num_devices=1)
    aps = {n: nc.dram_tensor(n + "_dram", v.shape, mybir.dt.from_np(v.dtype), kind="ExternalInput").ap()
           for n, v in arrays.items()}
    aps["out"] = nc.dram_tensor("out_dram", (NB, S, D), F32, kind="ExternalOutput").ap()
    build_program(nc, aps)
    r = run_bass_kernel_spmd(nc, [{n + "_dram": v for n, v in arrays.items()}], core_ids=[0])
    return r.results[0]["out_dram"]
```
